# Optimizing a Trainium2 kernel written in Bass

```python
import numpy as np
import jax
import jax.numpy as jnp

def _softmax(x, axis=-1):
    return jax.nn.softmax(x, axis=axis)

def _gelu(x):
    return jax.nn.gelu(x, approximate=True)

def _silu(x):
    return jax.nn.silu(x)

def _sigmoid(x):
    return jax.nn.sigmoid(x)

def _layernorm(x, axis=-1, eps=1e-05):
    m = jnp.mean(x, axis=axis, keepdims=True)
    v = jnp.var(x, axis=axis, keepdims=True)
    return (x - m) / jnp.sqrt(v + eps)

def _scatter_add(tgt, idx, src, axis=0):
    return tgt.at[idx].add(src)

def _segment_sum(src, seg, n):
    return jax.ops.segment_sum(src, seg, n)
kernel_name = 'mk_decoder_postln_d1_seqx_r8_0469ca'

def setup_inputs(seed: int=0):
    np.random.seed(seed)
    _w = jnp.asarray

    def _rec_inputs():
        import jax
        import jax.numpy as jnp
        _rk = jax.random.key(seed)
        x = 0.0003765 + 1 * jax.random.normal(jax.random.fold_in(_rk, 1), (16, 128, 256), jnp.float32)
        _lenS = 128 - jax.random.randint(jax.random.fold_in(_rk, 7), (16,), 0, max(1, 128 // 4) + 1, jnp.int32)
        _lenS2 = 128 - jax.random.randint(jax.random.fold_in(_rk, 8), (16,), 0, max(1, 128 // 4) + 1, jnp.int32)
        _ctx_2048P = jax.random.normal(jax.random.fold_in(_rk, 11), (16, 16, 256), jnp.float32)
        _ctx_2048c = jax.random.dirichlet(jax.random.fold_in(_rk, 511), 0.3 * jnp.ones((16,), jnp.float32), (16, 128))
        _ctx_2048t = jnp.einsum('bsk,bkd->bsd', _ctx_2048c, _ctx_2048P)
        _ctx_2048t = _ctx_2048t * jax.lax.rsqrt(jnp.mean(jnp.square(_ctx_2048t)) + 1e-12) * 0.953939
        ctx_2048 = -0.000292821 + 1.00034 * (_ctx_2048t + 0.3 * jax.random.normal(jax.random.fold_in(_rk, 611), (16, 128, 256), jnp.float32))
        return (x, ctx_2048)
    x, ctx_2048 = _rec_inputs()

    def _L0_attn_setup():
        import jax, jax.numpy as jnp
        import numpy as np
        EPS = 1e-08
        C_RGLRU = 8.0

        def rmsnorm(x, w):
            rms = jnp.sqrt(jnp.mean(x * x, axis=-1, keepdims=True) + EPS)
            return w * (x / rms)

        def causal_depthwise_conv(x, conv_w, conv_b):
            K = conv_w.shape[0]
            S = x.shape[1]
            xp = jnp.pad(x, ((0, 0), (K - 1, 0), (0, 0)))
            y = sum((conv_w[k] * xp[:, k:k + S, :] for k in range(K)))
            return y + conv_b

        def rg_lru(x, ga_W, ga_b, gx_W, gx_b, a_param):
            r = jax.nn.sigmoid(x @ ga_W + ga_b)
            i = jax.nn.sigmoid(x @ gx_W + gx_b)
            log_a = -C_RGLRU * jax.nn.softplus(a_param) * r
            a = jnp.exp(log_a)
            mult = jnp.sqrt(-jnp.expm1(2.0 * log_a))
            b = mult * (i * x)

            def combine(c1, c2):
                a1, b1 = c1
                a2, b2 = c2
                return (a1 * a2, a2 * b1 + b2)
            _, h = jax.lax.associative_scan(combine, (a, b), axis=1)
            return h
        D, H, F, K, B, S = (256, 256, 768, 4, 2, 256)
        key = jax.random.key(seed)
        ks = jax.random.split(key, 16)

        def lin(k, fan_in, shape):
            return jax.random.normal(k, shape, jnp.float32) * fan_in ** (-0.5)
        return {'x': jax.random.normal(ks[0], (B, S, D), jnp.float32), 'norm1_w': jnp.ones((D,), jnp.float32), 'left_W': lin(ks[1], D, (D, H)), 'left_b': jnp.zeros((H,), jnp.float32), 'right_W': lin(ks[2], D, (D, H)), 'right_b': jnp.zeros((H,), jnp.float32), 'conv_w': lin(ks[3], K, (K, H)), 'conv_b': jnp.zeros((H,), jnp.float32), 'ga_W': lin(ks[4], H, (H, H)), 'ga_b': jnp.zeros((H,), jnp.float32), 'gx_W': lin(ks[5], H, (H, H)), 'gx_b': jnp.zeros((H,), jnp.float32), 'a_param': jax.random.uniform(ks[6], (H,), jnp.float32, 0.5, 3.0), 'out_W': lin(ks[7], H, (H, D)), 'out_b': jnp.zeros((D,), jnp.float32), 'norm2_w': jnp.ones((D,), jnp.float32), 'up1_W': lin(ks[8], D, (D, F)), 'up1_b': jnp.zeros((F,), jnp.float32), 'up2_W': lin(ks[9], D, (D, F)), 'up2_b': jnp.zeros((F,), jnp.float32), 'down_W': lin(ks[10], F, (F, D)), 'down_b': jnp.zeros((D,), jnp.float32)}
    _L0_attn_all = _L0_attn_setup()
    _L0_attn_in = {k: v for k, v in _L0_attn_all.items() if k in ('norm1_w', 'left_W', 'left_b', 'right_W', 'right_b', 'conv_w', 'conv_b', 'ga_W', 'ga_b', 'gx_W', 'gx_b', 'a_param', 'out_W', 'out_b', 'norm2_w', 'up1_W', 'up1_b', 'up2_W', 'up2_b', 'down_W', 'down_b')}
    del _L0_attn_all

    def _L0_xattn_setup():
        import jax, jax.numpy as jnp
        import numpy as np
        key = jax.random.key(seed)
        k1, k2, k3, k4, k5 = jax.random.split(key, 5)
        B, D_MODEL, L = (2, 128, 256)
        HEAD_DIM = 8
        H = D_MODEL // HEAD_DIM
        return {'k': jax.random.normal(k1, (B, D_MODEL, L), dtype=jnp.float32), 'v': jax.random.normal(k2, (B, D_MODEL, L), dtype=jnp.float32), 'q': jax.random.normal(k3, (B, D_MODEL, L), dtype=jnp.float32), 'ssm_kernel': jax.random.normal(k4, (H, L), dtype=jnp.float32), 'D': jax.random.normal(k5, (H,), dtype=jnp.float32), 'head_dim': HEAD_DIM}
    _L0_xattn_all = _L0_xattn_setup()
    _L0_xattn_in = {k: v for k, v in _L0_xattn_all.items() if k in ('ssm_kernel', 'D')}
    del _L0_xattn_all

    def _L0_ffn_setup():
        import jax, jax.numpy as jnp
        import numpy as np
        H = 256
        F = 176
        E = 64
        TOP_K = 6
        CAP = 64
        SCALE = 1.0
        F_SH = 2 * F
        B, S = (1, 256)
        key = jax.random.key(seed)
        ks = jax.random.split(key, 8)
        s = 0.02
        return {'hidden_states': jax.random.normal(ks[0], (B, S, H), jnp.float32), 'gate_w': jax.random.normal(ks[1], (E, H), jnp.float32) * s, 'w_gate': jax.random.normal(ks[2], (E, H, F), jnp.float32) * s, 'w_up': jax.random.normal(ks[3], (E, H, F), jnp.float32) * s, 'w_down': jax.random.normal(ks[4], (E, F, H), jnp.float32) * s, 'sh_gate': jax.random.normal(ks[5], (F_SH, H), jnp.float32) * s, 'sh_up': jax.random.normal(ks[6], (F_SH, H), jnp.float32) * s, 'sh_down': jax.random.normal(ks[7], (H, F_SH), jnp.float32) * s}
    _L0_ffn_all = _L0_ffn_setup()
    _L0_ffn_in = {k: v for k, v in _L0_ffn_all.items() if k in ('gate_w', 'w_gate', 'w_up', 'w_down', 'sh_gate', 'sh_up', 'sh_down')}
    del _L0_ffn_all
    return {'x': x, 'ctx_2048': ctx_2048, 'L0_attn_norm1_w': _L0_attn_in['norm1_w'], 'L0_attn_left_W': _L0_attn_in['left_W'], 'L0_attn_left_b': _L0_attn_in['left_b'], 'L0_attn_right_W': _L0_attn_in['right_W'], 'L0_attn_right_b': _L0_attn_in['right_b'], 'L0_attn_conv_w': _L0_attn_in['conv_w'], 'L0_attn_conv_b': _L0_attn_in['conv_b'], 'L0_attn_ga_W': _L0_attn_in['ga_W'], 'L0_attn_ga_b': _L0_attn_in['ga_b'], 'L0_attn_gx_W': _L0_attn_in['gx_W'], 'L0_attn_gx_b': _L0_attn_in['gx_b'], 'L0_attn_a_param': _L0_attn_in['a_param'], 'L0_attn_out_W': _L0_attn_in['out_W'], 'L0_attn_out_b': _L0_attn_in['out_b'], 'L0_attn_norm2_w': _L0_attn_in['norm2_w'], 'L0_attn_up1_W': _L0_attn_in['up1_W'], 'L0_attn_up1_b': _L0_attn_in['up1_b'], 'L0_attn_up2_W': _L0_attn_in['up2_W'], 'L0_attn_up2_b': _L0_attn_in['up2_b'], 'L0_attn_down_W': _L0_attn_in['down_W'], 'L0_attn_down_b': _L0_attn_in['down_b'], 'L0_xattn_ssm_kernel': _L0_xattn_in['ssm_kernel'], 'L0_xattn_D': _L0_xattn_in['D'], 'L0_ffn_gate_w': _L0_ffn_in['gate_w'], 'L0_ffn_w_gate': _L0_ffn_in['w_gate'], 'L0_ffn_w_up': _L0_ffn_in['w_up'], 'L0_ffn_w_down': _L0_ffn_in['w_down'], 'L0_ffn_sh_gate': _L0_ffn_in['sh_gate'], 'L0_ffn_sh_up': _L0_ffn_in['sh_up'], 'L0_ffn_sh_down': _L0_ffn_in['sh_down']}

def reference(x, ctx_2048, L0_attn_norm1_w, L0_attn_left_W, L0_attn_left_b, L0_attn_right_W, L0_attn_right_b, L0_attn_conv_w, L0_attn_conv_b, L0_attn_ga_W, L0_attn_ga_b, L0_attn_gx_W, L0_attn_gx_b, L0_attn_a_param, L0_attn_out_W, L0_attn_out_b, L0_attn_norm2_w, L0_attn_up1_W, L0_attn_up1_b, L0_attn_up2_W, L0_attn_up2_b, L0_attn_down_W, L0_attn_down_b, L0_xattn_ssm_kernel, L0_xattn_D, L0_ffn_gate_w, L0_ffn_w_gate, L0_ffn_w_up, L0_ffn_w_down, L0_ffn_sh_gate, L0_ffn_sh_up, L0_ffn_sh_down):
    import jax
    import jax.numpy as jnp

    def _L0_attn_ref(x, norm1_w, left_W, left_b, right_W, right_b, conv_w, conv_b, ga_W, ga_b, gx_W, gx_b, a_param, out_W, out_b, norm2_w, up1_W, up1_b, up2_W, up2_b, down_W, down_b):
        import jax, jax.numpy as jnp
        import numpy as np
        EPS = 1e-08
        C_RGLRU = 8.0

        def rmsnorm(x, w):
            rms = jnp.sqrt(jnp.mean(x * x, axis=-1, keepdims=True) + EPS)
            return w * (x / rms)

        def causal_depthwise_conv(x, conv_w, conv_b):
            K = conv_w.shape[0]
            S = x.shape[1]
            xp = jnp.pad(x, ((0, 0), (K - 1, 0), (0, 0)))
            y = sum((conv_w[k] * xp[:, k:k + S, :] for k in range(K)))
            return y + conv_b

        def rg_lru(x, ga_W, ga_b, gx_W, gx_b, a_param):
            r = jax.nn.sigmoid(x @ ga_W + ga_b)
            i = jax.nn.sigmoid(x @ gx_W + gx_b)
            log_a = -C_RGLRU * jax.nn.softplus(a_param) * r
            a = jnp.exp(log_a)
            mult = jnp.sqrt(-jnp.expm1(2.0 * log_a))
            b = mult * (i * x)

            def combine(c1, c2):
                a1, b1 = c1
                a2, b2 = c2
                return (a1 * a2, a2 * b1 + b2)
            _, h = jax.lax.associative_scan(combine, (a, b), axis=1)
            return h
        gelu = lambda t: jax.nn.gelu(t, approximate=False)
        xn = rmsnorm(x, norm1_w)
        left = gelu(xn @ left_W + left_b)
        right = rg_lru(causal_depthwise_conv(xn @ right_W + right_b, conv_w, conv_b), ga_W, ga_b, gx_W, gx_b, a_param)
        x1 = left * right @ out_W + out_b + x
        x1n = rmsnorm(x1, norm2_w)
        mlp = gelu(x1n @ up1_W + up1_b) * (x1n @ up2_W + up2_b) @ down_W + down_b
        return mlp + x1

    def _L0_xattn_ref(k, v, q, ssm_kernel, D, head_dim):
        import jax, jax.numpy as jnp
        import numpy as np
        B, HD, L = k.shape
        H = HD // head_dim
        fft_size = 2 * L
        k_ = k.reshape(B, H, head_dim, L)
        v_ = v.reshape(B, H, head_dim, L)
        q_ = q.reshape(B, H, head_dim, L)
        kv = jnp.einsum('bhil,bhjl->bijhl', k_, v_)
        kv_f = jnp.fft.rfft(kv, n=fft_size)
        kernel_f = jnp.fft.rfft(ssm_kernel, n=fft_size)
        y = jnp.fft.irfft(kv_f * kernel_f, n=fft_size)[..., :L]
        out = y + kv * D[None, None, None, :, None]
        out = jnp.einsum('bijhl,bhil->bjhl', out, q_)
        out = jnp.transpose(out, (0, 2, 1, 3)).reshape(B, H * head_dim, L)
        return out.astype(k.dtype)

    def _L0_ffn_ref(hidden_states, gate_w, w_gate, w_up, w_down, sh_gate, sh_up, sh_down):
        import jax, jax.numpy as jnp
        import numpy as np
        H = 256
        F = 176
        E = 64
        TOP_K = 6
        CAP = 64
        SCALE = 1.0
        F_SH = 2 * F
        B, S = (1, 256)
        b, s, _ = hidden_states.shape
        x = hidden_states.reshape(-1, H)
        T = x.shape[0]
        logits = x.astype(jnp.float32) @ gate_w.astype(jnp.float32).T
        scores = jax.nn.softmax(logits, axis=-1)
        topk_w, topk_idx = jax.lax.top_k(scores, TOP_K)
        topk_w = topk_w * SCALE
        eid = topk_idx.reshape(-1)
        x_exp = jnp.repeat(x, TOP_K, axis=0)
        order = jnp.argsort(eid)
        eid_s = eid[order]
        counts = jnp.bincount(eid, length=E)
        starts = jnp.cumsum(counts) - counts
        pos = jnp.arange(T * TOP_K) - starts[eid_s]
        valid = pos < CAP
        pos_c = jnp.where(valid, pos, CAP)
        buf = jnp.zeros((E, CAP + 1, H), x.dtype).at[eid_s, pos_c].set(x_exp[order])
        g = jax.nn.silu(jnp.einsum('ech,ehf->ecf', buf, w_gate))
        u = jnp.einsum('ech,ehf->ecf', buf, w_up)
        d = jnp.einsum('ecf,efh->ech', g * u, w_down)
        out_s = jnp.where(valid[:, None], d[eid_s, pos_c], 0.0)
        out_exp = jnp.zeros_like(out_s).at[order].set(out_s)
        y = jnp.einsum('tkh,tk->th', out_exp.reshape(T, TOP_K, H), topk_w)
        y = y.astype(x.dtype).reshape(b, s, H)
        gs = jax.nn.silu(hidden_states @ sh_gate.T)
        us = hidden_states @ sh_up.T
        y = y + gs * us @ sh_down.T
        return y
    x = _layernorm(x + _L0_attn_ref(x, L0_attn_norm1_w, L0_attn_left_W, L0_attn_left_b, L0_attn_right_W, L0_attn_right_b, L0_attn_conv_w, L0_attn_conv_b, L0_attn_ga_W, L0_attn_ga_b, L0_attn_gx_W, L0_attn_gx_b, L0_attn_a_param, L0_attn_out_W, L0_attn_out_b, L0_attn_norm2_w, L0_attn_up1_W, L0_attn_up1_b, L0_attn_up2_W, L0_attn_up2_b, L0_attn_down_W, L0_attn_down_b), axis=-1)
    x = _layernorm(x + _L0_xattn_ref(ctx_2048, ctx_2048, x, L0_xattn_ssm_kernel, L0_xattn_D, 8), axis=-1)
    x = _layernorm(x + _L0_ffn_ref(x, L0_ffn_gate_w, L0_ffn_w_gate, L0_ffn_w_up, L0_ffn_w_down, L0_ffn_sh_gate, L0_ffn_sh_up, L0_ffn_sh_down), axis=-1)
    return x

_drawn_inputs = setup_inputs


def setup_inputs(seed=0):
    import zlib

    import numpy as np

    out = dict(_drawn_inputs(seed))
    spreads = {'L0_attn_norm1_w': (1.0, 0.2),
     'L0_attn_left_b': (0.0, 0.332),
     'L0_attn_right_b': (0.0, 0.1),
     'L0_attn_conv_b': (0.0, 0.275),
     'L0_attn_ga_b': (0.0, 0.8),
     'L0_attn_gx_b': (0.0, 0.8),
     'L0_attn_out_b': (0.0, 0.1),
     'L0_attn_norm2_w': (1.0, 0.2),
     'L0_attn_up1_b': (0.0, 0.1),
     'L0_attn_up2_b': (0.0, 0.1),
     'L0_attn_down_b': (0.0, 0.1)}
    factors = {'L0_attn_ga_W': 3.693,
     'L0_attn_a_param': 7.788,
     'L0_ffn_gate_w': 8.0,
     'L0_ffn_w_gate': 8.0,
     'L0_ffn_w_up': 8.0,
     'L0_ffn_w_down': 8.0,
     'L0_ffn_sh_gate': 2.89,
     'L0_ffn_sh_up': 2.846,
     'L0_ffn_sh_down': 2.855}
    for name, (base, spread) in spreads.items():
        noise = np.random.default_rng([zlib.crc32(name.encode()), seed]).standard_normal(out[name].shape)
        drawn = base * np.exp(spread * noise) if base else spread * noise
        out[name] = jnp.asarray(drawn.astype(out[name].dtype))
    for name, factor in factors.items():
        out[name] = (out[name] * factor).astype(out[name].dtype)
    return out
```

```python
from contextlib import ExitStack

import numpy as np
import concourse.bass as bass
from concourse import mybir

F32 = mybir.dt.float32
I32 = mybir.dt.int32
ALU = mybir.AluOpType
ACT = mybir.ActivationFunctionType
AX = mybir.AxisListType

P = 128
B, S, D = 16, 128, 256
T = B * S
C = D // P
G = 4
NB = B // G
TG = NB * S
F = 768
FJ = F // P
HD = 8
HEADS = S // HD
PAIRS = HD * (HD + 1) // 2
PW = PAIRS * NB
E, FE, CAP, TOPK = 64, 176, 64, 6
FH = FE // 2
FS = 352
FSC = [128, 128, 96]
EP = E // 2
RING = 4
ROW = D + 2 * E
NZ = T * TOPK
KW = P - 1 + D
EPS_RMS, EPS_LN, LRU_C = 1e-8, 1e-5, 8.0

COLS = {}
for _name, _n in (("norm1", C), ("norm2", C), ("left_b", C), ("right_b", C), ("conv_b", C), ("conv_w", 4 * C),
                  ("ga_b", C), ("gx_b", C), ("a_param", C), ("up1_b", FJ), ("up2_b", FJ)):
    COLS[_name] = sum(n for _, n in COLS.values()), _n
NCOLS = sum(n for _, n in COLS.values())

DOFF = [sum(HD - k for k in range(d)) for d in range(HD)]


class Steps:

    def __init__(self, sem, per):
        self.sem, self.per = sem, per

    def begin(self, g):
        self.base, self.n = self.per * g, 0

    def did(self, ins):
        ins.then_inc(self.sem, 1)
        self.n += 1
        return self.base + self.n

    def end(self):
        assert self.n == self.per, (self.n, self.per)


class Shared:
    pass


def build(nc, x, ctx_in, cols_in, outb_in, downb_in, d_in, kpad_in, wlr_in, wg_in, wo_in, wup_in, wdn_in,
          wgate_in, wsh_in, wshd_in, wgu_in, wd_in, out):
    v = Shared()
    v.x, v.ctx_in, v.cols_in, v.outb_in, v.downb_in, v.d_in, v.kpad_in, v.wlr_in, v.wg_in = \
        x, ctx_in, cols_in, outb_in, downb_in, d_in, kpad_in, wlr_in, wg_in
    v.wo_in, v.wup_in, v.wdn_in, v.wgate_in, v.wsh_in, v.wshd_in, v.wgu_in, v.wd_in, v.out = \
        wo_in, wup_in, wdn_in, wgate_in, wsh_in, wshd_in, wgu_in, wd_in, out
    v.rows_dram = nc.dram_tensor("rows_dram", (T + 1, ROW), F32, kind="Internal").ap()
    v.krep_dram = nc.dram_tensor("krep_dram", (HEADS, P * KW), F32, kind="Internal").ap()
    v.z_dram = nc.dram_tensor("z_dram", (NZ, D), F32, kind="Internal").ap()

    with ExitStack() as stack:
        def sb(name, shape, dt=F32):
            return stack.enter_context(nc.sbuf_tensor(name, shape, dt))

        def sem(name):
            return stack.enter_context(nc.semaphore(name))

        v.cols = sb("cols", [P, NCOLS])
        v.outb, v.downb = sb("outb", [P, D]), sb("downb", [P, D])
        v.d_sb = sb("d_sb", [P, HEADS])
        v.ident = sb("ident", [P, P])
        v.ones = sb("ones", [P, NB * E])
        v.zeros = sb("zeros", [P, 512])
        v.eps_rms, v.eps_ln, v.one = sb("eps_rms", [P, 1]), sb("eps_ln", [P, 1]), sb("one", [P, 1])
        v.lru = sb("lru", [P, 3, C])
        v.tnum = sb("tnum", [P, NB])
        v.zbase = sb("zbase", [P, NB])
        v.empty_row = sb("empty_row", [1, ROW])
        v.wsh = sb("wsh", [P, C, 2 * FS])
        v.wshd = sb("wshd", [P, len(FSC), D])
        v.wgate = sb("wgate", [P, C, E])
        v.x3T = sb("x3T", [P, C, T])
        v.votes = sb("votes", [P, B, E])
        v.first = sb("first", [E, CAP])
        v.firstd = sb("firstd", [E, 2, CAP])
        v.idx_all = sb("idx_all", [P, EP + RING], I32)
        v.idx_slot = sb("idx_slot", [P, RING], I32)
        v.z_slot = sb("z_slot", [P, RING], I32)
        v.pz_slot = sb("pz_slot", [P, RING, 2])

        wregion = sb("wregion", [P, 11264])
        at = [0]

        def take(n, region=None):
            v = (region or wregion)[:, at[0]:at[0] + n]
            at[0] += n
            return v

        v.wlr = take(C * 2 * D).rearrange("p (c n) -> p c n", c=C)
        v.wg = take(C * 2 * D).rearrange("p (c n) -> p c n", c=C)
        v.wo = take(C * D).rearrange("p (c n) -> p c n", c=C)
        v.wup = take(C * 2 * F).rearrange("p (c n) -> p c n", c=C)
        v.wdn = take(FJ * D).rearrange("p (c n) -> p c n", c=FJ)
        v.toep = take(HEADS * 2 * P).rearrange("p (h n) -> p h n", h=HEADS)
        at[0] = 0
        v.wgu = [take(2 * C * 2 * FE).rearrange("p (e c n) -> p e c n", e=2, c=C) for _ in range(RING)]
        v.wd = [take(2 * 2 * D).rearrange("p (e f n) -> p e f n", e=2, f=2) for _ in range(RING)]

        hregion = sb("hregion", [P, 13400])
        at[0] = 0
        v.xin = take(NB * D, hregion).rearrange("p (b n) -> p b n", b=NB)
        v.xn = take(NB * D, hregion).rearrange("p (b n) -> p b n", b=NB)
        v.xT = take(C * TG, hregion).rearrange("p (c n) -> p c n", c=C)
        v.left = take(C * TG, hregion).rearrange("p (c n) -> p c n", c=C)
        rt = take(C * NB * (S + 3), hregion)
        v.rtv = rt.rearrange("p (c b n) -> p c b n", c=C, b=NB)
        v.hs = take(C * TG, hregion).rearrange("p (c n) -> p c n", c=C)
        v.cv = take(C * TG, hregion).rearrange("p (c n) -> p c n", c=C)
        v.mlp = take(FJ * TG, hregion).rearrange("p (c n) -> p c n", c=FJ)
        v.ri = v.mlp[:, 0:4, :]
        v.th = v.mlp[:, 4:6, :]
        v.xo = take(NB * D, hregion).rearrange("p (b n) -> p b n", b=NB)
        v.xs = take(NB * D, hregion).rearrange("p (b n) -> p b n", b=NB)
        v.gl = take(2 * TG, hregion).rearrange("p (k n) -> p k n", k=2)
        at[0] = 0
        v.shared = take(B * D, hregion).rearrange("p (b n) -> p b n", b=B)
        v.sgl = take(len(FSC) * TG, hregion).rearrange("p (f n) -> p f n", f=len(FSC))
        v.shh = take(len(FSC) * TG, hregion).rearrange("p (f n) -> p f n", f=len(FSC))
        v.xg = take(RING * ROW, hregion).rearrange("p (r n) -> p r n", r=RING)
        v.xgT = take(2 * C * P, hregion).rearrange("p (k c n) -> p k c n", k=2, c=C)
        v.sge = take(2 * 4 * CAP, hregion).rearrange("p (k n) -> p k n", k=2)
        v.he = take(2 * 4 * CAP, hregion).rearrange("p (k e f n) -> p k e f n", k=2, e=2, f=2)
        v.dout = take(RING * D, hregion).rearrange("p (r n) -> p r n", r=RING)
        v.zin = v.x3T[:, :, :].rearrange("p c n -> p (c n)")[:, 0:2 * TOPK * D].rearrange("p (k n) -> p k n", k=2)

        v.cin = sb("cin", [P, NB, D])
        v.ctxT = sb("ctxT", [P, C, S * NB])
        v.kv = sb("kv", [P, 2, C, 4, PW])
        v.ycv = sb("ycv", [P, C, HEADS, PW])
        v.votesT = v.ycv[0:E].rearrange("p c h n -> p (c h n)")[:, 0:T]
        v.x2 = sb("x2", [P, NB, D])
        v.q = sb("q", [P, C, HEADS, HD * NB])
        v.acc = sb("acc", [P, C, HEADS, HD * NB])
        v.tmp = sb("tmp", [P, 2, C, HEADS, (HD - 1) * NB])
        v.u = sb("u", [P, NB, D])
        v.rows = sb("rows", [P, NB, ROW])
        v.logit = sb("logit", [P, NB, E])
        v.pp = sb("pp", [P, NB, E + 2])
        v.pr = sb("pr", [P, NB, E + 2])
        v.mask = sb("mask", [P, NB, E])
        v.cum = sb("cum", [P, NB, E])
        v.m8 = sb("m8", [P, NB, 8])
        st = sb("st", [P, 12, NB])
        v.bn = sb("bn", [P, 3, NB, 6])
        v.mv = sb("mv", [P, 3, NB, 2])
        v.sdF, v.isF = sb("sdF", [P, 2]), sb("isF", [P, 2])
        v.ss1, v.rms1, v.inv1 = st[:, 0], st[:, 1], st[:, 2]
        v.ss2, v.rms2, v.inv2 = st[:, 3], st[:, 4], st[:, 5]
        v.sdA, v.isA, v.sdB, v.isB, v.mx, v.sm = (st[:, k] for k in range(6, 12))

        v.tb = [stack.enter_context(nc.psum_tensor(f"tb{k}", [P, 512], F32)) for k in range(2)]
        v.mb = [stack.enter_context(nc.psum_tensor(f"mb{k}", [P, 512], F32)) for k in range(4)]
        v.kb = [stack.enter_context(nc.psum_tensor(f"kb{k}", [P, 512], F32)) for k in range(2)]

        names = """consts_in weights_in x_in ctx_in_s idn tables lru_s d_done tnum_s shw_in zero_out 
            ctx_tr ctxT_ready kv_ready conv_done conv_evac
            ss1_s rms1_s inv1_s xn_s x_tr xT_s lr_done left_s right_s cvs gates_done gate_s act_a th_s dve_h
            mult_s lr_s out_done xo_s xs_s x1_s ss2_s rms2_s x1n_s x1_tr x1T_s up_done gelu_s h_s down_done y_s
            lnA_s sdA_s x2_s x2_tr q_s qstep o_tr u_s lnB_s sdB_s x3_s x3_tr x3T_s x3T_all_s logit_done logit_read exp_s
            dve_r rows_s rows_out vote_tr voteT_s pick_s pickT_s idx_s shu_done shg_s shh_s shd_done sh_s x3_in
            wring0 wring1 wring2 wring3 gat0 gat1 gat2 gat3 scat0 scat1 scat2 scat3
            idxc_s pz_s zi_s g_tr gT_s gu_done sg_s he_s dn_done dout_s z0 z1 fdve fsd f_s out0 out1 isB_s isF_s mx_s consts_s krep_out""".split()
        v.s = {n: sem(n) for n in names}

        with nc.Block() as block:
            sync_program(nc, block, v)
            pool_program(nc, block, v)
            act_program(nc, block, v)
            pe_program(nc, block, v)
            dve_program(nc, block, v)


def col(v, name, k, p=P):
    o, n = COLS[name]
    assert k < n
    return v.cols[0:p, o + k:o + k + 1]


def wait(e, sem, value):
    if not (isinstance(value, int) and value <= 0):
        e.wait_ge(sem, value)


def wait_apart(e, v, sem, value):
    if not isinstance(value, int):
        value = e.to_reg(value)
        e.wait_ge(v.s["consts_s"], 1)
    e.wait_ge(sem, value)


def over_groups(e, step):
    step(0, None)
    with e.Fori(1, G) as g:
        step(g, g - 1)
    step(None, G - 1)


def sync_program(nc, block, v):
    s = v.s

    @block.sync
    def _(e):
        def load_x(g):
            if not (isinstance(g, int) and g == 0):
                wait_apart(e, v, s["xn_s"], 4 * g)
                wait(e, s["xo_s"], g)
                wait(e, s["xs_s"], 2 * g)
            e.dma_start(v.xin, v.x[bass.ds(g * NB, NB), :, :].rearrange("b s d -> s b d")).then_inc(s["x_in"], 16)

        def load_ctx(g):
            if not (isinstance(g, int) and g == 0):
                wait(e, s["ctx_tr"], 2 * g)
            e.dma_start(v.cin[:], v.ctx_in[bass.ds(g * NB, NB), :, :].rearrange("b s d -> s b d"))\
                .then_inc(s["ctx_in_s"], 16)

        load_x(0)
        for dst, src in ((v.cols[:], v.cols_in), (v.outb[:], v.outb_in.to_broadcast((P, D))),
                         (v.downb[:], v.downb_in.to_broadcast((P, D))), (v.d_sb[:], v.d_in.to_broadcast((P, HEADS)))):
            e.dma_start(dst, src).then_inc(s["consts_in"], 16)
        for dst, src in ((v.wlr, v.wlr_in), (v.wg, v.wg_in), (v.wo, v.wo_in), (v.wup, v.wup_in), (v.wdn, v.wdn_in)):
            e.dma_start(dst, src).then_inc(s["weights_in"], 16)
        e.dma_start(v.krep_dram.rearrange("h (m n) -> h m n", n=KW), v.kpad_in[:, None, :].to_broadcast((HEADS, P, KW)))\
            .then_inc(s["krep_out"], 16)
        load_ctx(0)
        for dst, src in ((v.wgate[:], v.wgate_in), (v.wsh[:], v.wsh_in), (v.wshd[:], v.wshd_in)):
            e.dma_start(dst, src).then_inc(s["shw_in"], 16)
        e.wait_ge(s["krep_out"], 16)
        k = v.krep_dram[0:HEADS, P - 1:P + 1]
        e.dma_start(v.toep, bass.AP(k.tensor, k.offset, [[KW - 1, P], [P * KW, HEADS], [1, 2 * P]])).then_inc(s["tables"], 16)
        e.wait_ge(s["idn"], 1)
        zv = v.z_dram.rearrange("(k p m) d -> k p (m d)", k=8, p=P)
        for k in range(8):
            e.dma_start(zv[k].rearrange("p (r n) -> p r n", n=512), v.zeros[:, None, :].to_broadcast((P, NZ * D // 8 // P // 512, 512)))\
                .then_inc(s["zero_out"], 16)
        e.wait_ge(s["logit_read"], 1)
        e.dma_start(v.rows_dram[T:T + 1, :], v.empty_row[:]).then_inc(s["rows_out"], 16)

        with e.Fori(1, G) as g:
            load_x(g)
            load_ctx(g)
            wait_apart(e, v, s["rows_s"], g)
            e.dma_start(v.rows_dram[bass.ds((g - 1) * TG, TG), :].rearrange("(b s) n -> s b n", s=S), v.rows[:])\
                .then_inc(s["rows_out"], 16)

        def load_pair(p, r):
            e.dma_start(v.wgu[r], v.wgu_in[bass.ds(p, 1)].rearrange("o p e c n -> (o p) e c n"))\
                .then_inc(s[f"wring{r}"], 16)
            e.dma_start(v.wd[r][0:FH], v.wd_in[bass.ds(p, 1)].rearrange("o p e f n -> (o p) e f n"))\
                .then_inc(s[f"wring{r}"], 16)

        e.wait_ge(s["down_done"], 2 * G)
        e.wait_ge(s["conv_done"], HEADS * G)
        for r in range(RING):
            load_pair(r, r)
        e.wait_ge(s["rows_s"], G)
        e.dma_start(v.rows_dram[(G - 1) * TG:T, :].rearrange("(b s) n -> s b n", s=S), v.rows[:])\
            .then_inc(s["rows_out"], 16)
        e.wait_ge(s["rows_out"], 16 * (G + 1))
        e.dma_start(v.shared, v.rows_dram[0:T, 0:D].rearrange("(b s) n -> s b n", s=S)).then_inc(s["x3_in"], 16)
        with e.Fori(1, EP // RING) as o:
            for r in range(RING):
                wait(e, s["dn_done"], (o - 1) * RING + r + 1)
                load_pair(o * RING + r, r)

        for r in range(RING):
            e.wait_ge(s[f"scat{r}"], 16 * (EP // RING))
        e.wait_ge(s["zero_out"], 16 * 8)
        e.wait_ge(s["shu_done"], 2 * len(FSC) * G)

        def load_z(b, k):
            e.dma_start(v.zin[:, k, :], v.z_dram[bass.ds(b * S * TOPK, S * TOPK), :].rearrange("(s k) d -> s (k d)", k=TOPK))\
                .then_inc(s[f"z{k}"], 16)

        def store(b, k, n):
            e.wait_ge(s["f_s"], n)
            e.dma_start(v.out[bass.ds(b, 1), :, :].rearrange("b s d -> (b s) d"), v.x2[:, k, :]).then_inc(s[f"out{k}"], 16)

        for k in range(2):
            load_z(k, k)
        with e.Fori(1, B // 2) as i:
            for k in range(2):
                wait(e, s["fdve"], ((i - 1) * 2 + k) * FDVE + 1)
                load_z(2 * i + k, k)
                store(2 * (i - 1) + k, k, 2 * (i - 1) + k + 1)
        for k in range(2):
            store(B - 2 + k, k, B - 2 + k + 1)
        for k in range(2):
            e.wait_ge(s[f"out{k}"], 16 * (B // 2))


FDVE = 4
HDVE = 9
RDVE = 12


def pool_program(nc, block, v):
    s = v.s

    @block.gpsimd
    def _(e):
        e.memset(v.zeros[:], 0.0).then_inc(s["idn"], 1)
        e.memset(v.ident[:], 0.0).then_inc(s["idn"], 1)
        e.wait_ge(s["idn"], 2)
        e.affine_select(out=v.ident[:], in_=v.ident[:], compare_op=ALU.not_equal, fill=1.0, base=0,
                        pattern=[[-1, P]], channel_multiplier=1).then_inc(s["idn"], 1)
        e.iota(v.tnum[:], pattern=[[-S, NB]], base=4096, channel_multiplier=-1, allow_small_or_imprecise_dtypes=True)
        e.iota(v.zbase[:], pattern=[[TOPK * S - TOPK, NB]], base=0, channel_multiplier=TOPK,
               allow_small_or_imprecise_dtypes=True).then_inc(s["tnum_s"], 1)
        e.wait_ge(s["tables"], 16)
        e.wait_ge(s["consts_in"], 16 * 4)
        e.wait_ge(s["idn"], 3)
        dtmp = v.ycv[:, 0, :, 0:P]
        e.tensor_tensor(dtmp, v.ident[:, None, :].to_broadcast((P, HEADS, P)),
                        v.d_sb[:, :, None].to_broadcast((P, HEADS, P)), ALU.mult).then_inc(s["d_done"], 1)
        e.wait_ge(s["d_done"], 1)
        e.tensor_tensor(v.toep[:, :, 0:P], v.toep[:, :, 0:P], dtmp, ALU.add).then_inc(s["d_done"], 1)

        def products(gt, hb):
            wait(e, s["ctxT_ready"], 2 * gt + 2)
            if hb >= 2:
                wait(e, s["conv_done"], HEADS * gt + 4 * (hb - 1))
            cx = v.ctxT[:].rearrange("p c (h n) -> p c h n", h=HEADS)[:, :, 4 * hb:4 * hb + 4, :]
            for d in range(HD):
                n = (HD - d) * NB
                last = e.tensor_tensor(v.kv[:, hb % 2, :, :, DOFF[d] * NB:DOFF[d] * NB + n],
                                       cx[:, :, :, 0:n], cx[:, :, :, d * NB:d * NB + n], ALU.mult)
            last.then_inc(s["kv_ready"], 1)

        def step(gh, gt):
            if gt is not None:
                products(gt, 0)
                products(gt, 1)
            if gh is not None:
                wait(e, s["x_in"], 16 * gh + 16)
                if not (isinstance(gh, int) and gh == 0):
                    wait(e, s["x2_s"], 4 * gh)
                    wait(e, s["x1n_s"], 4 * gh)
                e.tensor_tensor(v.xo, v.xin, v.outb[:, None, :].to_broadcast((P, NB, D)), ALU.add)\
                    .then_inc(s["xo_s"], 1)
                e.tensor_tensor(v.xs, v.xin, v.downb[:, None, :].to_broadcast((P, NB, D)), ALU.add)\
                    .then_inc(s["xs_s"], 1)
            if gt is not None:
                products(gt, 2)
                products(gt, 3)
            if gh is not None:
                wait(e, s["x1_s"], 2 * gh + 2)
                wait(e, s["xs_s"], 2 * gh + 1)
                e.tensor_tensor(v.xs, v.xs, v.xo, ALU.add).then_inc(s["xs_s"], 1)

        over_groups(e, step)

        def gather(r):
            e.indirect_dma_start(out=v.xg[:, r, :], out_offset=None, in_=v.rows_dram[:, :],
                                 in_offset=bass.IndirectOffsetOnAxis(ap=v.idx_slot[:, r:r + 1], axis=0))\
                .then_inc(s[f"gat{r}"], 16)

        def scatter(r):
            e.indirect_dma_start(out=v.z_dram[:, :], out_offset=bass.IndirectOffsetOnAxis(ap=v.z_slot[:, r:r + 1], axis=0),
                                 in_=v.dout[:, r, :], in_offset=None, bounds_check=NZ - 1, oob_is_err=False)\
                .then_inc(s[f"scat{r}"], 16)

        e.wait_ge(s["rows_out"], 16 * (G + 1))
        e.wait_ge(s["idxc_s"], 1)
        for r in range(RING):
            gather(r)
        e.wait_ge(s["zero_out"], 16 * 8)
        with e.Fori(0, EP // RING - 1) as o:
            for r in range(RING):
                wait_apart(e, v, s["dout_s"], o * RING + r + 1)
                scatter(r)
                wait_apart(e, v, s["idxc_s"], o * RING + r + 2)
                wait(e, s["g_tr"], o * RING + r + 1)
                gather(r)
        for r in range(RING):
            e.wait_ge(s["dout_s"], EP - RING + r + 1)
            scatter(r)


def act_program(nc, block, v):
    s = v.s

    @block.scalar
    def _(e):
        o, n = COLS["a_param"]
        ap = v.cols[:, o:o + n]
        e.wait_ge(s["consts_in"], 16 * 4)
        e.activation(v.lru[:, 0], ap, ACT.Abs).then_inc(s["lru_s"], 1)
        e.wait_ge(s["lru_s"], 1)
        e.activation(v.lru[:, 0], v.lru[:, 0], ACT.Exp, scale=-1.0).then_inc(s["lru_s"], 1)
        e.wait_ge(s["lru_s"], 2)
        e.wait_ge(s["consts_s"], 1)
        e.activation(v.lru[:, 0], v.lru[:, 0], ACT.Ln, bias=v.one[:]).then_inc(s["lru_s"], 1)
        e.activation(v.lru[:, 2], ap, ACT.Relu).then_inc(s["lru_s"], 1)

        def step(gh, gt):
            head, tail = gh is not None, gt is not None

            def conv_out(h):
                wait(e, s["conv_done"], HEADS * gt + h + 1)
                e.activation(v.ycv[:, :, h, :], v.mb[h % 4][:, 0:C * PW].rearrange("p (c n) -> p c n", c=C), ACT.Copy)\
                    .then_inc(s["conv_evac"], 1)

            def mean_square(src, dst, name):
                for b in range(NB):
                    last = e.activation(v.xn[:, b, :], src[:, b, :], ACT.Square, accum_out=dst[:, b:b + 1])
                last.then_inc(s[name], 1)

            if tail:
                for k in range(2):
                    wait(e, s["ctx_tr"], 2 * gt + k + 1)
                    e.activation(v.ctxT[:].rearrange("p c (s b) -> p b c s", b=NB)[:, 2 * k:2 * k + 2],
                                 v.tb[k][:].rearrange("p (b c s) -> p b c s", b=2, c=C), ACT.Copy)\
                        .then_inc(s["ctxT_ready"], 1)
            if head:
                wait(e, s["x_in"], 16 * gh + 16)
                if not (isinstance(gh, int) and gh == 0):
                    wait(e, s["x1_tr"], 2 * gh)
                mean_square(v.xin, v.ss1, "ss1_s")
                wait(e, s["ss1_s"], gh + 1)
                e.activation(v.rms1, v.ss1, ACT.Sqrt, scale=1.0 / D, bias=v.eps_rms[:]).then_inc(s["rms1_s"], 1)
            if tail:
                for h in range(4):
                    conv_out(h)
            if head:
                for c in range(C):
                    wait(e, s["lr_done"], 4 * gh + c + 1)
                    e.activation(v.left[:, c, :], v.mb[c][:], ACT.Gelu, bias=col(v, "left_b", c)).then_inc(s["left_s"], 1)
                for c in range(C):
                    wait(e, s["lr_done"], 4 * gh + C + c + 1)
                    e.activation(v.rtv[:, c, :, 3:], v.mb[C + c][:].rearrange("p (b n) -> p b n", b=NB), ACT.Identity,
                                 bias=col(v, "right_b", c)).then_inc(s["right_s"], 1)
            if tail:
                for h in range(4, 8):
                    conv_out(h)
            if head:
                for k in range(2 * C):
                    wait(e, s["gates_done"], 4 * gh + k + 1)
                    e.activation(v.ri[:, k, :], v.mb[k][:], ACT.Sigmoid, bias=col(v, ("ga_b", "gx_b")[k // C], k % C))\
                        .then_inc(s["gate_s"], 1)
                wait(e, s["gate_s"], 4 * gh + 2)
                wait(e, s["lru_s"], 6)
                for c in range(C):
                    e.activation(v.th[:, c, :], v.ri[:, c, :], ACT.Tanh, scale=v.lru[:, 0, c:c + 1]).then_inc(s["th_s"], 1)
                for c in range(C):
                    e.activation(v.ri[:, c, :], v.ri[:, c, :], ACT.Exp, scale=v.lru[:, 1, c:c + 1]).then_inc(s["act_a"], 1)
            if tail:
                for h in range(8, 12):
                    conv_out(h)
            if head:
                wait(e, s["dve_h"], HDVE * gh + 3)
                e.activation(v.th, v.th, ACT.Sqrt).then_inc(s["mult_s"], 1)
            if tail:
                for h in range(12, 16):
                    conv_out(h)
            if head:
                wait(e, s["x1_s"], 2 * gh + 2)
                wait(e, s["x_tr"], 2 * gh + 2)
                mean_square(v.xo, v.ss2, "ss2_s")
                wait(e, s["ss2_s"], gh + 1)
                e.activation(v.rms2, v.ss2, ACT.Sqrt, scale=1.0 / D, bias=v.eps_rms[:]).then_inc(s["rms2_s"], 1)
                for j in range(FJ):
                    wait(e, s["up_done"], 2 * FJ * gh + 2 * j + 1)
                    if j >= 2:
                        wait(e, s["h_s"], FJ * gh + j - 1)
                    e.activation(v.gl[:, j % 2, :], v.mb[2 * j % 4][:], ACT.Gelu, bias=col(v, "up1_b", j))\
                        .then_inc(s["gelu_s"], 1)
            if tail:
                wait(e, s["lnB_s"], gt + 1)
                e.activation(v.sdB, v.mv[:, 1, :, 1], ACT.Sqrt, bias=v.eps_ln[:]).then_inc(s["sdB_s"], 1)
                for k in range(2):
                    wait(e, s["x3_tr"], 2 * gt + k + 1)
                    e.activation(v.x3T[:, :, bass.ds(gt * TG + k * 2 * S, 2 * S)].rearrange("p c (b s) -> p b c s", b=2),
                                 v.tb[k][:].rearrange("p (b c s) -> p b c s", b=2, c=C), ACT.Copy)\
                        .then_inc(s["x3T_all_s"], 1)
                    e.activation(v.ctxT[:].rearrange("p c (b s) -> p b c s", b=NB)[:, 2 * k:2 * k + 2],
                                 v.tb[k][:].rearrange("p (b c s) -> p b c s", b=2, c=C), ACT.Copy)\
                        .then_inc(s["x3T_s"], 1)
            if head:
                wait(e, s["lnA_s"], gh + 1)
                e.activation(v.sdA, v.mv[:, 0, :, 1], ACT.Sqrt, bias=v.eps_ln[:]).then_inc(s["sdA_s"], 1)
            if tail:
                wait(e, s["logit_read"], gt + 2)
                e.activation(v.logit[:], v.logit[:], ACT.Exp).then_inc(s["exp_s"], 1)

        over_groups(e, step)

        with e.Fori(0, G) as g:
            for f, n in enumerate(FSC):
                wait(e, s["shu_done"], (g * len(FSC) + f) * 2 + 1)
                e.activation(v.sgl[0:n, f, :], v.mb[2 * f % 4][0:n, :], ACT.Silu).then_inc(s["shg_s"], 1)

        with e.Fori(0, EP // RING) as o:
            for r in range(RING):
                p = o * RING + r
                wait(e, s["g_tr"], p + 1)
                e.activation(v.xgT[:, r % 2], v.tb[r % 2][:, 0:C * P].rearrange("p (c n) -> p c n", c=C), ACT.Copy)\
                    .then_inc(s["gT_s"], 1)
                wait(e, s["gu_done"], p + 1)
                e.activation(v.sge[0:FH, r % 2, :], v.mb[r % 2][0:FH, 0:4 * CAP], ACT.Silu).then_inc(s["sg_s"], 1)

        with e.Fori(0, B // 2) as i:
            for k in range(2):
                n = i * 2 + k
                wait(e, s["fdve"], n * FDVE + 4)
                e.activation(v.sdF[:, k:k + 1], v.mv[:, 2, k, 1:2], ACT.Sqrt, bias=v.eps_ln[:]).then_inc(s["fsd"], 1)


def pe_program(nc, block, v):
    s = v.s
    tb, mb, kb = v.tb, v.mb, v.kb

    @block.tensor
    def _(e):
        def transposes(src, k, done):
            for b in range(2):
                for c in range(C):
                    last = e.transpose(tb[k][:, (b * C + c) * P:(b * C + c + 1) * P], src[:, 2 * k + b, c * P:(c + 1) * P],
                                       v.ident[:])
            last.then_inc(s[done], 1)

        def dense(bank, w, n0, rhs, done):
            for c in range(C):
                last = e.matmul(bank, w[:, c, n0:n0 + P], rhs[:, c, :], start=(c == 0), stop=(c == C - 1))
            last.then_inc(s[done], 1)

        e.wait_ge(s["idn"], 3)

        def step(gh, gt):
            head, tail = gh is not None, gt is not None

            def conv(h):
                if h % 4 == 0:
                    wait(e, s["kv_ready"], 4 * gt + h // 4 + 1)
                o = mb[h % 4]
                k = v.kv[:, h // 4 % 2, :, h % 4, :]
                e.matmul(o[:, 0:PW], v.toep[:, h, 0:P], k[:, 0, :], start=True, stop=True)
                e.matmul(o[:, PW:2 * PW], v.toep[:, h, P:2 * P], k[:, 0, :], start=True, stop=False)
                e.matmul(o[:, PW:2 * PW], v.toep[:, h, 0:P], k[:, 1, :], start=False, stop=True)\
                    .then_inc(s["conv_done"], 1)

            if tail:
                wait(e, s["ctx_in_s"], 16 * gt + 16)
                for k in range(2):
                    transposes(v.cin, k, "ctx_tr")
                wait(e, s["logit_read"], gt + 1)
                e.wait_ge(s["d_done"], 2)
                for h in range(4):
                    conv(h)
            if head:
                wait(e, s["xn_s"], 4 * gh + 4)
                if tail:
                    wait(e, s["ctxT_ready"], 2 * gt + 2)
                for k in range(2):
                    transposes(v.xn, k, "x_tr")
                e.wait_ge(s["weights_in"], 16 * 5)
                wait(e, s["xT_s"], 4 * gh + 4)
                for k in range(4):
                    if tail:
                        wait(e, s["conv_evac"], HEADS * gt + k + 1)
                    dense(mb[k][:], v.wlr, k * P, v.xT, "lr_done")
            if tail:
                for h in range(4, 8):
                    if head:
                        wait(e, s["left_s"] if h < 6 else s["right_s"], 2 * gh + h % 2 + 1)
                    else:
                        wait(e, s["conv_evac"], HEADS * gt + h - 3)
                    conv(h)
            if head:
                wait(e, s["cvs"], 8 * gh + 8)
                for k in range(4):
                    if tail:
                        wait(e, s["conv_evac"], HEADS * gt + 5 + k)
                    else:
                        wait(e, s["left_s"] if k < 2 else s["right_s"], 2 * gh + k % 2 + 1)
                    dense(mb[k][:], v.wg, k * P, v.cv, "gates_done")
            if tail:
                wait(e, s["x2_s"], 4 * gt + 4)
                if not head:
                    wait(e, s["ctxT_ready"], 2 * gt + 2)
                for k in range(2):
                    transposes(v.x2, k, "x2_tr")
                for h in range(8, 16):
                    if head and h < 12:
                        wait(e, s["gate_s"], 4 * gh + h - 7)
                    else:
                        wait(e, s["conv_evac"], HEADS * gt + h - 3)
                    conv(h)
            if head:
                wait(e, s["lr_s"], gh + 1)
                if not (isinstance(gh, int) and gh == 0):
                    wait(e, s["y_s"], 2 * gh)
                for k in range(2):
                    for b in range(2):
                        for c in range(C):
                            t0 = (2 * k + b) * S
                            last = e.matmul(kb[k][:, b * D:(b + 1) * D], v.left[:, c, t0:t0 + S], v.wo[:, c, :],
                                            start=(c == 0), stop=(c == C - 1))
                    last.then_inc(s["out_done"], 1)
                if tail:
                    wait(e, s["q_s"], 2 * gt + 2)
                wait(e, s["x1n_s"], 4 * gh + 4)
                for k in range(2):
                    transposes(v.xn, k, "x1_tr")
                wait(e, s["x1T_s"], 4 * gh + 4)
                for j in range(FJ):
                    for k in range(2):
                        i = 2 * j + k
                        if i < 4 and tail:
                            wait(e, s["conv_evac"], HEADS * gt + 13 + i)
                        elif i < 4:
                            wait(e, s["gate_s"], 4 * gh + i + 1)
                        else:
                            wait(e, s["gelu_s"] if k == 0 else s["h_s"], FJ * gh + j - 1)
                        dense(mb[i % 4][:], v.wup, k * F + j * P, v.xT, "up_done")
            if tail:
                wait(e, s["qstep"], QSTEPS * gt + QSTEPS)
                if not head:
                    wait(e, s["q_s"], 2 * gt + 2)
                for k in range(2):
                    for b in range(2):
                        for c in range(C):
                            last = e.transpose(tb[k][:, (b * C + c) * P:(b * C + c + 1) * P],
                                               v.acc[:, c].rearrange("p h (i b) -> p (h i) b", b=NB)[:, :, 2 * k + b],
                                               v.ident[:])
                    last.then_inc(s["o_tr"], 1)
            if head:
                wait(e, s["h_s"], FJ * gh + FJ)
                wait(e, s["x1_s"], 2 * gh + 2)
                for k in range(2):
                    for b in range(2):
                        for j in range(FJ):
                            t0 = (2 * k + b) * S
                            last = e.matmul(kb[k][:, b * D:(b + 1) * D], v.mlp[:, j, t0:t0 + S], v.wdn[:, j, :],
                                            start=(j == 0), stop=(j == FJ - 1))
                    last.then_inc(s["down_done"], 1)
            if tail:
                e.wait_ge(s["shw_in"], 16 * 3)
                wait(e, s["x3_s"], 4 * gt + 4)
                for k in range(2):
                    transposes(v.rows, k, "x3_tr")
                wait(e, s["x3T_s"], 2 * gt + 2)
                if not head:
                    wait(e, s["conv_evac"], HEADS * gt + HEADS)
                for b in range(NB):
                    for c in range(C):
                        last = e.matmul(mb[0][:, b * E:(b + 1) * E], v.ctxT[:, c, b * S:(b + 1) * S], v.wgate[:, c, :],
                                        start=(c == 0), stop=(c == C - 1))
                last.then_inc(s["logit_done"], 1)

        over_groups(e, step)

        e.wait_ge(s["dve_r"], RDVE * G)
        for k in range(G):
            if k >= 2:
                e.wait_ge(s["voteT_s"], k - 1)
            for b in range(NB):
                last = e.transpose(tb[k % 2][0:E, b * S:(b + 1) * S], v.votes[:, NB * k + b, :], v.ident[:])
            last.then_inc(s["vote_tr"], 1)

        NF = len(FSC)
        e.wait_ge(s["x3T_all_s"], 2 * G)
        e.wait_ge(s["logit_read"], G + 1)
        e.wait_ge(s["y_s"], 2 * G)

        def shared(g, again):
            for f, n in enumerate(FSC):
                for k in range(2):
                    i = 2 * f + k
                    if i >= 4:
                        wait(e, s["shg_s"] if k == 0 else s["shh_s"], NF * g + f - 1)
                    elif again:
                        wait(e, s["shg_s"] if k == 0 else s["shh_s"], NF * g)
                    for c in range(C):
                        last = e.matmul(mb[i % 4][0:n, :], v.wsh[:, c, k * FS + f * P:k * FS + f * P + n],
                                        v.x3T[:, c, bass.ds(g * TG, TG)], start=(c == 0), stop=(c == C - 1))
                    last.then_inc(s["shu_done"], 1)
            wait(e, s["shh_s"], NF * g + NF)
            for k in range(2):
                if again:
                    wait(e, s["sh_s"], 2 * g - 1 + k)
                for b in range(2):
                    for f, n in enumerate(FSC):
                        t0 = (2 * k + b) * S
                        last = e.matmul(kb[k][:, b * D:(b + 1) * D], v.shh[0:n, f, t0:t0 + S], v.wshd[0:n, f, :],
                                        start=(f == 0), stop=(f == NF - 1))
                last.then_inc(s["shd_done"], 1)

        shared(0, False)
        with e.Fori(1, G) as g:
            shared(g, True)

        e.wait_ge(s["pick_s"], 17)
        e.transpose(tb[0][:, 0:E], v.firstd[:].rearrange("p k n -> p (k n)"), v.ident[0:E, 0:E]).then_inc(s["pickT_s"], 1)
        e.wait_ge(s["idx_s"], 2)
        e.wait_ge(s["sh_s"], 2 * G)
        e.wait_ge(s["shh_s"], NF * G)

        def place_rows(o, r):
            p = o * RING + r
            wait(e, s[f"gat{r}"], 16 * o + 16)
            if not (isinstance(p, int) and p < 2):
                wait(e, s["gT_s"], p - 1)
            for c in range(C):
                last = e.transpose(tb[r % 2][:, c * P:(c + 1) * P], v.xg[:, r, c * P:(c + 1) * P], v.ident[:])
            last.then_inc(s["g_tr"], 1)

        def gate_up(o, r):
            p = o * RING + r
            wait(e, s["gT_s"], p + 1)
            wait(e, s[f"wring{r}"], 32 * o + 32)
            if not (isinstance(p, int) and p < 2):
                wait(e, s["he_s"], p - 1)
            for k in range(2):
                for x in range(2):
                    for f in range(2):
                        o1 = mb[r % 2][0:FH, k * 256 + (2 * x + f) * CAP:k * 256 + (2 * x + f + 1) * CAP]
                        for c in range(C):
                            last = e.matmul(o1, v.wgu[r][:, x, c, k * FE + f * FH:k * FE + (f + 1) * FH],
                                            v.xgT[:, r % 2, c, x * CAP:(x + 1) * CAP], start=(c == 0), stop=(c == C - 1))
            last.then_inc(s["gu_done"], 1)

        def down(p, r):
            wait(e, s["he_s"], p + 1)
            if not (isinstance(p, int) and p < 2):
                wait(e, s["dout_s"], p - 1)
            for x in range(2):
                for f in range(2):
                    last = e.matmul(kb[r % 2][x * CAP:(x + 1) * CAP, 0:D], v.he[0:FH, r % 2, x, f, :], v.wd[r][0:FH, x, f, :],
                                    start=(f == 0), stop=(f == 1))
            last.then_inc(s["dn_done"], 1)

        def turn(o):
            for r in range(RING):
                p = o * RING + r
                place_rows(o, r)
                if not (isinstance(p, int) and p < 2):
                    down(p - 2, (r - 2) % RING)
                gate_up(o, r)

        turn(0)
        with e.Fori(1, EP // RING) as o:
            turn(o)
        for r in (2, 3):
            down(EP - RING + r, r)


QSTEPS = 1 + 4 * (HD - 1)


def dve_program(nc, block, v):
    s = v.s
    tb, mb, kb = v.tb, v.mb, v.kb
    hsteps, rsteps, qsteps = Steps(s["dve_h"], HDVE), Steps(s["dve_r"], RDVE), Steps(s["qstep"], QSTEPS)

    @block.vector
    def _(e):
        e.memset(v.eps_rms[:], EPS_RMS)
        e.memset(v.eps_ln[:], EPS_LN)
        e.memset(v.one[:], 1.0)
        e.memset(v.ones[:], 1.0)
        e.memset(v.pp[:], 2.0)
        e.memset(v.rtv[:, :, :, 0:3], 0.0)
        e.memset(v.empty_row[:], 0.0)
        e.memset(v.idx_all[:], T).then_inc(s["consts_s"], 1)
        e.wait_ge(s["consts_s"], 1)
        e.memset(v.empty_row[0:1, D:ROW], float(4 * NZ)).then_inc(s["logit_read"], 1)
        e.wait_ge(s["lru_s"], 4)
        e.tensor_tensor(v.lru[:, 0], v.lru[:, 0], v.lru[:, 2], ALU.add).then_inc(s["lru_s"], 1)
        e.wait_ge(s["lru_s"], 5)
        e.tensor_scalar(v.lru[:, 1], v.lru[:, 0], -LRU_C, None, ALU.mult)
        e.tensor_scalar(v.lru[:, 0], v.lru[:, 0], LRU_C, None, ALU.mult).then_inc(s["lru_s"], 1)
        e.wait_ge(s["tnum_s"], 1)

        def norm_apply(dst, src, inv, done):
            for b in range(NB):
                e.tensor_scalar(dst[:, b, :], src[:, b, :], inv[:, b:b + 1], None, ALU.mult).then_inc(s[done], 1)

        def feature_copy(k, name, done):
            for c in range(C):
                e.tensor_scalar(v.xT[:, c, k * 2 * S:(k + 1) * 2 * S].rearrange("p (b s) -> p b s", b=2),
                                tb[k][:].rearrange("p (b c s) -> p b c s", b=2, c=C)[:, :, c, :],
                                col(v, name, c), None, ALU.mult).then_inc(s[done], 1)

        def step(gh, gt):
            head, tail = gh is not None, gt is not None
            if head:
                hsteps.begin(gh)
                wait(e, s["rms1_s"], gh + 1)
                e.reciprocal(v.inv1, v.rms1).then_inc(s["inv1_s"], 1)
                wait(e, s["inv1_s"], gh + 1)
                norm_apply(v.xn, v.xin, v.inv1, "xn_s")
                for k in range(2):
                    wait(e, s["x_tr"], 2 * gh + k + 1)
                    feature_copy(k, "norm1", "xT_s")
                for c in range(C):
                    wait(e, s["right_s"], 2 * gh + c + 1)
                    o = v.cv[:, c, :].rearrange("p (b n) -> p b n", b=NB)
                    e.tensor_scalar(o, v.rtv[:, c, :, 0:S], col(v, "conv_w", c), col(v, "conv_b", c), ALU.mult, ALU.add)\
                        .then_inc(s["cvs"], 1)
                for k in range(1, 4):
                    for c in range(C):
                        o = v.cv[:, c, :].rearrange("p (b n) -> p b n", b=NB)
                        wait(e, s["cvs"], 8 * gh + 2 * k - 1 + c)
                        e.scalar_tensor_tensor(out=o, in0=v.rtv[:, c, :, k:k + S], scalar=col(v, "conv_w", C * k + c),
                                               in1=o, op0=ALU.mult, op1=ALU.add).then_inc(s["cvs"], 1)
            if tail:
                for k in range(2):
                    wait(e, s["x2_tr"], 2 * gt + k + 1)
                    e.tensor_copy(v.q[:].rearrange("p c h (i b) -> p b c (h i)", b=NB)[:, 2 * k:2 * k + 2],
                                  tb[k][:].rearrange("p (b c s) -> p b c s", b=2, c=C)).then_inc(s["q_s"], 1)
            if head:
                a, i = v.ri[:, 0:2, :], v.ri[:, 2:4, :]
                wait(e, s["gate_s"], 4 * gh + 4)
                wait(e, s["gates_done"], 4 * gh + 4)
                wait(e, s["cvs"], 8 * gh + 8)
                hsteps.did(e.tensor_tensor(i, i, v.cv, ALU.mult))
                wait(e, s["act_a"], 2 * gh + 2)
                n = hsteps.did(e.tensor_tensor(v.hs, a, a, ALU.mult))
                wait(e, hsteps.sem, n)
                wait(e, s["th_s"], 2 * gh + 2)
                hsteps.did(e.scalar_tensor_tensor(out=v.th, in0=v.hs, scalar=1.0, in1=v.th, op0=ALU.add, op1=ALU.mult))
                n = hsteps.did(e.memset(v.ri[:, 0:2, :].rearrange("p c (b s) -> p (c b) s", b=NB)[:, :, 0:1], 0.0))
                wait(e, s["mult_s"], gh + 1)
                n = hsteps.did(e.tensor_tensor(v.th, v.th, i, ALU.mult))
                wait(e, hsteps.sem, n)
                n = hsteps.did(e.tensor_tensor_scan(v.hs.rearrange("p c n -> p (c n)"), a.rearrange("p c n -> p (c n)"),
                                                    v.th.rearrange("p c n -> p (c n)"), 0.0, ALU.mult, ALU.add))
                wait(e, hsteps.sem, n)
                wait(e, s["left_s"], 2 * gh + 2)
                e.tensor_tensor(v.left, v.left, v.hs, ALU.mult).then_inc(s["lr_s"], 1)
                for k in range(2):
                    wait(e, s["out_done"], 2 * gh + k + 1)
                    wait(e, s["xo_s"], gh + 1)
                    e.tensor_tensor(v.xo[:, 2 * k:2 * k + 2, :], kb[k][:].rearrange("p (b n) -> p b n", b=2),
                                    v.xo[:, 2 * k:2 * k + 2, :], ALU.add).then_inc(s["x1_s"], 1)
                wait(e, s["rms2_s"], gh + 1)
                n = hsteps.did(e.reciprocal(v.inv2, v.rms2))
                wait(e, hsteps.sem, n)
                norm_apply(v.xn, v.xo, v.inv2, "x1n_s")
                for k in range(2):
                    wait(e, s["x1_tr"], 2 * gh + k + 1)
                    feature_copy(k, "norm2", "x1T_s")

            def qy(d):
                n = (HD - d) * NB
                y = v.ycv[:, :, :, DOFF[d] * NB:DOFF[d] * NB + n]
                lo, hi = slice(0, n), slice(d * NB, d * NB + n)
                if d == 0:
                    def only():
                        qsteps.did(e.tensor_tensor(v.acc[:], v.q[:], y, ALU.mult))
                    return [only]

                def product(t, sl):
                    def run():
                        wait(e, qsteps.sem, qsteps.base + qsteps.n)
                        qsteps.did(e.tensor_tensor(v.tmp[:, t, :, :, 0:n], v.q[:, :, :, sl], y, ALU.mult))
                    return run

                def add(t, sl):
                    def run():
                        wait(e, qsteps.sem, qsteps.base + qsteps.n - (1 if t == 0 else 0))
                        qsteps.did(e.tensor_tensor(v.acc[:, :, :, sl], v.acc[:, :, :, sl], v.tmp[:, t, :, :, 0:n], ALU.add))
                    return run
                return [product(0, hi), product(1, lo), add(0, lo), add(1, hi)]

            if tail:
                qsteps.begin(gt)
                parts = [f for d in range(HD) for f in qy(d)]
                wait(e, s["conv_evac"], HEADS * gt + HEADS)
                wait(e, s["q_s"], 2 * gt + 2)
            else:
                parts = []
            if head:
                for j in range(FJ):
                    wait(e, s["gelu_s"], FJ * gh + j + 1)
                    wait(e, s["up_done"], 2 * FJ * gh + 2 * j + 2)
                    e.scalar_tensor_tensor(out=v.mlp[:, j, :], in0=mb[(2 * j + 1) % 4][:], scalar=col(v, "up2_b", j),
                                           in1=v.gl[:, j % 2, :], op0=ALU.add, op1=ALU.mult).then_inc(s["h_s"], 1)
                    for f in parts[5 * j:5 * j + 5]:
                        f()
            else:
                for f in parts:
                    f()
            if tail:
                qsteps.end()
                rsteps.begin(gt)
                for k in range(2):
                    wait(e, s["o_tr"], 2 * gt + k + 1)
                    e.tensor_tensor(v.u[:, 2 * k:2 * k + 2, :], tb[k][:].rearrange("p (b n) -> p b n", b=2),
                                    v.x2[:, 2 * k:2 * k + 2, :], ALU.add).then_inc(s["u_s"], 1)
                wait(e, s["u_s"], 2 * gt + 2)
                for b in range(NB):
                    last = e.bn_stats(v.bn[:, 1, b, :], v.u[:, b, :])
                n = rsteps.did(last)
                wait_apart(e, v, rsteps.sem, n)
                for b in range(NB):
                    last = e.bn_aggr(v.mv[:, 1, b, :], v.bn[:, 1, b, :])
                last.then_inc(s["lnB_s"], 1)
                wait(e, s["sdB_s"], gt + 1)
                e.reciprocal(v.isB, v.sdB).then_inc(s["isB_s"], 1)
                wait(e, s["isB_s"], gt + 1)
                wait(e, s["rows_out"], 16 * gt + 16)
                for b in range(NB):
                    e.tensor_scalar(v.rows[:, b, 0:D], v.u[:, b, :], v.mv[:, 1, b, 0:1], v.isB[:, b:b + 1],
                                    ALU.subtract, ALU.mult).then_inc(s["x3_s"], 1)
            if head:
                for k in range(2):
                    wait(e, s["down_done"], 2 * gh + k + 1)
                    wait(e, s["xs_s"], 2 * gh + 2)
                    e.tensor_tensor(v.xs[:, 2 * k:2 * k + 2, :], kb[k][:].rearrange("p (b n) -> p b n", b=2),
                                    v.xs[:, 2 * k:2 * k + 2, :], ALU.add).then_inc(s["y_s"], 1)
                wait(e, s["y_s"], 2 * gh + 2)
                for b in range(NB):
                    last = e.bn_stats(v.bn[:, 0, b, :], v.xs[:, b, :])
                n = hsteps.did(last)
                wait_apart(e, v, hsteps.sem, n)
                for b in range(NB):
                    last = e.bn_aggr(v.mv[:, 0, b, :], v.bn[:, 0, b, :])
                last.then_inc(s["lnA_s"], 1)
                wait(e, s["sdA_s"], gh + 1)
                n = hsteps.did(e.reciprocal(v.isA, v.sdA))
                wait(e, hsteps.sem, n)
                for b in range(NB):
                    e.tensor_scalar(v.x2[:, b, :], v.xs[:, b, :], v.mv[:, 0, b, 0:1], v.isA[:, b:b + 1],
                                    ALU.subtract, ALU.mult).then_inc(s["x2_s"], 1)
                hsteps.end()
            if tail:
                r, sem_r = rsteps, rsteps.sem
                lg = mb[0][:, 0:NB * E].rearrange("p (b n) -> p b n", b=NB)
                wait(e, s["logit_done"], gt + 1)
                e.tensor_reduce(v.mx, lg, AX.X, ALU.max).then_inc(s["mx_s"], 1)
                wait(e, s["mx_s"], gt + 1)
                e.tensor_tensor(v.logit[:], lg, v.mx[:, :, None].to_broadcast((P, NB, E)), ALU.subtract)\
                    .then_inc(s["logit_read"], 1)
                wait(e, s["exp_s"], gt + 1)
                n = r.did(e.tensor_reduce(v.sm, v.logit[:], AX.X, ALU.add))
                wait(e, sem_r, n)
                n = r.did(e.reciprocal(v.sm, v.sm))
                wait(e, sem_r, n)
                pv = v.pp[:, :, 2:]
                n = r.did(e.tensor_tensor(pv, v.logit[:], v.sm[:, :, None].to_broadcast((P, NB, E)), ALU.mult))
                wait_apart(e, v, sem_r, n)
                for b in range(NB):
                    last = e.max(v.m8[:, b, :], v.pp[:, b, :])
                n = r.did(last)
                e.tensor_copy(v.rows[:, :, D::2], pv)
                wait_apart(e, v, sem_r, n)
                for b in range(NB):
                    last = e.match_replace(v.pr[:, b, :], v.m8[:, b, :], v.pp[:, b, :], -1.0)
                n = r.did(last)
                wait(e, sem_r, n)
                n = r.did(e.tensor_scalar(v.mask[:], v.pr[:, :, 2:], 0.0, None, ALU.is_lt))
                wait(e, sem_r, n)
                r.did(e.tensor_tensor(v.votes[:, bass.ds(gt * NB, NB), :], v.mask[:],
                                      v.tnum[:, :, None].to_broadcast((P, NB, E)), ALU.mult))
                n = r.did(e.tensor_tensor_scan(v.cum[:].rearrange("p b n -> p (b n)"), v.ones[:],
                                               v.mask[:].rearrange("p b n -> p (b n)"), 0.0, ALU.mult, ALU.add))
                wait(e, sem_r, n)
                n = r.did(e.tensor_tensor(v.cum[:], v.cum[:], v.mask[:], ALU.subtract))
                wait(e, sem_r, n)
                e.tensor_tensor(v.rows[:, :, D + 1::2], v.cum[:], v.zbase[:, :, None].to_broadcast((P, NB, E)), ALU.add)\
                    .then_inc(s["rows_s"], 1)
                r.did(e.tensor_scalar(v.tnum[:], v.tnum[:], float(-TG), None, ALU.add))
                wait(e, s["rows_s"], gt + 1)
                r.did(e.tensor_scalar(v.zbase[:], v.zbase[:], float(TOPK * TG), None, ALU.add))
                r.end()

        over_groups(e, step)
        epilogue(nc, e, v)


def epilogue(nc, e, v):
    s = v.s
    tb, mb, kb = v.tb, v.mb, v.kb
    NF = len(FSC)

    def shared_rows(g):
        for f, n in enumerate(FSC):
            wait(e, s["shg_s"], NF * g + f + 1)
            wait(e, s["shu_done"], (NF * g + f) * 2 + 2)
            e.tensor_tensor(v.shh[0:n, f, :], mb[(2 * f + 1) % 4][0:n, :], v.sgl[0:n, f, :], ALU.mult)\
                .then_inc(s["shh_s"], 1)

    def shared_sums(g):
        for k in range(2):
            wait(e, s["shd_done"], 2 * g + k + 1)
            o = v.shared[:, bass.ds(g * NB + 2 * k, 2), :]
            e.tensor_tensor(o, kb[k][:].rearrange("p (b n) -> p b n", b=2), o, ALU.add).then_inc(s["sh_s"], 1)

    picks = [0]

    def pick(ins):
        picks[0] += 1
        ins.then_inc(s["pick_s"], 1)
        return picks[0]

    for k in range(G):
        e.wait_ge(s["vote_tr"], k + 1)
        e.tensor_copy(v.votesT[:, k * TG:(k + 1) * TG], tb[k % 2][0:E, :]).then_inc(s["voteT_s"], 1)
    e.wait_ge(s["voteT_s"], G)
    e.wait_ge(s["x3_in"], 16)

    def rounds(a, b):
        for k in range(a, b):
            m = v.first[:, 8 * k:8 * k + 8]
            if k:
                e.wait_ge(s["pick_s"], 2 * k)
            e.wait_ge(s["pick_s"], pick(e.max(m, v.votesT[:])))
            pick(e.match_replace(v.votesT[:], m, v.votesT[:], 0.0))

    for g in range(G):
        shared_rows(g)
        rounds(2 * g, 2 * g + 2)
        shared_sums(g)
    e.wait_ge(s["pick_s"], 16)
    for k in range(2):
        last = e.tensor_scalar(v.firstd[:, k, :], v.first[:], -1.0, 4096.0, ALU.mult, ALU.add)
    pick(last)
    e.wait_ge(s["pickT_s"], 1)
    for x in range(2):
        e.tensor_scalar(v.idx_all[x * CAP:(x + 1) * CAP, 0:EP], tb[0][x * CAP:(x + 1) * CAP, x:E:2], float(T), None, ALU.min)\
            .then_inc(s["idx_s"], 1)
    e.wait_ge(s["idx_s"], 2)
    e.tensor_copy(v.idx_slot[:], v.idx_all[:, 0:RING]).then_inc(s["idxc_s"], 1)

    def places(o, r):
        p = o * RING + r
        wait(e, s[f"gat{r}"], 16 * o + 16)
        if not (isinstance(o, int) and o == 0):
            wait(e, s[f"scat{r}"], 16 * o)
        for x in range(2):
            last = e.tensor_copy(v.pz_slot[x * CAP:(x + 1) * CAP, r, :],
                                 v.xg[x * CAP:(x + 1) * CAP, r, bass.ds(p * 4 + (D + 2 * x), 2)])
        last.then_inc(s["pz_s"], 1)
        wait(e, s["pz_s"], p + 1)
        e.tensor_copy(v.z_slot[:, r:r + 1], v.pz_slot[:, r, 1:2]).then_inc(s["zi_s"], 1)
        e.tensor_copy(v.idx_slot[:, r:r + 1], v.idx_all[:, bass.ds(p + RING, 1)]).then_inc(s["idxc_s"], 1)

    def hidden(o, r):
        p = o * RING + r
        wait(e, s["sg_s"], p + 1)
        if not (isinstance(p, int) and p < 2):
            wait(e, s["dn_done"], p - 1)
        e.tensor_tensor(v.he[0:FH, r % 2].rearrange("p e f n -> p (e f n)"), mb[r % 2][0:FH, 256:512],
                        v.sge[0:FH, r % 2, :], ALU.mult).then_inc(s["he_s"], 1)

    def weighted(p, r):
        wait(e, s["dn_done"], p + 1)
        e.tensor_scalar(v.dout[:, r, :], kb[r % 2][:, 0:D], v.pz_slot[:, r, 0:1], None, ALU.mult).then_inc(s["dout_s"], 1)

    def turn(o):
        for r in range(RING):
            p = o * RING + r
            places(o, r)
            if not (isinstance(p, int) and p < 2):
                weighted(p - 2, (r - 2) % RING)
            hidden(o, r)

    turn(0)
    with e.Fori(1, EP // RING) as o:
        turn(o)
    for r in (2, 3):
        weighted(EP - RING + r, r)

    def final(i):
        for k in range(2):
            n = i * 2 + k
            y = v.u[:, k, :]
            wait(e, s[f"z{k}"], 16 * i + 16)
            e.tensor_reduce(y, v.zin[:, k, :].rearrange("p (k d) -> p d k", k=TOPK), AX.X, ALU.add)\
                .then_inc(s["fdve"], 1)
            wait(e, s["fdve"], n * FDVE + 1)
            e.tensor_tensor(y, y, v.shared[:, bass.ds(n, 1), :].rearrange("p o n -> p (o n)"), ALU.add)\
                .then_inc(s["fdve"], 1)
            wait(e, s["fdve"], n * FDVE + 2)
            e.bn_stats(v.bn[:, 2, k, :], y).then_inc(s["fdve"], 1)
            wait_apart(e, v, s["fdve"], n * FDVE + 3)
            e.bn_aggr(v.mv[:, 2, k, :], v.bn[:, 2, k, :]).then_inc(s["fdve"], 1)
            wait(e, s["fsd"], n + 1)
            e.reciprocal(v.isF[:, k:k + 1], v.sdF[:, k:k + 1]).then_inc(s["isF_s"], 1)
            wait(e, s["isF_s"], n + 1)
            if not isinstance(i, int):
                wait(e, s[f"out{k}"], 16 * i)
            e.tensor_scalar(v.x2[:, k, :], y, v.mv[:, 2, k, 0:1], v.isF[:, k:k + 1], ALU.subtract, ALU.mult)\
                .then_inc(s["f_s"], 1)

    final(0)
    with e.Fori(1, B // 2) as i:
        final(i)


def _by_chunk(np_, a):
    return np_.ascontiguousarray(a.reshape(-1, P, a.shape[-1]).transpose(1, 0, 2))


def kernel(**inputs):
    import numpy as _np
    import concourse.bacc as _bacc
    from concourse import mybir as _mybir
    from concourse.bass_utils import run_bass_kernel_spmd as _run

    a = {k: _np.asarray(w) for k, w in inputs.items()}
    at = lambda n: a["L0_attn_" + n]
    ff = lambda n: a["L0_ffn_" + n]
    column = lambda w: w.reshape(-1, P).T
    cols = _np.concatenate([column(at("norm1_w")), column(at("norm2_w")), column(at("left_b")), column(at("right_b")),
                            column(at("conv_b"))] + [column(at("conv_w")[k]) for k in range(4)] +
                           [column(at(n)) for n in ("ga_b", "gx_b", "a_param", "up1_b", "up2_b")], axis=1)
    both = lambda m, n: _by_chunk(_np, _np.concatenate([at(m), at(n)], axis=1))
    ssm = a["L0_xattn_ssm_kernel"]
    kpad = _np.concatenate([_np.zeros((HEADS, P - 1), ssm.dtype), ssm], axis=1)
    shd = ff("sh_down").T
    shd = _np.concatenate([shd, _np.zeros((len(FSC) * P - FS, D), shd.dtype)], axis=0)
    gu = _np.stack([ff("w_gate"), ff("w_up")], axis=2)
    arrays = {
        "x": a["x"], "ctx": a["ctx_2048"], "cols": cols,
        "out_b": at("out_b")[None], "down_b": at("down_b")[None], "d": a["L0_xattn_D"][None], "kpad": kpad,
        "w_left_right": both("left_W", "right_W"), "w_gates": both("ga_W", "gx_W"), "w_out": _by_chunk(_np, at("out_W")),
        "w_up": both("up1_W", "up2_W"), "w_down": _by_chunk(_np, at("down_W")),
        "w_router": _by_chunk(_np, ff("gate_w").T),
        "w_shared": _by_chunk(_np, _np.concatenate([ff("sh_gate").T, ff("sh_up").T], axis=1)),
        "w_shared_down": _by_chunk(_np, shd),
        "w_experts": gu.reshape(EP, 2, C, P, 2 * FE).transpose(0, 3, 1, 2, 4),
        "w_experts_down": ff("w_down").reshape(EP, 2, 2, FH, D).transpose(0, 3, 1, 2, 4),
    }
    nc = _bacc.Bacc("TRN2", target_bir_lowering=False, num_devices=1)
    feeds, args = {}, []
    for name, w in arrays.items():
        w = _np.ascontiguousarray(w)
        feeds[f"in_{name}_dram"] = w
        args.append(nc.dram_tensor(f"in_{name}_dram", w.shape, _mybir.dt.from_np(w.dtype), kind="ExternalInput").ap())
    args.append(nc.dram_tensor("out_0_dram", (B, S, D), F32, kind="ExternalOutput").ap())
    build(nc, *args)
    r = _run(nc, [feeds], core_ids=[0])
    return r.results[0]["out_0_dram"]
```

```python
from contextlib import ExitStack

import concourse.bass as bass
from concourse import mybir

F32 = mybir.dt.float32
I32 = mybir.dt.int32
ALU = mybir.AluOpType
ACT = mybir.ActivationFunctionType
AX = mybir.AxisListType

P = 128
B, S, D = 16, 128, 256
T = B * S
C = D // P
G = 4
NB = B // G
TG = NB * S
F = 768
FJ = F // P
HD = 8
HEADS = S // HD
HEADS_DVE = 11
PAIRS = HD * (HD + 1) // 2
PW = PAIRS * NB
E, FE, CAP, TOPK = 64, 176, 64, 6
FH = FE // 2
FS = 352
FSC = [128, 128, 96]
EP = E // 2
RING = 4
ROW = D + 2 * E
NZ = T * (TOPK + 1)
ZR = TOPK + 1
KW = P - 1 + D
FR = 4
EPS_RMS, EPS_LN, LRU_C = 1e-8, 1e-5, 8.0

COLS = {}
for _name, _n in (("norm1", C), ("norm2", C), ("left_b", C), ("right_b", C), ("conv_b", C), ("conv_w", 4 * C),
                  ("ga_b", C), ("gx_b", C), ("a_param", C), ("up1_b", FJ), ("up2_b", FJ)):
    COLS[_name] = sum(n for _, n in COLS.values()), _n
NCOLS = sum(n for _, n in COLS.values())

DOFF = [sum(HD - k for k in range(d)) for d in range(HD)]


class Steps:

    def __init__(self, sem, per):
        self.sem, self.per = sem, per

    def begin(self, g):
        self.base, self.n = self.per * g, 0

    def did(self, ins):
        ins.then_inc(self.sem, 1)
        self.n += 1
        return self.base + self.n

    def end(self):
        assert self.n == self.per, (self.n, self.per)


class Shared:
    pass


def build(nc, x, ctx_in, cols_in, outb_in, downb_in, d_in, kpad_in, wlr_in, wg_in, wo_in, wup_in, wdn_in,
          wgate_in, wsh_in, wshd_in, wgu_in, wd_in, out):
    v = Shared()
    v.x, v.ctx_in, v.cols_in, v.outb_in, v.downb_in, v.d_in, v.kpad_in, v.wlr_in, v.wg_in = \
        x, ctx_in, cols_in, outb_in, downb_in, d_in, kpad_in, wlr_in, wg_in
    v.wo_in, v.wup_in, v.wdn_in, v.wgate_in, v.wsh_in, v.wshd_in, v.wgu_in, v.wd_in, v.out = \
        wo_in, wup_in, wdn_in, wgate_in, wsh_in, wshd_in, wgu_in, wd_in, out
    v.rows_dram = nc.dram_tensor("rows_dram", (T + 1, ROW), F32, kind="Internal").ap()
    v.krep_dram = nc.dram_tensor("krep_dram", (HEADS, P * KW), F32, kind="Internal").ap()
    v.z_dram = nc.dram_tensor("z_dram", (NZ, D), F32, kind="Internal").ap()

    with ExitStack() as stack:
        def sb(name, shape, dt=F32):
            return stack.enter_context(nc.sbuf_tensor(name, shape, dt))

        def sem(name):
            return stack.enter_context(nc.semaphore(name))

        v.cols = sb("cols", [P, NCOLS])
        v.outb, v.downb = sb("outb", [P, D]), sb("downb", [P, D])
        v.d_sb = sb("d_sb", [P, HEADS])
        v.ident = sb("ident", [P, P])
        v.ones = sb("ones", [P, NB * E])
        v.zeros = sb("zeros", [P, 512])
        v.table = sb("table", [P, 1])
        v.eps_rms, v.eps_ln, v.one = sb("eps_rms", [P, 1]), sb("eps_ln", [P, 1]), sb("one", [P, 1])
        v.lru = sb("lru", [P, 3, C])
        v.tnum = sb("tnum", [P, NB])
        v.zbase = sb("zbase", [P, NB])
        v.empty_row = sb("empty_row", [1, ROW])
        v.wsh = sb("wsh", [P, C, 2 * FS])
        v.wshd = sb("wshd", [P, len(FSC), D])
        v.wgate = sb("wgate", [P, C, E])
        v.x3T = sb("x3T", [P, C, TG])
        v.votes = sb("votes", [P, NB, E])
        v.cand = sb("cand", [E, CAP + TG])
        v.sgl = sb("sgl", [P, 2, TG])
        v.shh = sb("shh", [P, len(FSC), TG])
        v.first = sb("first", [E, CAP])
        v.firstd = sb("firstd", [E, 2, CAP])
        v.idx_all = sb("idx_all", [P, EP + RING], I32)
        v.idx_slot = sb("idx_slot", [P, RING], I32)
        v.z_slot = sb("z_slot", [P, RING], I32)
        v.pz_slot = sb("pz_slot", [P, RING, 2])

        wregion = sb("wregion", [P, 11264])
        at = [0]

        def take(n, region=None):
            v = (region or wregion)[:, at[0]:at[0] + n]
            at[0] += n
            return v

        v.wlr = take(C * 2 * D).rearrange("p (c n) -> p c n", c=C)
        v.wg = take(C * 2 * D).rearrange("p (c n) -> p c n", c=C)
        v.wo = take(C * D).rearrange("p (c n) -> p c n", c=C)
        v.wup = take(C * 2 * F).rearrange("p (c n) -> p c n", c=C)
        v.wdn = take(FJ * D).rearrange("p (c n) -> p c n", c=FJ)
        v.toep = take(HEADS * 2 * P).rearrange("p (h n) -> p h n", h=HEADS)
        at[0] = 0
        v.wgu = [take(2 * C * 2 * FE).rearrange("p (e c n) -> p e c n", e=2, c=C) for _ in range(RING)]
        v.wd = [take(2 * 2 * D).rearrange("p (e f n) -> p e f n", e=2, f=2) for _ in range(RING)]
        at[0] = 0
        v.zin = take(FR * ZR * D).rearrange("p (k n) -> p k n", k=FR)

        hregion = sb("hregion", [P, 13400])
        at[0] = 0
        v.xin = take(NB * D, hregion).rearrange("p (b n) -> p b n", b=NB)
        v.xn = take(NB * D, hregion).rearrange("p (b n) -> p b n", b=NB)
        v.xT = take(C * TG, hregion).rearrange("p (c n) -> p c n", c=C)
        v.left = take(C * TG, hregion).rearrange("p (c n) -> p c n", c=C)
        rt = take(C * NB * (S + 3), hregion)
        v.rtv = rt.rearrange("p (c b n) -> p c b n", c=C, b=NB)
        v.hs = take(C * TG, hregion).rearrange("p (c n) -> p c n", c=C)
        v.cv = take(C * TG, hregion).rearrange("p (c n) -> p c n", c=C)
        v.mlp = take(FJ * TG, hregion).rearrange("p (c n) -> p c n", c=FJ)
        v.ri = v.mlp[:, 0:4, :]
        v.th = v.mlp[:, 4:6, :]
        v.xo = take(NB * D, hregion).rearrange("p (b n) -> p b n", b=NB)
        v.xs = take(NB * D, hregion).rearrange("p (b n) -> p b n", b=NB)
        v.gl = take(2 * TG, hregion).rearrange("p (k n) -> p k n", k=2)
        at[0] = 0
        v.xg = take(RING * ROW, hregion).rearrange("p (r n) -> p r n", r=RING)
        v.xgT = take(2 * C * P, hregion).rearrange("p (k c n) -> p k c n", k=2, c=C)
        v.sge = take(2 * 4 * CAP, hregion).rearrange("p (k n) -> p k n", k=2)
        v.he = take(2 * 4 * CAP, hregion).rearrange("p (k e f n) -> p k e f n", k=2, e=2, f=2)
        v.dout = take(RING * D, hregion).rearrange("p (r n) -> p r n", r=RING)

        v.cin = sb("cin", [P, NB, D])
        v.ctxT = sb("ctxT", [P, C, S * NB])
        v.kv = sb("kv", [P, 2, C, 4, PW])
        v.ycv = sb("ycv", [P, C, HEADS, PW])
        v.x2 = sb("x2", [P, NB, D])
        v.q = sb("q", [P, C, HEADS, HD * NB])
        v.acc = sb("acc", [P, C, HEADS, HD * NB])
        v.tmp = sb("tmp", [P, 2, C, HEADS, (HD - 1) * NB])
        v.u = sb("u", [P, NB, D])
        v.rows = sb("rows", [P, NB, ROW])
        v.logit = sb("logit", [P, NB, E])
        v.pp = sb("pp", [P, NB, E + 2])
        v.pr = sb("pr", [P, NB, E + 2])
        v.mask = sb("mask", [P, NB, E])
        v.cum = sb("cum", [P, NB, E])
        v.m8 = sb("m8", [P, NB, 8])
        st = sb("st", [P, 12, NB])
        v.bn = sb("bn", [P, 3, NB, 6])
        v.mv = sb("mv", [P, 3, NB, 2])
        v.sdF, v.isF = sb("sdF", [P, FR]), sb("isF", [P, FR])
        v.ss1, v.rms1, v.inv1 = st[:, 0], st[:, 1], st[:, 2]
        v.ss2, v.rms2, v.inv2 = st[:, 3], st[:, 4], st[:, 5]
        v.sdA, v.isA, v.sdB, v.isB, v.mx, v.sm = (st[:, k] for k in range(6, 12))

        v.tb = [stack.enter_context(nc.psum_tensor(f"tb{k}", [P, 512], F32)) for k in range(2)]
        v.mb = [stack.enter_context(nc.psum_tensor(f"mb{k}", [P, 512], F32)) for k in range(4)]
        v.kb = [stack.enter_context(nc.psum_tensor(f"kb{k}", [P, 512], F32)) for k in range(2)]

        names = """consts_in weights_in x_in ctx_in_s idn tables lru_s d_done tnum_s shw_in zero_out 
            ctx_tr ctxT_ready kv_ready conv_done conv_evac
            ss1_s rms1_s inv1_s xn_s x_tr xT_s lr_done left_s right_s cvs gates_done gate_s act_a th_s dve_h
            mult_s lr_s out_done xo_s xs_s x1_s ss2_s rms2_s x1n_s x1_tr x1T_s up_done gelu_s h_s down_done y_s
            lnA_s sdA_s x2_s x2_tr q_s qstep qpool o_tr u_s lnB_s sdB_s x3_s x3_tr x3T_s logit_done logit_read exp_s
            dve_r rows_s rows_out vote_tr voteT_s pick_s pickT_s idx_s shu_done shg_s shh_s shd_done sh_s sums_out
            wring0 wring1 wring2 wring3 gat0 gat1 gat2 gat3 scat0 scat1 scat2 scat3
            idxc_s pz_s zi_s g_tr gT_s gu_done sg_s he_s dn_done dout_s z0 z1 z2 z3 fdve fsd f_s out0 out1 out2 out3 isB_s isF_s mx_s consts_s krep_out""".split()
        v.s = {n: sem(n) for n in names}

        with nc.Block() as block:
            sync_program(nc, block, v)
            pool_program(nc, block, v)
            act_program(nc, block, v)
            pe_program(nc, block, v)
            dve_program(nc, block, v)


def col(v, name, k, p=P):
    o, n = COLS[name]
    assert k < n
    return v.cols[0:p, o + k:o + k + 1]


def wait(e, sem, value):
    if not (isinstance(value, int) and value <= 0):
        e.wait_ge(sem, value)


def wait_apart(e, v, sem, value):
    if not isinstance(value, int):
        value = e.to_reg(value)
        e.wait_ge(v.s["consts_s"], 1)
    e.wait_ge(sem, value)


def over_groups(e, step):
    step(0, None, None)
    step(1, 0, None)
    with e.Fori(2, G) as g:
        step(g, g - 1, g - 2)
    step(None, G - 1, G - 2)


def sync_program(nc, block, v):
    s = v.s

    @block.sync
    def _(e):
        def load_x(g):
            if not (isinstance(g, int) and g == 0):
                wait_apart(e, v, s["xn_s"], 4 * g)
                wait(e, s["xo_s"], g)
                wait(e, s["xs_s"], 2 * g)
            e.dma_start(v.xin, v.x[bass.ds(g * NB, NB), :, :].rearrange("b s d -> s b d")).then_inc(s["x_in"], 16)

        def load_ctx(g):
            if not (isinstance(g, int) and g == 0):
                wait(e, s["ctx_tr"], 2 * g)
            e.dma_start(v.cin[:], v.ctx_in[bass.ds(g * NB, NB), :, :].rearrange("b s d -> s b d"))\
                .then_inc(s["ctx_in_s"], 16)

        load_x(0)
        for dst, src in ((v.cols[:], v.cols_in), (v.outb[:], v.outb_in.to_broadcast((P, D))),
                         (v.downb[:], v.downb_in.to_broadcast((P, D))), (v.d_sb[:], v.d_in.to_broadcast((P, HEADS)))):
            e.dma_start(dst, src).then_inc(s["consts_in"], 16)
        for dst, src in ((v.wlr, v.wlr_in), (v.wg, v.wg_in), (v.wo, v.wo_in), (v.wup, v.wup_in), (v.wdn, v.wdn_in)):
            e.dma_start(dst, src).then_inc(s["weights_in"], 16)
        e.dma_start(v.krep_dram.rearrange("h (m n) -> h m n", n=KW), v.kpad_in[:, None, :].to_broadcast((HEADS, P, KW)))\
            .then_inc(s["krep_out"], 16)
        load_ctx(0)
        for dst, src in ((v.wgate[:], v.wgate_in), (v.wsh[:], v.wsh_in), (v.wshd[:], v.wshd_in)):
            e.dma_start(dst, src).then_inc(s["shw_in"], 16)
        e.wait_ge(s["krep_out"], 16)
        k = v.krep_dram[0:HEADS, P - 1:P + 1]
        e.dma_start(v.toep, bass.AP(k.tensor, k.offset, [[KW - 1, P], [P * KW, HEADS], [1, 2 * P]])).then_inc(s["tables"], 16)
        e.wait_ge(s["idn"], 1)
        zv = v.z_dram.rearrange("(k p m) d -> k p (m d)", k=8, p=P)
        for k in range(8):
            e.dma_start(zv[k].rearrange("p (r n) -> p r n", n=512), v.zeros[:, None, :].to_broadcast((P, NZ * D // 8 // P // 512, 512)))\
                .then_inc(s["zero_out"], 16)
        with e.Fori(1, G) as g:
            load_x(g)
            load_ctx(g)

        def load_pair(p, r):
            e.dma_start(v.wgu[r], v.wgu_in[bass.ds(p, 1)].rearrange("o p e c n -> (o p) e c n"))\
                .then_inc(s[f"wring{r}"], 16)
            e.dma_start(v.wd[r][0:FH], v.wd_in[bass.ds(p, 1)].rearrange("o p e f n -> (o p) e f n"))\
                .then_inc(s[f"wring{r}"], 16)

        e.wait_ge(s["down_done"], 2 * G)
        e.wait_ge(s["conv_done"], HEADS * G)
        for r in range(RING):
            load_pair(r, r)
        with e.Fori(1, EP // RING) as o:
            for r in range(RING):
                wait(e, s["dn_done"], (o - 1) * RING + r + 1)
                load_pair(o * RING + r, r)

        for r in range(RING):
            e.wait_ge(s[f"scat{r}"], 16 * (EP // RING))
        e.wait_ge(s["sums_out"], 16 * G)

        def load_sums(b, k):
            e.dma_start(v.zin[:, k, :], v.z_dram[bass.ds(b * S * ZR, S * ZR), :].rearrange("(s k) d -> s (k d)", k=ZR))\
                .then_inc(s[f"z{k}"], 16)

        def store(b, k, n):
            wait(e, s["f_s"], n)
            e.dma_start(v.out[bass.ds(b, 1), :, :].rearrange("b s d -> (b s) d"), v.x2[:, k, :]).then_inc(s[f"out{k}"], 16)

        for k in range(FR):
            load_sums(k, k)
        with e.Fori(1, B // FR) as i:
            for k in range(FR):
                wait(e, s["fdve"], ((i - 1) * FR + k) * FDVE + 1)
                load_sums(FR * i + k, k)
                store(FR * (i - 1) + k, k, FR * (i - 1) + k + 1)
        for k in range(FR):
            store(B - FR + k, k, B - FR + k + 1)
        for k in range(FR):
            e.wait_ge(s[f"out{k}"], 16 * (B // FR))


FDVE = 3
HDVE = 9
RDVE = 12
QSTEPS = 1 + 4 * (HD - 1)
PDVE = 17


def pool_program(nc, block, v):
    s = v.s
    psteps = Steps(s["qpool"], QSTEPS)

    @block.gpsimd
    def _(e):
        e.memset(v.zeros[:], 0.0).then_inc(s["idn"], 1)
        e.memset(v.ident[:], 0.0).then_inc(s["idn"], 1)
        e.wait_ge(s["idn"], 2)
        e.affine_select(out=v.ident[:], in_=v.ident[:], compare_op=ALU.not_equal, fill=1.0, base=0,
                        pattern=[[-1, P]], channel_multiplier=1).then_inc(s["idn"], 1)
        e.iota(v.tnum[:], pattern=[[-S, NB]], base=4096, channel_multiplier=-1, allow_small_or_imprecise_dtypes=True)
        e.iota(v.zbase[:], pattern=[[ZR * S - TOPK, NB]], base=0, channel_multiplier=ZR,
               allow_small_or_imprecise_dtypes=True).then_inc(s["tnum_s"], 1)
        e.wait_ge(s["logit_read"], 1)
        e.dma_start(v.rows_dram[T:T + 1, :], v.empty_row[:]).then_inc(s["rows_out"], 16)
        e.wait_ge(s["tables"], 16)
        e.wait_ge(s["consts_in"], 16 * 4)
        e.wait_ge(s["idn"], 3)
        dtmp = v.ycv[:, 0, :, 0:P]
        e.tensor_tensor(dtmp, v.ident[:, None, :].to_broadcast((P, HEADS, P)),
                        v.d_sb[:, :, None].to_broadcast((P, HEADS, P)), ALU.mult).then_inc(s["d_done"], 1)
        e.wait_ge(s["d_done"], 1)
        e.tensor_tensor(v.toep[:, :, 0:P], v.toep[:, :, 0:P], dtmp, ALU.add).then_inc(s["d_done"], 1)

        def products(gt, hb):
            wait(e, s["ctxT_ready"], 2 * gt + 2)
            wait(e, s["conv_done"], HEADS * gt + 4 * (hb - 1))
            cx = v.ctxT[:].rearrange("p c (h n) -> p c h n", h=HEADS)[:, :, 4 * hb:4 * hb + 4, :]
            for d in range(HD):
                n = (HD - d) * NB
                last = e.tensor_tensor(v.kv[:, hb % 2, :, :, DOFF[d] * NB:DOFF[d] * NB + n],
                                       cx[:, :, :, 0:n], cx[:, :, :, d * NB:d * NB + n], ALU.mult)
            last.then_inc(s["kv_ready"], 1)

        def step(gh, gt, gs):
            if gh is not None:
                wait(e, s["x_in"], 16 * gh + 16)
                if not (isinstance(gh, int) and gh == 0):
                    wait(e, s["x2_s"], 4 * gh)
                    wait(e, s["x1n_s"], 4 * gh)
                e.tensor_tensor(v.xo, v.xin, v.outb[:, None, :].to_broadcast((P, NB, D)), ALU.add)\
                    .then_inc(s["xo_s"], 1)
                if gt is not None:
                    products(gt, 2)
                e.tensor_tensor(v.xs, v.xin, v.downb[:, None, :].to_broadcast((P, NB, D)), ALU.add)\
                    .then_inc(s["xs_s"], 1)
            elif gt is not None:
                products(gt, 2)
            if gt is not None:
                products(gt, 3)
            if gh is not None:
                products(gh, 0)
                products(gh, 1)
                wait(e, s["x1_s"], 2 * gh + 2)
                wait(e, s["xs_s"], 2 * gh + 1)
                e.tensor_tensor(v.xs, v.xs, v.xo, ALU.add).then_inc(s["xs_s"], 1)
            if gt is not None:
                psteps.begin(gt)
                wait(e, s["conv_evac"], HEADS * gt + HEADS)
                wait(e, s["q_s"], 2 * gt + 2)
                for f in query_products(e, v, psteps, slice(HEADS_DVE, HEADS)):
                    f()
                psteps.end()
            if gs is not None:
                store_sums(gs)
            if gt is not None:
                wait(e, s["rows_s"], gt + 1)
                e.dma_start(v.rows_dram[bass.ds(gt * TG, TG), :].rearrange("(b s) n -> s b n", s=S), v.rows[:])\
                    .then_inc(s["rows_out"], 16)

        def store_sums(g):
            e.wait_ge(s["zero_out"], 16 * 8)
            wait(e, s["sh_s"], 2 * g + 2)
            e.dma_start(v.z_dram.rearrange("(b s k) d -> s b k d", s=S, k=ZR)[:, bass.ds(g * NB, NB), TOPK, :], v.u[:])\
                .then_inc(s["sums_out"], 16)

        over_groups(e, step)

        def gather(r):
            e.indirect_dma_start(out=v.xg[:, r, :], out_offset=None, in_=v.rows_dram[:, :],
                                 in_offset=bass.IndirectOffsetOnAxis(ap=v.idx_slot[:, r:r + 1], axis=0))\
                .then_inc(s[f"gat{r}"], 16)

        def scatter(r):
            e.indirect_dma_start(out=v.z_dram[:, :], out_offset=bass.IndirectOffsetOnAxis(ap=v.z_slot[:, r:r + 1], axis=0),
                                 in_=v.dout[:, r, :], in_offset=None, bounds_check=NZ - 1, oob_is_err=False)\
                .then_inc(s[f"scat{r}"], 16)

        e.wait_ge(s["rows_out"], 16 * (G + 1))
        e.wait_ge(s["idxc_s"], 1)
        for r in range(RING):
            gather(r)
        store_sums(G - 1)
        with e.Fori(0, EP // RING - 1) as o:
            for r in range(RING):
                wait_apart(e, v, s["dout_s"], o * RING + r + 1)
                scatter(r)
                wait_apart(e, v, s["idxc_s"], o * RING + r + 2)
                wait(e, s["g_tr"], o * RING + r + 1)
                gather(r)
        for r in range(RING):
            e.wait_ge(s["dout_s"], EP - RING + r + 1)
            scatter(r)


def act_program(nc, block, v):
    s = v.s
    mb, kb = v.mb, v.kb

    @block.scalar
    def _(e):
        o, n = COLS["a_param"]
        ap = v.cols[:, o:o + n]
        e.wait_ge(s["consts_in"], 16 * 4)
        e.activation(v.lru[:, 0], ap, ACT.Abs).then_inc(s["lru_s"], 1)
        e.wait_ge(s["lru_s"], 1)
        e.activation(v.lru[:, 0], v.lru[:, 0], ACT.Exp, scale=-1.0).then_inc(s["lru_s"], 1)
        e.wait_ge(s["lru_s"], 2)
        e.wait_ge(s["consts_s"], 1)
        e.activation(v.lru[:, 0], v.lru[:, 0], ACT.Ln, bias=v.one[:]).then_inc(s["lru_s"], 1)
        e.activation(v.lru[:, 2], ap, ACT.Relu).then_inc(s["lru_s"], 1)

        def silu_shared(g, f):
            n, bank = FSC[f], (mb[0], mb[2], kb[0])[f]
            wait(e, s["shu_done"], (g * len(FSC) + f) * 2 + 1)
            if f >= 2:
                wait(e, s["shh_s"], g * len(FSC) + f - 1)
            e.activation(v.sgl[0:n, f % 2, :], bank[0:n, :], ACT.Silu).then_inc(s["shg_s"], 1)

        def step(gh, gt, gs):
            head, tail = gh is not None, gt is not None

            def conv_out(h):
                wait(e, s["conv_done"], HEADS * gt + h + 1)
                e.activation(v.ycv[:, :, h, :], v.mb[h % 4][:, 0:C * PW].rearrange("p (c n) -> p c n", c=C), ACT.Copy)\
                    .then_inc(s["conv_evac"], 1)

            def mean_square(src, dst, name):
                for b in range(NB):
                    last = e.activation(v.xn[:, b, :], src[:, b, :], ACT.Square, accum_out=dst[:, b:b + 1])
                last.then_inc(s[name], 1)

            if head:
                wait(e, s["x_in"], 16 * gh + 16)
                if not (isinstance(gh, int) and gh == 0):
                    wait(e, s["x1_tr"], 2 * gh)
                mean_square(v.xin, v.ss1, "ss1_s")
                wait(e, s["ss1_s"], gh + 1)
                e.activation(v.rms1, v.ss1, ACT.Sqrt, scale=1.0 / D, bias=v.eps_rms[:]).then_inc(s["rms1_s"], 1)
            if tail:
                for h in range(8):
                    conv_out(h)
            if head:
                for c in range(C):
                    wait(e, s["lr_done"], 4 * gh + c + 1)
                    e.activation(v.rtv[:, c, :, 3:], mb[c][:].rearrange("p (b n) -> p b n", b=NB), ACT.Identity,
                                 bias=col(v, "right_b", c)).then_inc(s["right_s"], 1)
                for c in range(C):
                    wait(e, s["lr_done"], 4 * gh + C + c + 1)
                    e.activation(v.left[:, c, :], mb[C + c][:], ACT.Gelu, bias=col(v, "left_b", c)).then_inc(s["left_s"], 1)
            if tail:
                for h in range(8, 12):
                    conv_out(h)
            if head:
                for k in range(2 * C):
                    wait(e, s["gates_done"], 4 * gh + k + 1)
                    e.activation(v.ri[:, k, :], v.mb[k][:], ACT.Sigmoid, bias=col(v, ("ga_b", "gx_b")[k // C], k % C))\
                        .then_inc(s["gate_s"], 1)
                wait(e, s["gate_s"], 4 * gh + 2)
                wait(e, s["lru_s"], 6)
                for c in range(C):
                    e.activation(v.th[:, c, :], v.ri[:, c, :], ACT.Tanh, scale=v.lru[:, 0, c:c + 1]).then_inc(s["th_s"], 1)
                for c in range(C):
                    e.activation(v.ri[:, c, :], v.ri[:, c, :], ACT.Exp, scale=v.lru[:, 1, c:c + 1]).then_inc(s["act_a"], 1)
            if tail:
                for h in range(12, 16):
                    conv_out(h)
            if head:
                wait(e, s["dve_h"], HDVE * gh + 3)
                e.activation(v.th, v.th, ACT.Sqrt).then_inc(s["mult_s"], 1)
                for k in range(2):
                    wait(e, s["ctx_tr"], 2 * gh + k + 1)
                    if tail:
                        wait(e, s["kv_ready"], 4 * gt + 4)
                    e.activation(v.ctxT[:].rearrange("p c (s b) -> p b c s", b=NB)[:, 2 * k:2 * k + 2],
                                 v.tb[k][:].rearrange("p (b c s) -> p b c s", b=2, c=C), ACT.Copy)\
                        .then_inc(s["ctxT_ready"], 1)
            if gs is not None:
                silu_shared(gs, 0)
                silu_shared(gs, 1)
            if head:
                e.activation(v.table[:], v.one[:], ACT.Sqrt)
                wait(e, s["x1_s"], 2 * gh + 2)
                wait(e, s["x_tr"], 2 * gh + 2)
                mean_square(v.xo, v.ss2, "ss2_s")
                wait(e, s["ss2_s"], gh + 1)
                e.activation(v.rms2, v.ss2, ACT.Sqrt, scale=1.0 / D, bias=v.eps_rms[:]).then_inc(s["rms2_s"], 1)
            if gs is not None and not head:
                silu_shared(gs, 2)
            if head:
                for j in range(FJ):
                    if j == 2 and gs is not None:
                        silu_shared(gs, 2)
                    wait(e, s["up_done"], 2 * FJ * gh + 2 * j + 1)
                    if j >= 2:
                        wait(e, s["h_s"], FJ * gh + j - 1)
                    e.activation(v.gl[:, j % 2, :], v.mb[2 * j % 4][:], ACT.Gelu, bias=col(v, "up1_b", j))\
                        .then_inc(s["gelu_s"], 1)
            if tail:
                wait(e, s["lnB_s"], gt + 1)
                e.activation(v.sdB, v.mv[:, 1, :, 1], ACT.Sqrt, bias=v.eps_ln[:]).then_inc(s["sdB_s"], 1)
                for k in range(2):
                    wait(e, s["x3_tr"], 2 * gt + k + 1)
                    if gs is not None:
                        wait(e, s["shu_done"], 2 * len(FSC) * (gs + 1))
                    e.activation(v.x3T[:, :, k * 2 * S:(k + 1) * 2 * S].rearrange("p c (b s) -> p b c s", b=2),
                                 v.tb[k][:].rearrange("p (b c s) -> p b c s", b=2, c=C), ACT.Copy)\
                        .then_inc(s["x3T_s"], 1)
            if tail:
                wait(e, s["logit_read"], gt + 2)
                e.activation(v.logit[:], v.logit[:], ACT.Exp).then_inc(s["exp_s"], 1)
            if head:
                wait(e, s["lnA_s"], gh + 1)
                e.activation(v.sdA, v.mv[:, 0, :, 1], ACT.Sqrt, bias=v.eps_ln[:]).then_inc(s["sdA_s"], 1)

        over_groups(e, step)

        for f in range(len(FSC)):
            silu_shared(G - 1, f)

        with e.Fori(0, EP // RING) as o:
            for r in range(RING):
                p = o * RING + r
                wait(e, s["g_tr"], p + 1)
                e.activation(v.xgT[:, r % 2], v.tb[r % 2][:, 0:C * P].rearrange("p (c n) -> p c n", c=C), ACT.Copy)\
                    .then_inc(s["gT_s"], 1)
                wait(e, s["gu_done"], p + 1)
                e.activation(v.sge[0:FH, r % 2, :], v.mb[r % 2][0:FH, 0:4 * CAP], ACT.Silu).then_inc(s["sg_s"], 1)

        with e.Fori(0, B // FR) as i:
            for k in range(FR):
                n = i * FR + k
                wait(e, s["fdve"], n * FDVE + 3)
                e.activation(v.sdF[:, k:k + 1], v.mv[:, 2, k, 1:2], ACT.Sqrt, bias=v.eps_ln[:]).then_inc(s["fsd"], 1)


def pe_program(nc, block, v):
    s = v.s
    tb, mb, kb = v.tb, v.mb, v.kb

    @block.tensor
    def _(e):
        def transposes(src, k, done):
            for b in range(2):
                for c in range(C):
                    last = e.transpose(tb[k][:, (b * C + c) * P:(b * C + c + 1) * P], src[:, 2 * k + b, c * P:(c + 1) * P],
                                       v.ident[:])
            last.then_inc(s[done], 1)

        def dense(bank, w, n0, rhs, done):
            for c in range(C):
                last = e.matmul(bank, w[:, c, n0:n0 + P], rhs[:, c, :], start=(c == 0), stop=(c == C - 1))
            last.then_inc(s[done], 1)

        e.wait_ge(s["idn"], 3)

        NF = len(FSC)

        def shared_up(g, f, free):
            n, banks = FSC[f], ((mb[0], mb[1]), (mb[2], mb[3]), (kb[0], kb[1]))[f]
            for k in range(2):
                wait(e, *free[k])
                for c in range(C):
                    last = e.matmul(banks[k][0:n, :], v.wsh[:, c, k * FS + f * P:k * FS + f * P + n],
                                    v.x3T[:, c, :], start=(c == 0), stop=(c == C - 1))
                last.then_inc(s["shu_done"], 1)

        def shared_down(g):
            wait(e, s["shh_s"], NF * g + NF)
            for k in range(2):
                for b in range(2):
                    for f, n in enumerate(FSC):
                        t0 = (2 * k + b) * S
                        last = e.matmul(kb[k][:, b * D:(b + 1) * D], v.shh[0:n, f, t0:t0 + S], v.wshd[0:n, f, :],
                                        start=(f == 0), stop=(f == NF - 1))
                last.then_inc(s["shd_done"], 1)

        def votes_by_expert(g):
            for b in range(NB):
                last = e.transpose(kb[0][0:E, b * S:(b + 1) * S], v.votes[:, b, :], v.ident[:])
            last.then_inc(s["vote_tr"], 1)

        def step(gh, gt, gs):
            head, tail = gh is not None, gt is not None

            def conv(h):
                if h % 4 == 0:
                    wait(e, s["kv_ready"], 4 * gt + h // 4 + 1)
                o = mb[h % 4]
                k = v.kv[:, h // 4 % 2, :, h % 4, :]
                e.matmul(o[:, 0:PW], v.toep[:, h, 0:P], k[:, 0, :], start=True, stop=True)
                e.matmul(o[:, PW:2 * PW], v.toep[:, h, P:2 * P], k[:, 0, :], start=True, stop=False)
                e.matmul(o[:, PW:2 * PW], v.toep[:, h, 0:P], k[:, 1, :], start=False, stop=True)\
                    .then_inc(s["conv_done"], 1)

            if tail:
                wait(e, s["logit_read"], gt + 1)
                e.wait_ge(s["d_done"], 2)
                for h in range(4):
                    conv(h)
                for h in range(4, 8):
                    wait(e, s["conv_evac"], HEADS * gt + h - 3)
                    conv(h)
            if head:
                wait(e, s["xn_s"], 4 * gh + 4)
                if gs is not None:
                    wait(e, s["x3T_s"], 2 * gt)
                for k in range(2):
                    transposes(v.xn, k, "x_tr")
            if gs is not None:
                wait_apart(e, v, s["y_s"], 2 * gt + 2)
                wait_apart(e, v, s["dve_r"], RDVE * gt)
                votes_by_expert(gs)
            if head:
                e.wait_ge(s["weights_in"], 16 * 5)
                wait(e, s["xT_s"], 4 * gh + 4)
                for k in range(4):
                    if tail:
                        wait(e, s["conv_evac"], HEADS * gt + 5 + k)
                    dense(mb[k][:], v.wlr, (k + 2) % 4 * P, v.xT, "lr_done")
            if tail:
                wait(e, s["x2_s"], 4 * gt + 4)
                if not head:
                    wait(e, s["x3T_s"], 2 * gt)
                for k in range(2):
                    transposes(v.x2, k, "x2_tr")
                for h in range(8, 12):
                    if head:
                        wait(e, s["right_s"] if h < 10 else s["left_s"], 2 * gh + h % 2 + 1)
                    else:
                        wait(e, s["conv_evac"], HEADS * gt + h - 3)
                    conv(h)
            if head:
                wait(e, s["cvs"], 8 * gh + 8)
                for k in range(4):
                    if tail:
                        wait(e, s["conv_evac"], HEADS * gt + 9 + k)
                    else:
                        wait(e, s["right_s"] if k < 2 else s["left_s"], 2 * gh + k % 2 + 1)
                    dense(mb[k][:], v.wg, k * P, v.cv, "gates_done")
            if tail:
                for h in range(12, 16):
                    if head:
                        wait(e, s["gate_s"], 4 * gh + h - 11)
                    else:
                        wait(e, s["conv_evac"], HEADS * gt + h - 3)
                    conv(h)
            if head:
                wait(e, s["ctx_in_s"], 16 * gh + 16)
                if tail:
                    wait(e, s["q_s"], 2 * gt + 2)
                for k in range(2):
                    transposes(v.cin, k, "ctx_tr")
            if gs is not None:
                for f in range(2):
                    shared_up(gs, f, [(s["conv_evac"], HEADS * gt + 13 + 2 * f + k) for k in range(2)])
            if head:
                wait(e, s["lr_s"], gh + 1)
                if gs is not None:
                    wait(e, s["voteT_s"], gs + 1)
                elif tail:
                    wait(e, s["y_s"], 2 * gh)
                for k in range(2):
                    for b in range(2):
                        for c in range(C):
                            t0 = (2 * k + b) * S
                            last = e.matmul(kb[k][:, b * D:(b + 1) * D], v.left[:, c, t0:t0 + S], v.wo[:, c, :],
                                            start=(c == 0), stop=(c == C - 1))
                    last.then_inc(s["out_done"], 1)
                if gs is not None:
                    wait(e, s["x1_s"], 2 * gh + 2)
                    shared_up(gs, 2, [(s["shg_s"], NF * gs + 2), (s["shh_s"], NF * gs + 2)])
                wait(e, s["ctxT_ready"], 2 * gh + 2)
                wait(e, s["x1n_s"], 4 * gh + 4)
                for k in range(2):
                    transposes(v.xn, k, "x1_tr")
                wait(e, s["x1T_s"], 4 * gh + 4)
                for j in range(FJ):
                    if j == 4 and gs is not None:
                        shared_down(gs)
                    for k in range(2):
                        i = 2 * j + k
                        if i < 4 and gs is not None:
                            wait(e, s["shg_s"] if k == 0 else s["shh_s"], NF * gs + j + 1)
                        elif i < 4 and tail:
                            wait(e, s["conv_evac"], HEADS * gt + 13 + i)
                        elif i < 4:
                            wait(e, s["gate_s"], 4 * gh + i + 1)
                        else:
                            wait(e, s["gelu_s"] if k == 0 else s["h_s"], FJ * gh + j - 1)
                        dense(mb[i % 4][:], v.wup, k * F + j * P, v.xT, "up_done")
            elif gs is not None:
                wait(e, s["voteT_s"], gs + 1)
                shared_up(gs, 2, [(s["shg_s"], NF * gs + 2), (s["shh_s"], NF * gs + 2)])
                shared_down(gs)
            if tail:
                wait(e, s["qstep"], QSTEPS * gt + QSTEPS)
                wait(e, s["qpool"], QSTEPS * gt + QSTEPS)
                if not head:
                    wait(e, s["q_s"], 2 * gt + 2)
                for k in range(2):
                    for b in range(2):
                        for c in range(C):
                            last = e.transpose(tb[k][:, (b * C + c) * P:(b * C + c + 1) * P],
                                               v.acc[:, c].rearrange("p h (i b) -> p (h i) b", b=NB)[:, :, 2 * k + b],
                                               v.ident[:])
                    last.then_inc(s["o_tr"], 1)
            def down(blocks, done):
                for k, b in blocks:
                    for j in range(FJ):
                        t0 = (2 * k + b) * S
                        last = e.matmul(kb[k][:, b * D:(b + 1) * D], v.mlp[:, j, t0:t0 + S], v.wdn[:, j, :],
                                        start=(j == 0), stop=(j == FJ - 1))
                if done:
                    last.then_inc(s["down_done"], 1)

            if head:
                wait(e, s["h_s"], FJ * gh + FJ)
                if gs is not None:
                    wait(e, s["sh_s"], 2 * gs + 2)
                down([(0, 0), (0, 1)], True)
            if tail:
                e.wait_ge(s["shw_in"], 16 * 3)
                wait(e, s["x3_s"], 4 * gt + 4)
                for k in range(2):
                    transposes(v.rows, k, "x3_tr")
            if head:
                down([(1, 0)], False)
            if tail:
                wait(e, s["x3T_s"], 2 * gt + 2)
                if not head:
                    wait(e, s["shh_s"], NF * gs + 1)
                for b in range(NB):
                    for c in range(C):
                        last = e.matmul(mb[0][:, b * E:(b + 1) * E], v.x3T[:, c, b * S:(b + 1) * S], v.wgate[:, c, :],
                                        start=(c == 0), stop=(c == C - 1))
                last.then_inc(s["logit_done"], 1)
            if head:
                down([(1, 1)], True)

        over_groups(e, step)

        e.wait_ge(s["logit_read"], G + 1)
        for f in range(2):
            shared_up(G - 1, f, [(s["x3T_s"], 2 * G)] * 2)
        e.wait_ge(s["sh_s"], 2 * (G - 1))
        e.wait_ge(s["dve_r"], RDVE * G)
        votes_by_expert(G - 1)
        shared_up(G - 1, 2, [(s["voteT_s"], G)] * 2)
        shared_down(G - 1)

        e.wait_ge(s["pick_s"], PDVE * (G - 1) + 17)
        e.transpose(tb[0][:, 0:E], v.firstd[:].rearrange("p k n -> p (k n)"), v.ident[0:E, 0:E]).then_inc(s["pickT_s"], 1)
        e.wait_ge(s["idx_s"], 2)
        e.wait_ge(s["sh_s"], 2 * G)
        e.wait_ge(s["shh_s"], NF * G)

        def place_rows(o, r):
            p = o * RING + r
            wait(e, s[f"gat{r}"], 16 * o + 16)
            if not (isinstance(p, int) and p < 2):
                wait(e, s["gT_s"], p - 1)
            for c in range(C):
                last = e.transpose(tb[r % 2][:, c * P:(c + 1) * P], v.xg[:, r, c * P:(c + 1) * P], v.ident[:])
            last.then_inc(s["g_tr"], 1)

        def gate_up(o, r):
            p = o * RING + r
            wait(e, s["gT_s"], p + 1)
            wait(e, s[f"wring{r}"], 32 * o + 32)
            if not (isinstance(p, int) and p < 2):
                wait(e, s["he_s"], p - 1)
            for k in range(2):
                for x in range(2):
                    for f in range(2):
                        o1 = mb[r % 2][0:FH, k * 256 + (2 * x + f) * CAP:k * 256 + (2 * x + f + 1) * CAP]
                        for c in range(C):
                            last = e.matmul(o1, v.wgu[r][:, x, c, k * FE + f * FH:k * FE + (f + 1) * FH],
                                            v.xgT[:, r % 2, c, x * CAP:(x + 1) * CAP], start=(c == 0), stop=(c == C - 1))
            last.then_inc(s["gu_done"], 1)

        def down(p, r):
            wait(e, s["he_s"], p + 1)
            if not (isinstance(p, int) and p < 2):
                wait(e, s["dout_s"], p - 1)
            for x in range(2):
                for f in range(2):
                    last = e.matmul(kb[r % 2][x * CAP:(x + 1) * CAP, 0:D], v.he[0:FH, r % 2, x, f, :], v.wd[r][0:FH, x, f, :],
                                    start=(f == 0), stop=(f == 1))
            last.then_inc(s["dn_done"], 1)

        def turn(o):
            for r in range(RING):
                p = o * RING + r
                place_rows(o, r)
                if not (isinstance(p, int) and p < 2):
                    down(p - 2, (r - 2) % RING)
                gate_up(o, r)

        turn(0)
        with e.Fori(1, EP // RING) as o:
            turn(o)
        for r in (2, 3):
            down(EP - RING + r, r)




def query_products(e, v, steps, heads):
    parts = []

    def product(d, t, cols):
        n = (HD - d) * NB
        y = v.ycv[:, :, heads, DOFF[d] * NB:DOFF[d] * NB + n]
        if d == 0:
            steps.did(e.tensor_tensor(v.acc[:, :, heads, :], v.q[:, :, heads, :], y, ALU.mult))
        else:
            wait(e, steps.sem, steps.base + steps.n)
            steps.did(e.tensor_tensor(v.tmp[:, t, :, heads, 0:n], v.q[:, :, heads, cols], y, ALU.mult))

    def add(d, t, cols):
        n = (HD - d) * NB
        wait(e, steps.sem, steps.base + steps.n - (1 if t == 0 else 0))
        steps.did(e.tensor_tensor(v.acc[:, :, heads, cols], v.acc[:, :, heads, cols], v.tmp[:, t, :, heads, 0:n], ALU.add))

    parts.append(lambda: product(0, 0, None))
    for d in range(1, HD):
        lo, hi = slice(0, (HD - d) * NB), slice(d * NB, HD * NB)
        for step, t, cols in ((product, 0, hi), (product, 1, lo), (add, 0, lo), (add, 1, hi)):
            parts.append(lambda step=step, d=d, t=t, cols=cols: step(d, t, cols))
    return parts


def dve_program(nc, block, v):
    s = v.s
    tb, mb, kb = v.tb, v.mb, v.kb
    hsteps, rsteps, qsteps = Steps(s["dve_h"], HDVE), Steps(s["dve_r"], RDVE), Steps(s["qstep"], QSTEPS)
    psteps = Steps(s["pick_s"], PDVE)
    NF = len(FSC)

    @block.vector
    def _(e):
        e.memset(v.eps_rms[:], EPS_RMS)
        e.memset(v.eps_ln[:], EPS_LN)
        e.memset(v.one[:], 1.0)
        e.memset(v.ones[:], 1.0)
        e.memset(v.pp[:], 2.0)
        e.memset(v.rtv[:, :, :, 0:3], 0.0)
        e.memset(v.cand[:], 0.0)
        e.memset(v.empty_row[:], 0.0)
        e.memset(v.idx_all[:], T).then_inc(s["consts_s"], 1)
        e.wait_ge(s["consts_s"], 1)
        e.memset(v.empty_row[0:1, D:ROW], float(4 * NZ)).then_inc(s["logit_read"], 1)
        e.wait_ge(s["lru_s"], 4)
        e.tensor_tensor(v.lru[:, 0], v.lru[:, 0], v.lru[:, 2], ALU.add).then_inc(s["lru_s"], 1)
        e.wait_ge(s["lru_s"], 5)
        e.tensor_scalar(v.lru[:, 1], v.lru[:, 0], -LRU_C, None, ALU.mult)
        e.tensor_scalar(v.lru[:, 0], v.lru[:, 0], LRU_C, None, ALU.mult).then_inc(s["lru_s"], 1)
        e.wait_ge(s["tnum_s"], 1)

        def norm_apply(dst, src, inv, done):
            for b in range(NB):
                e.tensor_scalar(dst[:, b, :], src[:, b, :], inv[:, b:b + 1], None, ALU.mult).then_inc(s[done], 1)

        def feature_copy(k, name, done):
            for c in range(C):
                e.tensor_scalar(v.xT[:, c, k * 2 * S:(k + 1) * 2 * S].rearrange("p (b s) -> p b s", b=2),
                                tb[k][:].rearrange("p (b c s) -> p b c s", b=2, c=C)[:, :, c, :],
                                col(v, name, c), None, ALU.mult).then_inc(s[done], 1)

        def votes_in(g):
            psteps.begin(g)
            wait(e, s["vote_tr"], g + 1)
            e.tensor_copy(v.cand[:, CAP:], kb[0][0:E, :]).then_inc(s["voteT_s"], 1)
            wait_apart(e, v, s["voteT_s"], g + 1)

        def rounds(a, b):
            for k in range(a, b):
                m = v.first[:, 8 * k:8 * k + 8]
                if k:
                    wait_apart(e, v, psteps.sem, psteps.base + psteps.n)
                n = psteps.did(e.max(m, v.cand[:]))
                wait_apart(e, v, psteps.sem, n)
                n = psteps.did(e.match_replace(v.cand[:], m, v.cand[:], 0.0))

        def keep_first():
            wait(e, psteps.sem, psteps.base + psteps.n)
            psteps.did(e.tensor_copy(v.cand[:, 0:CAP], v.first[:]))
            psteps.end()

        def shared_rows(g, f):
            n, bank = FSC[f], (mb[1], mb[3], kb[1])[f]
            wait(e, s["shg_s"], NF * g + f + 1)
            wait(e, s["shu_done"], (NF * g + f) * 2 + 2)
            e.tensor_tensor(v.shh[0:n, f, :], bank[0:n, :], v.sgl[0:n, f % 2, :], ALU.mult).then_inc(s["shh_s"], 1)

        def shared_sums(g):
            for k in range(2):
                wait(e, s["shd_done"], 2 * g + k + 1)
                e.tensor_tensor(v.u[:, 2 * k:2 * k + 2, :], kb[k][:].rearrange("p (b n) -> p b n", b=2),
                                v.rows[:, 2 * k:2 * k + 2, 0:D], ALU.add).then_inc(s["sh_s"], 1)

        def step(gh, gt, gs):
            head, tail = gh is not None, gt is not None
            if head:
                hsteps.begin(gh)
                wait(e, s["rms1_s"], gh + 1)
                e.reciprocal(v.inv1, v.rms1).then_inc(s["inv1_s"], 1)
                wait(e, s["inv1_s"], gh + 1)
                norm_apply(v.xn, v.xin, v.inv1, "xn_s")
                for k in range(2):
                    wait(e, s["x_tr"], 2 * gh + k + 1)
                    feature_copy(k, "norm1", "xT_s")
            if gs is not None:
                votes_in(gs)
                rounds(0, 4)
            if head:
                for c in range(C):
                    wait(e, s["right_s"], 2 * gh + c + 1)
                    o = v.cv[:, c, :].rearrange("p (b n) -> p b n", b=NB)
                    e.tensor_scalar(o, v.rtv[:, c, :, 0:S], col(v, "conv_w", c), col(v, "conv_b", c), ALU.mult, ALU.add)\
                        .then_inc(s["cvs"], 1)
                for k in range(1, 4):
                    for c in range(C):
                        o = v.cv[:, c, :].rearrange("p (b n) -> p b n", b=NB)
                        wait(e, s["cvs"], 8 * gh + 2 * k - 1 + c)
                        e.scalar_tensor_tensor(out=o, in0=v.rtv[:, c, :, k:k + S], scalar=col(v, "conv_w", C * k + c),
                                               in1=o, op0=ALU.mult, op1=ALU.add).then_inc(s["cvs"], 1)
            if tail:
                for k in range(2):
                    wait(e, s["x2_tr"], 2 * gt + k + 1)
                    e.tensor_copy(v.q[:].rearrange("p c h (i b) -> p b c (h i)", b=NB)[:, 2 * k:2 * k + 2],
                                  tb[k][:].rearrange("p (b c s) -> p b c s", b=2, c=C)).then_inc(s["q_s"], 1)
            if gs is not None:
                rounds(4, 8)
                keep_first()
            if head:
                a, i = v.ri[:, 0:2, :], v.ri[:, 2:4, :]
                wait(e, s["gate_s"], 4 * gh + 4)
                wait(e, s["gates_done"], 4 * gh + 4)
                wait(e, s["cvs"], 8 * gh + 8)
                hsteps.did(e.tensor_tensor(i, i, v.cv, ALU.mult))
                wait(e, s["act_a"], 2 * gh + 2)
                n = hsteps.did(e.tensor_tensor(v.hs, a, a, ALU.mult))
                wait(e, hsteps.sem, n)
                wait(e, s["th_s"], 2 * gh + 2)
                hsteps.did(e.scalar_tensor_tensor(out=v.th, in0=v.hs, scalar=1.0, in1=v.th, op0=ALU.add, op1=ALU.mult))
                n = hsteps.did(e.memset(v.ri[:, 0:2, :].rearrange("p c (b s) -> p (c b) s", b=NB)[:, :, 0:1], 0.0))
                wait(e, s["mult_s"], gh + 1)
                n = hsteps.did(e.tensor_tensor(v.th, v.th, i, ALU.mult))
                wait(e, hsteps.sem, n)
                n = hsteps.did(e.tensor_tensor_scan(v.hs.rearrange("p c n -> p (c n)"), a.rearrange("p c n -> p (c n)"),
                                                    v.th.rearrange("p c n -> p (c n)"), 0.0, ALU.mult, ALU.add))
                wait(e, hsteps.sem, n)
                wait(e, s["left_s"], 2 * gh + 2)
                e.tensor_tensor(v.left, v.left, v.hs, ALU.mult).then_inc(s["lr_s"], 1)
            if gs is not None and head:
                shared_rows(gs, 0)
                shared_rows(gs, 1)
            if head:
                for k in range(2):
                    wait(e, s["out_done"], 2 * gh + k + 1)
                    wait(e, s["xo_s"], gh + 1)
                    e.tensor_tensor(v.xo[:, 2 * k:2 * k + 2, :], kb[k][:].rearrange("p (b n) -> p b n", b=2),
                                    v.xo[:, 2 * k:2 * k + 2, :], ALU.add).then_inc(s["x1_s"], 1)
                wait(e, s["rms2_s"], gh + 1)
                n = hsteps.did(e.reciprocal(v.inv2, v.rms2))
                wait(e, hsteps.sem, n)
                norm_apply(v.xn, v.xo, v.inv2, "x1n_s")
                for k in range(2):
                    wait(e, s["x1_tr"], 2 * gh + k + 1)
                    feature_copy(k, "norm2", "x1T_s")

            if tail:
                qsteps.begin(gt)
                parts = query_products(e, v, qsteps, slice(0, HEADS_DVE))
                wait(e, s["conv_evac"], HEADS * gt + HEADS)
                wait(e, s["q_s"], 2 * gt + 2)
            else:
                parts = []
            if head:
                for j in range(FJ):
                    if j == 2 and gs is not None:
                        shared_rows(gs, 2)
                    if j == 5 and gs is not None:
                        shared_sums(gs)
                    wait(e, s["gelu_s"], FJ * gh + j + 1)
                    wait(e, s["up_done"], 2 * FJ * gh + 2 * j + 2)
                    e.scalar_tensor_tensor(out=v.mlp[:, j, :], in0=mb[(2 * j + 1) % 4][:], scalar=col(v, "up2_b", j),
                                           in1=v.gl[:, j % 2, :], op0=ALU.add, op1=ALU.mult).then_inc(s["h_s"], 1)
                    for f in parts[5 * j:5 * j + 5]:
                        f()
            else:
                for n, f in enumerate(parts):
                    if gs is not None and n in (4, 8, 12):
                        shared_rows(gs, n // 4 - 1)
                    if gs is not None and n == 24:
                        shared_sums(gs)
                    f()
            if tail:
                qsteps.end()
                rsteps.begin(gt)
                if gs is not None:
                    wait(e, s["sums_out"], 16 * gs + 16)
                for k in range(2):
                    wait(e, s["o_tr"], 2 * gt + k + 1)
                    e.tensor_tensor(v.u[:, 2 * k:2 * k + 2, :], tb[k][:].rearrange("p (b n) -> p b n", b=2),
                                    v.x2[:, 2 * k:2 * k + 2, :], ALU.add).then_inc(s["u_s"], 1)
                wait(e, s["u_s"], 2 * gt + 2)
                for b in range(NB):
                    last = e.bn_stats(v.bn[:, 1, b, :], v.u[:, b, :])
                n = rsteps.did(last)
                wait_apart(e, v, rsteps.sem, n)
                for b in range(NB):
                    last = e.bn_aggr(v.mv[:, 1, b, :], v.bn[:, 1, b, :])
                last.then_inc(s["lnB_s"], 1)
                wait(e, s["sdB_s"], gt + 1)
                e.reciprocal(v.isB, v.sdB).then_inc(s["isB_s"], 1)
                wait(e, s["isB_s"], gt + 1)
                wait(e, s["rows_out"], 16 * gt + 16)
                for b in range(NB):
                    e.tensor_scalar(v.rows[:, b, 0:D], v.u[:, b, :], v.mv[:, 1, b, 0:1], v.isB[:, b:b + 1],
                                    ALU.subtract, ALU.mult).then_inc(s["x3_s"], 1)
            def residual(k):
                wait(e, s["down_done"], 2 * gh + k + 1)
                wait(e, s["xs_s"], 2 * gh + 2)
                e.tensor_tensor(v.xs[:, 2 * k:2 * k + 2, :], kb[k][:].rearrange("p (b n) -> p b n", b=2),
                                v.xs[:, 2 * k:2 * k + 2, :], ALU.add).then_inc(s["y_s"], 1)
                wait(e, s["y_s"], 2 * gh + k + 1)
                for b in range(2 * k, 2 * k + 2):
                    last = e.bn_stats(v.bn[:, 0, b, :], v.xs[:, b, :])
                return last

            if head:
                residual(0)
            if tail:
                r, sem_r = rsteps, rsteps.sem
                lg = mb[0][:, 0:NB * E].rearrange("p (b n) -> p b n", b=NB)
                wait(e, s["logit_done"], gt + 1)
                e.tensor_reduce(v.mx, lg, AX.X, ALU.max).then_inc(s["mx_s"], 1)
                wait(e, s["mx_s"], gt + 1)
                e.tensor_tensor(v.logit[:], lg, v.mx[:, :, None].to_broadcast((P, NB, E)), ALU.subtract)\
                    .then_inc(s["logit_read"], 1)
            if head:
                n = hsteps.did(residual(1))
                wait_apart(e, v, hsteps.sem, n)
                for b in range(NB):
                    last = e.bn_aggr(v.mv[:, 0, b, :], v.bn[:, 0, b, :])
                last.then_inc(s["lnA_s"], 1)
            if tail:
                wait(e, s["exp_s"], gt + 1)
                n = r.did(e.tensor_reduce(v.sm, v.logit[:], AX.X, ALU.add))
                wait(e, sem_r, n)
                n = r.did(e.reciprocal(v.sm, v.sm))
                wait(e, sem_r, n)
                pv = v.pp[:, :, 2:]
                n = r.did(e.tensor_tensor(pv, v.logit[:], v.sm[:, :, None].to_broadcast((P, NB, E)), ALU.mult))
                wait_apart(e, v, sem_r, n)
                for b in range(NB):
                    last = e.max(v.m8[:, b, :], v.pp[:, b, :])
                n = r.did(last)
                e.tensor_copy(v.rows[:, :, D::2], pv)
                wait_apart(e, v, sem_r, n)
                for b in range(NB):
                    last = e.match_replace(v.pr[:, b, :], v.m8[:, b, :], v.pp[:, b, :], -1.0)
                n = r.did(last)
                wait(e, sem_r, n)
                n = r.did(e.tensor_scalar(v.mask[:], v.pr[:, :, 2:], 0.0, None, ALU.is_lt))
                wait(e, sem_r, n)
                r.did(e.tensor_tensor(v.votes[:], v.mask[:],
                                      v.tnum[:, :, None].to_broadcast((P, NB, E)), ALU.mult))
                n = r.did(e.tensor_tensor_scan(v.cum[:].rearrange("p b n -> p (b n)"), v.ones[:],
                                               v.mask[:].rearrange("p b n -> p (b n)"), 0.0, ALU.mult, ALU.add))
                wait(e, sem_r, n)
                n = r.did(e.tensor_tensor(v.cum[:], v.cum[:], v.mask[:], ALU.subtract))
                wait(e, sem_r, n)
                e.tensor_tensor(v.rows[:, :, D + 1::2], v.cum[:], v.zbase[:, :, None].to_broadcast((P, NB, E)), ALU.add)\
                    .then_inc(s["rows_s"], 1)
                r.did(e.tensor_scalar(v.tnum[:], v.tnum[:], float(-TG), None, ALU.add))
                wait(e, s["rows_s"], gt + 1)
                r.did(e.tensor_scalar(v.zbase[:], v.zbase[:], float(ZR * TG), None, ALU.add))
                r.end()
            if head:
                wait(e, s["sdA_s"], gh + 1)
                n = hsteps.did(e.reciprocal(v.isA, v.sdA))
                wait(e, hsteps.sem, n)
                for b in range(NB):
                    e.tensor_scalar(v.x2[:, b, :], v.xs[:, b, :], v.mv[:, 0, b, 0:1], v.isA[:, b:b + 1],
                                    ALU.subtract, ALU.mult).then_inc(s["x2_s"], 1)
                hsteps.end()

        over_groups(e, step)

        votes_in(G - 1)
        rounds(0, 2)
        for f in range(2):
            shared_rows(G - 1, f)
        rounds(2, 4)
        shared_rows(G - 1, 2)
        rounds(4, 8)
        e.wait_ge(psteps.sem, PDVE * (G - 1) + 16)
        for k in range(2):
            last = e.tensor_scalar(v.firstd[:, k, :], v.first[:], -1.0, 4096.0, ALU.mult, ALU.add)
        psteps.did(last)
        epilogue(nc, e, v, lambda: shared_sums(G - 1))


def epilogue(nc, e, v, last_sums):
    s = v.s
    tb, mb, kb = v.tb, v.mb, v.kb

    e.wait_ge(s["pickT_s"], 1)
    for x in range(2):
        e.tensor_scalar(v.idx_all[x * CAP:(x + 1) * CAP, 0:EP], tb[0][x * CAP:(x + 1) * CAP, x:E:2], float(T), None, ALU.min)\
            .then_inc(s["idx_s"], 1)
    e.wait_ge(s["idx_s"], 2)
    e.tensor_copy(v.idx_slot[:], v.idx_all[:, 0:RING]).then_inc(s["idxc_s"], 1)
    last_sums()

    def places(o, r):
        p = o * RING + r
        wait(e, s[f"gat{r}"], 16 * o + 16)
        if not (isinstance(o, int) and o == 0):
            wait(e, s[f"scat{r}"], 16 * o)
        for x in range(2):
            last = e.tensor_copy(v.pz_slot[x * CAP:(x + 1) * CAP, r, :],
                                 v.xg[x * CAP:(x + 1) * CAP, r, bass.ds(p * 4 + (D + 2 * x), 2)])
        last.then_inc(s["pz_s"], 1)
        wait(e, s["pz_s"], p + 1)
        e.tensor_copy(v.z_slot[:, r:r + 1], v.pz_slot[:, r, 1:2]).then_inc(s["zi_s"], 1)
        e.tensor_copy(v.idx_slot[:, r:r + 1], v.idx_all[:, bass.ds(p + RING, 1)]).then_inc(s["idxc_s"], 1)

    def hidden(o, r):
        p = o * RING + r
        wait(e, s["sg_s"], p + 1)
        if not (isinstance(p, int) and p < 2):
            wait(e, s["dn_done"], p - 1)
        e.tensor_tensor(v.he[0:FH, r % 2].rearrange("p e f n -> p (e f n)"), mb[r % 2][0:FH, 256:512],
                        v.sge[0:FH, r % 2, :], ALU.mult).then_inc(s["he_s"], 1)

    def weighted(p, r):
        wait(e, s["dn_done"], p + 1)
        e.tensor_scalar(v.dout[:, r, :], kb[r % 2][:, 0:D], v.pz_slot[:, r, 0:1], None, ALU.mult).then_inc(s["dout_s"], 1)

    def turn(o):
        for r in range(RING):
            p = o * RING + r
            places(o, r)
            if not (isinstance(p, int) and p < 2):
                weighted(p - 2, (r - 2) % RING)
            hidden(o, r)

    turn(0)
    with e.Fori(1, EP // RING) as o:
        turn(o)
    for r in (2, 3):
        weighted(EP - RING + r, r)

    def sums(i, k):
        n = i * FR + k
        y = v.u[:, k, :]
        wait(e, s[f"z{k}"], 16 * i + 16)
        e.tensor_reduce(y, v.zin[:, k, :].rearrange("p (k d) -> p d k", k=ZR), AX.X, ALU.add).then_inc(s["fdve"], 1)
        wait(e, s["fdve"], n * FDVE + 1)
        e.bn_stats(v.bn[:, 2, k, :], y).then_inc(s["fdve"], 1)

    def spread(i, k):
        n = i * FR + k
        wait_apart(e, v, s["fdve"], n * FDVE + 2)
        e.bn_aggr(v.mv[:, 2, k, :], v.bn[:, 2, k, :]).then_inc(s["fdve"], 1)

    def normalise(i, k, fresh):
        n = i * FR + k
        wait(e, s["fsd"], n + 1)
        e.reciprocal(v.isF[:, k:k + 1], v.sdF[:, k:k + 1]).then_inc(s["isF_s"], 1)
        wait(e, s["isF_s"], n + 1)
        if not fresh:
            wait(e, s[f"out{k}"], 16 * i)
        e.tensor_scalar(v.x2[:, k, :], v.u[:, k, :], v.mv[:, 2, k, 0:1], v.isF[:, k:k + 1], ALU.subtract, ALU.mult)\
            .then_inc(s["f_s"], 1)

    def final(i, first):
        for k in range(FR):
            sums(i, k)
            if k:
                normalise(i, k - 1, first)
            spread(i, k)
        normalise(i, FR - 1, first)

    final(0, True)
    with e.Fori(1, B // FR) as i:
        final(i, False)


def _by_chunk(np_, a):
    return np_.ascontiguousarray(a.reshape(-1, P, a.shape[-1]).transpose(1, 0, 2))


def kernel(**inputs):
    import numpy as _np
    import concourse.bacc as _bacc
    from concourse import mybir as _mybir
    from concourse.bass_utils import run_bass_kernel_spmd as _run

    a = {k: _np.asarray(w) for k, w in inputs.items()}
    at = lambda n: a["L0_attn_" + n]
    ff = lambda n: a["L0_ffn_" + n]
    column = lambda w: w.reshape(-1, P).T
    cols = _np.concatenate([column(at("norm1_w")), column(at("norm2_w")), column(at("left_b")), column(at("right_b")),
                            column(at("conv_b"))] + [column(at("conv_w")[k]) for k in range(4)] +
                           [column(at(n)) for n in ("ga_b", "gx_b", "a_param", "up1_b", "up2_b")], axis=1)
    both = lambda m, n: _by_chunk(_np, _np.concatenate([at(m), at(n)], axis=1))
    ssm = a["L0_xattn_ssm_kernel"]
    kpad = _np.concatenate([_np.zeros((HEADS, P - 1), ssm.dtype), ssm], axis=1)
    shd = ff("sh_down").T
    shd = _np.concatenate([shd, _np.zeros((len(FSC) * P - FS, D), shd.dtype)], axis=0)
    gu = _np.stack([ff("w_gate"), ff("w_up")], axis=2)
    arrays = {
        "x": a["x"], "ctx": a["ctx_2048"], "cols": cols,
        "out_b": at("out_b")[None], "down_b": at("down_b")[None], "d": a["L0_xattn_D"][None], "kpad": kpad,
        "w_left_right": both("left_W", "right_W"), "w_gates": both("ga_W", "gx_W"), "w_out": _by_chunk(_np, at("out_W")),
        "w_up": both("up1_W", "up2_W"), "w_down": _by_chunk(_np, at("down_W")),
        "w_router": _by_chunk(_np, ff("gate_w").T),
        "w_shared": _by_chunk(_np, _np.concatenate([ff("sh_gate").T, ff("sh_up").T], axis=1)),
        "w_shared_down": _by_chunk(_np, shd),
        "w_experts": gu.reshape(EP, 2, C, P, 2 * FE).transpose(0, 3, 1, 2, 4),
        "w_experts_down": ff("w_down").reshape(EP, 2, 2, FH, D).transpose(0, 3, 1, 2, 4),
    }
    nc = _bacc.Bacc("TRN2", target_bir_lowering=False, num_devices=1)
    feeds, args = {}, []
    for name, w in arrays.items():
        w = _np.ascontiguousarray(w)
        feeds[f"in_{name}_dram"] = w
        args.append(nc.dram_tensor(f"in_{name}_dram", w.shape, _mybir.dt.from_np(w.dtype), kind="ExternalInput").ap())
    args.append(nc.dram_tensor("out_0_dram", (B, S, D), F32, kind="ExternalOutput").ap())
    build(nc, *args)
    r = _run(nc, [feeds], core_ids=[0])
    return r.results[0]["out_0_dram"]
```

```python
from contextlib import ExitStack

import concourse.bass as bass
from concourse import mybir

F32 = mybir.dt.float32
I32 = mybir.dt.int32
ALU = mybir.AluOpType
ACT = mybir.ActivationFunctionType
AX = mybir.AxisListType

P = 128
B, S, D = 16, 128, 256
T = B * S
C = D // P
G = 4
NB = B // G
TG = NB * S
F = 768
FJ = F // P
HD = 8
HEADS = S // HD
HEADS_DVE = 11
PAIRS = HD * (HD + 1) // 2
PW = PAIRS * NB
E, FE, CAP, TOPK = 64, 176, 64, 6
FH = FE // 2
FS = 352
FSC = [128, 128, 96]
EP = E // 2
RING = 5
WRING = 10
ROW = D + 2 * E
NZ = T * (TOPK + 1)
ZR = TOPK + 1
KW = P - 1 + D
FR = 4
EPS_RMS, EPS_LN, LRU_C = 1e-8, 1e-5, 8.0

COLS = {}
for _name, _n in (("norm1", C), ("norm2", C), ("left_b", C), ("right_b", C), ("conv_b", C), ("conv_w", 4 * C),
                  ("ga_b", C), ("gx_b", C), ("a_param", C), ("up1_b", FJ), ("up2_b", FJ)):
    COLS[_name] = sum(n for _, n in COLS.values()), _n
NCOLS = sum(n for _, n in COLS.values())

DOFF = [sum(HD - k for k in range(d)) for d in range(HD)]


class Steps:

    def __init__(self, sem, per):
        self.sem, self.per = sem, per

    def begin(self, g):
        self.base, self.n = self.per * g, 0

    def did(self, ins):
        ins.then_inc(self.sem, 1)
        self.n += 1
        return self.base + self.n

    def end(self):
        assert self.n == self.per, (self.n, self.per)


class Shared:
    pass


def build(nc, x, ctx_in, cols_in, outb_in, downb_in, d_in, kpad_in, wlr_in, wg_in, wo_in, wup_in, wdn_in,
          wgate_in, wsh_in, wshd_in, wgu_in, wd_in, out):
    v = Shared()
    v.x, v.ctx_in, v.cols_in, v.outb_in, v.downb_in, v.d_in, v.kpad_in, v.wlr_in, v.wg_in = \
        x, ctx_in, cols_in, outb_in, downb_in, d_in, kpad_in, wlr_in, wg_in
    v.wo_in, v.wup_in, v.wdn_in, v.wgate_in, v.wsh_in, v.wshd_in, v.wgu_in, v.wd_in, v.out = \
        wo_in, wup_in, wdn_in, wgate_in, wsh_in, wshd_in, wgu_in, wd_in, out
    v.rows_dram = nc.dram_tensor("rows_dram", (T + 1, ROW), F32, kind="Internal").ap()
    v.krep_dram = nc.dram_tensor("krep_dram", (HEADS, P * KW), F32, kind="Internal").ap()
    v.z_dram = nc.dram_tensor("z_dram", (NZ, D), F32, kind="Internal").ap()

    with ExitStack() as stack:
        def sb(name, shape, dt=F32):
            return stack.enter_context(nc.sbuf_tensor(name, shape, dt))

        def sem(name):
            return stack.enter_context(nc.semaphore(name))

        v.cols = sb("cols", [P, NCOLS])
        v.outb, v.downb = sb("outb", [P, D]), sb("downb", [P, D])
        v.d_sb = sb("d_sb", [P, HEADS])
        v.ident = sb("ident", [P, P])
        v.ones = sb("ones", [P, NB * E])
        v.zeros = sb("zeros", [P, 512])
        v.table = sb("table", [P, 1])
        v.eps_rms, v.eps_ln, v.one = sb("eps_rms", [P, 1]), sb("eps_ln", [P, 1]), sb("one", [P, 1])
        v.lru = sb("lru", [P, 3, C])
        v.tnum = sb("tnum", [P, NB])
        v.zbase = sb("zbase", [P, NB])
        v.empty_row = sb("empty_row", [1, ROW])
        v.wsh = sb("wsh", [P, C, 2 * FS])
        v.wshd = sb("wshd", [P, len(FSC), D])
        v.wgate = sb("wgate", [P, C, E])
        v.x3T = sb("x3T", [P, C, TG])
        v.votes = sb("votes", [P, NB, E])
        v.cand = sb("cand", [E, CAP + TG])
        v.sgl = sb("sgl", [P, 2, TG])
        v.shh = sb("shh", [P, len(FSC), TG])
        v.first = sb("first", [E, CAP])
        v.firstd = sb("firstd", [E, 2, CAP])
        v.idx_all = sb("idx_all", [P, EP + RING], I32)
        v.idx_slot = sb("idx_slot", [P, RING], I32)
        v.z_slot = sb("z_slot", [P, RING], I32)
        v.pz_slot = sb("pz_slot", [P, RING, 2])

        wregion = sb("wregion", [P, 11264])
        at = [0]

        def take(n, region=None):
            v = (region or wregion)[:, at[0]:at[0] + n]
            at[0] += n
            return v

        v.wlr = take(C * 2 * D).rearrange("p (c n) -> p c n", c=C)
        v.wg = take(C * 2 * D).rearrange("p (c n) -> p c n", c=C)
        v.wo = take(C * D).rearrange("p (c n) -> p c n", c=C)
        v.wup = take(C * 2 * F).rearrange("p (c n) -> p c n", c=C)
        v.wdn = take(FJ * D).rearrange("p (c n) -> p c n", c=FJ)
        v.toep = take(HEADS * 2 * P).rearrange("p (h n) -> p h n", h=HEADS)

        def expert_weights(n, region):
            wgu = [take(2 * C * 2 * FE, region).rearrange("p (e c n) -> p e c n", e=2, c=C) for _ in range(n)]
            wd = [take(2 * 2 * D, region).rearrange("p (e f n) -> p e f n", e=2, f=2) for _ in range(n)]
            return list(zip(wgu, wd))

        at[0] = 0
        w_ring = expert_weights(4, wregion)
        v.he = take(2 * 4 * CAP).rearrange("p (k e f n) -> p k e f n", k=2, e=2, f=2)
        at[0] = 0
        v.zin = take(FR * ZR * D).rearrange("p (k n) -> p k n", k=FR)

        hregion = sb("hregion", [P, 13400])
        at[0] = 0
        v.xin = take(NB * D, hregion).rearrange("p (b n) -> p b n", b=NB)
        v.xn = take(NB * D, hregion).rearrange("p (b n) -> p b n", b=NB)
        v.xT = take(C * TG, hregion).rearrange("p (c n) -> p c n", c=C)
        v.left = take(C * TG, hregion).rearrange("p (c n) -> p c n", c=C)
        rt = take(C * NB * (S + 3), hregion)
        v.rtv = rt.rearrange("p (c b n) -> p c b n", c=C, b=NB)
        v.hs = take(C * TG, hregion).rearrange("p (c n) -> p c n", c=C)
        v.cv = take(C * TG, hregion).rearrange("p (c n) -> p c n", c=C)
        v.mlp = take(FJ * TG, hregion).rearrange("p (c n) -> p c n", c=FJ)
        v.ri = v.mlp[:, 0:4, :]
        v.th = v.mlp[:, 4:6, :]
        v.xo = take(NB * D, hregion).rearrange("p (b n) -> p b n", b=NB)
        v.xs = take(NB * D, hregion).rearrange("p (b n) -> p b n", b=NB)
        v.gl = take(2 * TG, hregion).rearrange("p (k n) -> p k n", k=2)
        at[0] = 0
        h_ring = expert_weights(4, hregion)
        v.xg = take(RING * ROW, hregion).rearrange("p (r n) -> p r n", r=RING)
        v.xgT = take(2 * C * P, hregion).rearrange("p (k c n) -> p k c n", k=2, c=C)
        v.sge = take(2 * 4 * CAP, hregion).rearrange("p (k n) -> p k n", k=2)

        v.ctxT = sb("ctxT", [P, C, S * NB])
        cregion = sb("cregion", [P, 10752])
        at[0] = 0
        v.kv = take(2 * C * 4 * PW, cregion).rearrange("p (k c h n) -> p k c h n", k=2, c=C, h=4)
        v.ycv = take(C * HEADS * PW, cregion).rearrange("p (c h n) -> p c h n", c=C, h=HEADS)
        v.q = take(C * HEADS * HD * NB, cregion).rearrange("p (c h n) -> p c h n", c=C, h=HEADS)
        v.acc = take(C * HEADS * HD * NB, cregion).rearrange("p (c h n) -> p c h n", c=C, h=HEADS)
        v.tmp = take(2 * C * HEADS * (HD - 1) * NB, cregion).rearrange("p (t c h n) -> p t c h n", t=2, c=C, h=HEADS)
        at[0] = 0
        v.ring = h_ring + w_ring + expert_weights(WRING - 8, cregion)
        v.dout = take(RING * D, cregion).rearrange("p (r n) -> p r n", r=RING)
        v.x2 = sb("x2", [P, NB, D])
        v.u = sb("u", [P, NB, D])
        v.rows = sb("rows", [P, NB, ROW])
        v.logit = sb("logit", [P, NB, E])
        v.pp = sb("pp", [P, NB, E + 2])
        v.pr = sb("pr", [P, NB, E + 2])
        v.mask = sb("mask", [P, NB, E])
        v.cum = sb("cum", [P, NB, E])
        v.m8 = sb("m8", [P, NB, 8])
        st = sb("st", [P, 12, NB])
        v.bn = sb("bn", [P, 3, NB, 6])
        v.mv = sb("mv", [P, 3, NB, 2])
        v.sdF, v.isF = sb("sdF", [P, FR]), sb("isF", [P, FR])
        v.ss1, v.rms1, v.inv1 = st[:, 0], st[:, 1], st[:, 2]
        v.ss2, v.rms2, v.inv2 = st[:, 3], st[:, 4], st[:, 5]
        v.sdA, v.isA, v.sdB, v.isB, v.mx, v.sm = (st[:, k] for k in range(6, 12))

        v.tb = [stack.enter_context(nc.psum_tensor(f"tb{k}", [P, 512], F32)) for k in range(2)]
        v.mb = [stack.enter_context(nc.psum_tensor(f"mb{k}", [P, 512], F32)) for k in range(4)]
        v.kb = [stack.enter_context(nc.psum_tensor(f"kb{k}", [P, 512], F32)) for k in range(2)]

        names = """consts_in weights_in x_in ctx_in_s idn tables lru_s d_done tnum_s shw_in zero_out 
            kv_ready conv_done conv_evac
            ss1_s rms1_s inv1_s xn_s x_tr xT_s lr_done left_s right_s cvs gates_done gate_s act_a th_s dve_h
            mult_s lr_s out_done xo_s xs_s x1_s ss2_s rms2_s x1n_s x1_tr x1T_s up_done gelu_s h_s down_done y_s
            lnA_s sdA_s x2_s x2_tr q_s qstep qpool o_tr u_s lnB_s sdB_s x3_s x3_tr x3T_s logit_done logit_read exp_s
            dve_r rows_s rows_out vote_tr voteT_s pick_s pickT_s idx_s shu_done shg_s shh_s shd_done sh_s sums_out
            
            idxc_s pz_s zi_s g_tr gT_s gu_done sg_s he_s dn_done dout_s z0 z1 z2 z3 sum_pe sum_dve stats_s aggr_s fsd f_s out0 out1 out2 out3 isA_s isB_s isF_s mx_s consts_s krep_out""".split()
        for n, count in (("wring", WRING), ("gat", RING), ("scat", RING)):
            names += [f"{n}{k}" for k in range(count)]
        v.s = {n: sem(n) for n in names}

        with nc.Block() as block:
            sync_program(nc, block, v)
            pool_program(nc, block, v)
            act_program(nc, block, v)
            pe_program(nc, block, v)
            dve_program(nc, block, v)


def col(v, name, k, p=P):
    o, n = COLS[name]
    assert k < n
    return v.cols[0:p, o + k:o + k + 1]


def wait(e, sem, value):
    if not (isinstance(value, int) and value <= 0):
        e.wait_ge(sem, value)


def wait_apart(e, v, sem, value):
    if not isinstance(value, int):
        value = e.to_reg(value)
        e.wait_ge(v.s["consts_s"], 1)
    e.wait_ge(sem, value)


class Pair:

    def __init__(self, i, j):
        self.p = WRING * i + (2 + j)
        self.row, self.turn = (2 + j) % RING, WRING // RING * i + (2 + j) // RING
        self.slot, self.load = (2 + j) % WRING, i + (2 + j) // WRING
        self.half = j % 2

    def first(self, n):
        return isinstance(self.p, int) and self.p < n


def over_pairs(e, step):
    def turn(i):
        for j in range(WRING):
            step(Pair(i, j), Pair(i, j - 2))

    for j in (-2, -1):
        step(Pair(0, j), None)
    turn(0)
    with e.Fori(1, (EP - 2) // WRING) as i:
        turn(i)
    for j in (-2, -1):
        step(None, Pair((EP - 2) // WRING, j))


def over_groups(e, step):
    step(0, None, None)
    step(1, 0, None)
    with e.Fori(2, G) as g:
        step(g, g - 1, g - 2)
    step(None, G - 1, G - 2)


def sync_program(nc, block, v):
    s = v.s

    @block.sync
    def _(e):
        def load_x(g):
            if not (isinstance(g, int) and g == 0):
                wait_apart(e, v, s["xn_s"], 4 * g)
                wait(e, s["xo_s"], g)
                wait(e, s["xs_s"], 2 * g)
            e.dma_start(v.xin, v.x[bass.ds(g * NB, NB), :, :].rearrange("b s d -> s b d")).then_inc(s["x_in"], 16)

        def load_ctx(g):
            if not (isinstance(g, int) and g == 0):
                wait_apart(e, v, s["kv_ready"], 4 * g)
            e.dma_start(v.ctxT[:], v.ctx_in[bass.ds(g, 1)].rearrange("o p c n -> (o p) c n")).then_inc(s["ctx_in_s"], 16)

        load_x(0)
        for dst, src in ((v.cols[:], v.cols_in), (v.outb[:], v.outb_in.to_broadcast((P, D))),
                         (v.downb[:], v.downb_in.to_broadcast((P, D))), (v.d_sb[:], v.d_in.to_broadcast((P, HEADS)))):
            e.dma_start(dst, src).then_inc(s["consts_in"], 16)
        for dst, src in ((v.wlr, v.wlr_in), (v.wg, v.wg_in), (v.wo, v.wo_in), (v.wup, v.wup_in), (v.wdn, v.wdn_in)):
            e.dma_start(dst, src).then_inc(s["weights_in"], 16)
        e.dma_start(v.krep_dram.rearrange("h (m n) -> h m n", n=KW), v.kpad_in[:, None, :].to_broadcast((HEADS, P, KW)))\
            .then_inc(s["krep_out"], 16)
        load_ctx(0)
        for dst, src in ((v.wgate[:], v.wgate_in), (v.wsh[:], v.wsh_in), (v.wshd[:], v.wshd_in)):
            e.dma_start(dst, src).then_inc(s["shw_in"], 16)
        e.wait_ge(s["krep_out"], 16)
        k = v.krep_dram[0:HEADS, P - 1:P + 1]
        e.dma_start(v.toep, bass.AP(k.tensor, k.offset, [[KW - 1, P], [P * KW, HEADS], [1, 2 * P]])).then_inc(s["tables"], 16)
        e.wait_ge(s["idn"], 1)
        zv = v.z_dram.rearrange("(k p m) d -> k p (m d)", k=8, p=P)
        for k in range(8):
            e.dma_start(zv[k].rearrange("p (r n) -> p r n", n=512), v.zeros[:, None, :].to_broadcast((P, NZ * D // 8 // P // 512, 512)))\
                .then_inc(s["zero_out"], 16)
        with e.Fori(1, G) as g:
            load_x(g)
            load_ctx(g)

        def load_pair(p, place, name):
            e.dma_start(place[0], v.wgu_in[bass.ds(p, 1)].rearrange("o p e c n -> (o p) e c n")).then_inc(s[name], 16)
            e.dma_start(place[1][0:FH], v.wd_in[bass.ds(p, 1)].rearrange("o p e f n -> (o p) e f n")).then_inc(s[name], 16)

        e.wait_ge(s["x2_s"], 4 * G)
        for p in range(4):
            load_pair(p, v.ring[p], f"wring{p}")
        e.wait_ge(s["conv_done"], HEADS * G)
        for p in range(4, 8):
            load_pair(p, v.ring[p], f"wring{p}")
        e.wait_ge(s["o_tr"], 2 * G)
        for p in range(8, WRING):
            load_pair(p, v.ring[p], f"wring{p}")
        def refill(p, w):
            wait(e, s["dn_done"], p - (WRING - 1))
            load_pair(p, v.ring[w], f"wring{w}")

        with e.Fori(0, EP // WRING - 1) as i:
            for w in range(WRING):
                refill(i * WRING + (WRING + w), w)
        for p in range(EP // WRING * WRING, EP):
            refill(p, p % WRING)

        for r in range(RING):
            e.wait_ge(s[f"scat{r}"], 16 * len(range(r, EP, RING)))
        e.wait_ge(s["sums_out"], 16 * G)

        def load_sums(b, k):
            e.dma_start(v.zin[:, k, :], v.z_dram[bass.ds(b * S * ZR, S * ZR), :].rearrange("(s k) d -> s (k d)", k=ZR))\
                .then_inc(s[f"z{k}"], 16)

        def store(b, k, n):
            wait(e, s["f_s"], n)
            e.dma_start(v.out[bass.ds(b, 1), :, :].rearrange("b s d -> (b s) d"), v.x2[:, k, :]).then_inc(s[f"out{k}"], 16)

        for k in range(FR):
            load_sums(k, k)
        with e.Fori(1, B // FR) as i:
            for k in range(FR):
                wait(e, s["sum_pe" if k % 2 else "sum_dve"], (i - 1) * (FR // 2) + k // 2 + 1)
                load_sums(FR * i + k, k)
                store(FR * (i - 1) + k, k, FR * (i - 1) + k + 1)
        for k in range(FR):
            store(B - FR + k, k, B - FR + k + 1)
        for k in range(FR):
            e.wait_ge(s[f"out{k}"], 16 * (B // FR))


HDVE = 12
RDVE = 12
QSTEPS = 1 + 4 * (HD - 1)
PDVE = 17


def pool_program(nc, block, v):
    s = v.s
    psteps = Steps(s["qpool"], QSTEPS)

    @block.gpsimd
    def _(e):
        e.memset(v.zeros[:], 0.0).then_inc(s["idn"], 1)
        e.memset(v.ident[:], 0.0).then_inc(s["idn"], 1)
        e.wait_ge(s["idn"], 2)
        e.affine_select(out=v.ident[:], in_=v.ident[:], compare_op=ALU.not_equal, fill=1.0, base=0,
                        pattern=[[-1, P]], channel_multiplier=1).then_inc(s["idn"], 1)
        e.iota(v.tnum[:], pattern=[[-S, NB]], base=4096, channel_multiplier=-1, allow_small_or_imprecise_dtypes=True)
        e.iota(v.zbase[:], pattern=[[ZR * S - TOPK, NB]], base=0, channel_multiplier=ZR,
               allow_small_or_imprecise_dtypes=True).then_inc(s["tnum_s"], 1)
        e.wait_ge(s["logit_read"], 1)
        e.dma_start(v.rows_dram[T:T + 1, :], v.empty_row[:]).then_inc(s["rows_out"], 16)
        e.wait_ge(s["tables"], 16)
        e.wait_ge(s["consts_in"], 16 * 4)
        e.wait_ge(s["idn"], 3)
        dtmp = v.ycv[:, 0, :, 0:P]
        e.tensor_tensor(dtmp, v.ident[:, None, :].to_broadcast((P, HEADS, P)),
                        v.d_sb[:, :, None].to_broadcast((P, HEADS, P)), ALU.mult).then_inc(s["d_done"], 1)
        e.wait_ge(s["d_done"], 1)
        e.tensor_tensor(v.toep[:, :, 0:P], v.toep[:, :, 0:P], dtmp, ALU.add).then_inc(s["d_done"], 1)

        def products(gt, hb):
            wait(e, s["ctx_in_s"], 16 * gt + 16)
            wait(e, s["conv_done"], HEADS * gt + 4 * (hb - 1))
            cx = v.ctxT[:].rearrange("p c (h n) -> p c h n", h=HEADS)[:, :, 4 * hb:4 * hb + 4, :]
            for d in range(HD):
                n = (HD - d) * NB
                last = e.tensor_tensor(v.kv[:, hb % 2, :, :, DOFF[d] * NB:DOFF[d] * NB + n],
                                       cx[:, :, :, 0:n], cx[:, :, :, d * NB:d * NB + n], ALU.mult)
            last.then_inc(s["kv_ready"], 1)

        def step(gh, gt, gs):
            if gh is not None:
                wait(e, s["x_in"], 16 * gh + 16)
                if not (isinstance(gh, int) and gh == 0):
                    wait(e, s["x1n_s"], 4 * gh)
                e.tensor_tensor(v.xo, v.xin, v.outb[:, None, :].to_broadcast((P, NB, D)), ALU.add)\
                    .then_inc(s["xo_s"], 1)
                if gt is not None:
                    products(gt, 2)
                if gt is not None:
                    wait(e, s["x2_s"], 4 * gh)
                e.tensor_tensor(v.xs, v.xin, v.downb[:, None, :].to_broadcast((P, NB, D)), ALU.add)\
                    .then_inc(s["xs_s"], 1)
            elif gt is not None:
                products(gt, 2)
            if gt is not None:
                products(gt, 3)
            if gh is not None:
                products(gh, 0)
                products(gh, 1)
                wait(e, s["x1_s"], 2 * gh + 2)
                wait(e, s["xs_s"], 2 * gh + 1)
                e.tensor_tensor(v.xs, v.xs, v.xo, ALU.add).then_inc(s["xs_s"], 1)
            if gt is not None:
                psteps.begin(gt)
                wait(e, s["conv_evac"], HEADS * gt + HEADS)
                wait(e, s["q_s"], 2 * gt + 2)
                for f in query_products(e, v, psteps, slice(HEADS_DVE, HEADS)):
                    f()
                psteps.end()
            if gs is not None:
                store_sums(gs)
            if gt is not None:
                wait(e, s["rows_s"], gt + 1)
                e.dma_start(v.rows_dram[bass.ds(gt * TG, TG), :].rearrange("(b s) n -> s b n", s=S), v.rows[:])\
                    .then_inc(s["rows_out"], 16)

        def store_sums(g):
            e.wait_ge(s["zero_out"], 16 * 8)
            wait(e, s["sh_s"], 2 * g + 2)
            e.dma_start(v.z_dram.rearrange("(b s k) d -> s b k d", s=S, k=ZR)[:, bass.ds(g * NB, NB), TOPK, :], v.u[:])\
                .then_inc(s["sums_out"], 16)

        over_groups(e, step)

        def gather(r):
            e.indirect_dma_start(out=v.xg[:, r, :], out_offset=None, in_=v.rows_dram[:, :],
                                 in_offset=bass.IndirectOffsetOnAxis(ap=v.idx_slot[:, r:r + 1], axis=0))\
                .then_inc(s[f"gat{r}"], 16)

        def scatter(r):
            e.indirect_dma_start(out=v.z_dram[:, :], out_offset=bass.IndirectOffsetOnAxis(ap=v.z_slot[:, r:r + 1], axis=0),
                                 in_=v.dout[:, r, :], in_offset=None, bounds_check=NZ - 1, oob_is_err=False)\
                .then_inc(s[f"scat{r}"], 16)

        e.wait_ge(s["rows_out"], 16 * (G + 1))
        e.wait_ge(s["idxc_s"], 1)
        for r in range(RING):
            gather(r)
        store_sums(G - 1)
        def scatter_next(o, r, more):
            p = o * RING + r
            wait_apart(e, v, s["dout_s"], p + 1)
            scatter(r)
            if more:
                wait_apart(e, v, s["idxc_s"], p + 2)
                wait(e, s["g_tr"], p + 1)
                gather(r)

        with e.Fori(0, EP // RING - 1) as o:
            for r in range(RING):
                scatter_next(o, r, True)
        for p in range((EP // RING - 1) * RING, EP):
            scatter_next(p // RING, p % RING, p + RING < EP)


def act_program(nc, block, v):
    s = v.s
    mb, kb = v.mb, v.kb

    @block.scalar
    def _(e):
        def softplus():
            o, n = COLS["a_param"]
            ap = v.cols[:, o:o + n]
            e.wait_ge(s["consts_in"], 16 * 4)
            e.activation(v.lru[:, 0], ap, ACT.Abs).then_inc(s["lru_s"], 1)
            e.wait_ge(s["lru_s"], 1)
            e.activation(v.lru[:, 0], v.lru[:, 0], ACT.Exp, scale=-1.0).then_inc(s["lru_s"], 1)
            e.wait_ge(s["lru_s"], 2)
            e.wait_ge(s["consts_s"], 1)
            e.activation(v.lru[:, 0], v.lru[:, 0], ACT.Ln, bias=v.one[:]).then_inc(s["lru_s"], 1)
            e.activation(v.lru[:, 2], ap, ACT.Relu).then_inc(s["lru_s"], 1)

        def silu_shared(g, f):
            n, bank = FSC[f], (mb[0], mb[2], kb[0])[f]
            wait(e, s["shu_done"], (g * len(FSC) + f) * 2 + 1)
            if f >= 2:
                wait(e, s["shh_s"], g * len(FSC) + f - 1)
            e.activation(v.sgl[0:n, f % 2, :], bank[0:n, :], ACT.Silu).then_inc(s["shg_s"], 1)

        def step(gh, gt, gs):
            head, tail = gh is not None, gt is not None

            def conv_out(h):
                wait(e, s["conv_done"], HEADS * gt + h + 1)
                e.activation(v.ycv[:, :, h, :], v.mb[h % 4][:, 0:C * PW].rearrange("p (c n) -> p c n", c=C), ACT.Copy)\
                    .then_inc(s["conv_evac"], 1)

            def mean_square(src, dst, name):
                for b in range(NB):
                    last = e.activation(v.xn[:, b, :], src[:, b, :], ACT.Square, accum_out=dst[:, b:b + 1])
                last.then_inc(s[name], 1)

            if head:
                wait(e, s["x_in"], 16 * gh + 16)
                if not (isinstance(gh, int) and gh == 0):
                    wait(e, s["x1_tr"], 2 * gh)
                mean_square(v.xin, v.ss1, "ss1_s")
                wait(e, s["ss1_s"], gh + 1)
                if not tail:
                    e.wait_ge(s["consts_s"], 1)
                e.activation(v.rms1, v.ss1, ACT.Sqrt, scale=1.0 / D, bias=v.eps_rms[:]).then_inc(s["rms1_s"], 1)
                if not tail:
                    softplus()
            if tail:
                wait(e, s["lnA_s"], gt + 1)
                e.activation(v.sdA, v.mv[:, 0, :, 1], ACT.Sqrt, bias=v.eps_ln[:]).then_inc(s["sdA_s"], 1)
            if tail:
                for h in range(8):
                    conv_out(h)
            if head:
                for c in range(C):
                    wait(e, s["lr_done"], 4 * gh + c + 1)
                    e.activation(v.rtv[:, c, :, 3:], mb[c][:].rearrange("p (b n) -> p b n", b=NB), ACT.Identity,
                                 bias=col(v, "right_b", c)).then_inc(s["right_s"], 1)
                for c in range(C):
                    wait(e, s["lr_done"], 4 * gh + C + c + 1)
                    e.activation(v.left[:, c, :], mb[C + c][:], ACT.Gelu, bias=col(v, "left_b", c)).then_inc(s["left_s"], 1)
            if tail:
                for h in range(8, 12):
                    conv_out(h)
            if head:
                for k in range(2 * C):
                    wait(e, s["gates_done"], 4 * gh + k + 1)
                    e.activation(v.ri[:, k, :], v.mb[k][:], ACT.Sigmoid, bias=col(v, ("ga_b", "gx_b")[k // C], k % C))\
                        .then_inc(s["gate_s"], 1)
                wait(e, s["gate_s"], 4 * gh + 2)
                wait(e, s["lru_s"], 6)
                for c in range(C):
                    e.activation(v.th[:, c, :], v.ri[:, c, :], ACT.Tanh, scale=v.lru[:, 0, c:c + 1]).then_inc(s["th_s"], 1)
                for c in range(C):
                    e.activation(v.ri[:, c, :], v.ri[:, c, :], ACT.Exp, scale=v.lru[:, 1, c:c + 1]).then_inc(s["act_a"], 1)
            if tail:
                for h in range(12, 16):
                    conv_out(h)
            if head:
                for c in range(C):
                    wait(e, s["dve_h"], HDVE * gh + 3 + 2 * c)
                    e.activation(v.th[:, c, :], v.th[:, c, :], ACT.Sqrt).then_inc(s["mult_s"], 1)
            if gs is not None:
                silu_shared(gs, 0)
                silu_shared(gs, 1)
            if head:
                e.activation(v.table[:], v.one[:], ACT.Sqrt)
                wait(e, s["x1_s"], 2 * gh + 2)
                wait(e, s["x_tr"], 2 * gh + 2)
                mean_square(v.xo, v.ss2, "ss2_s")
                wait(e, s["ss2_s"], gh + 1)
                e.activation(v.rms2, v.ss2, ACT.Sqrt, scale=1.0 / D, bias=v.eps_rms[:]).then_inc(s["rms2_s"], 1)
            if gs is not None and not head:
                silu_shared(gs, 2)
            if head:
                for j in range(FJ):
                    if j == 2 and gs is not None:
                        silu_shared(gs, 2)
                    wait(e, s["up_done"], 2 * FJ * gh + 2 * j + 1)
                    if j >= 2:
                        wait(e, s["h_s"], FJ * gh + j - 1)
                    e.activation(v.gl[:, j % 2, :], v.mb[2 * j % 4][:], ACT.Gelu, bias=col(v, "up1_b", j))\
                        .then_inc(s["gelu_s"], 1)
            if tail:
                wait(e, s["lnB_s"], gt + 1)
                e.activation(v.sdB, v.mv[:, 1, :, 1], ACT.Sqrt, bias=v.eps_ln[:]).then_inc(s["sdB_s"], 1)
                for k in range(2):
                    wait(e, s["x3_tr"], 2 * gt + k + 1)
                    if gs is not None:
                        wait(e, s["shu_done"], 2 * len(FSC) * (gs + 1))
                    e.activation(v.x3T[:, :, k * 2 * S:(k + 1) * 2 * S].rearrange("p c (b s) -> p b c s", b=2),
                                 v.tb[k][:].rearrange("p (b c s) -> p b c s", b=2, c=C), ACT.Copy)\
                        .then_inc(s["x3T_s"], 1)
            if tail:
                wait(e, s["logit_read"], gt + 2)
                e.activation(v.logit[:], v.logit[:], ACT.Exp).then_inc(s["exp_s"], 1)

        over_groups(e, step)

        for f in range(len(FSC)):
            silu_shared(G - 1, f)

        with e.Fori(0, EP // 2) as o:
            for half in range(2):
                p = o * 2 + half
                wait(e, s["g_tr"], p + 1)
                e.activation(v.xgT[:, half], v.tb[half][:, 0:C * P].rearrange("p (c n) -> p c n", c=C), ACT.Copy)\
                    .then_inc(s["gT_s"], 1)
                wait(e, s["gu_done"], p + 1)
                e.activation(v.sge[0:FH, half, :], mb[half][0:FH, 0:4 * CAP], ACT.Silu).then_inc(s["sg_s"], 1)

        with e.Fori(0, B // FR) as i:
            for k in range(FR):
                n = i * FR + k
                wait(e, s["aggr_s"], n + 1)
                e.activation(v.sdF[:, k:k + 1], v.mv[:, 2, k, 1:2], ACT.Sqrt, bias=v.eps_ln[:]).then_inc(s["fsd"], 1)


def pe_program(nc, block, v):
    s = v.s
    tb, mb, kb = v.tb, v.mb, v.kb

    @block.tensor
    def _(e):
        def transposes(src, k, done):
            for b in range(2):
                for c in range(C):
                    last = e.transpose(tb[k][:, (b * C + c) * P:(b * C + c + 1) * P], src[:, 2 * k + b, c * P:(c + 1) * P],
                                       v.ident[:])
            last.then_inc(s[done], 1)

        def dense(bank, w, n0, rhs, done):
            for c in range(C):
                last = e.matmul(bank, w[:, c, n0:n0 + P], rhs[:, c, :], start=(c == 0), stop=(c == C - 1))
            last.then_inc(s[done], 1)

        def keep_clock(bank, n):
            for _ in range(n):
                e.matmul(bank[:], v.ident[:], v.zeros[:], start=True, stop=True)

        e.wait_ge(s["idn"], 3)
        keep_clock(mb[0], 8)

        NF = len(FSC)

        def shared_up(g, f, free):
            n, banks = FSC[f], ((mb[0], mb[1]), (mb[2], mb[3]), (kb[0], kb[1]))[f]
            for k in range(2):
                wait(e, *free[k])
                for c in range(C):
                    last = e.matmul(banks[k][0:n, :], v.wsh[:, c, k * FS + f * P:k * FS + f * P + n],
                                    v.x3T[:, c, :], start=(c == 0), stop=(c == C - 1))
                last.then_inc(s["shu_done"], 1)

        def shared_down(g, banks):
            for k in banks:
                for b in range(2):
                    for f, n in enumerate(FSC):
                        t0 = (2 * k + b) * S
                        last = e.matmul(kb[k][:, b * D:(b + 1) * D], v.shh[0:n, f, t0:t0 + S], v.wshd[0:n, f, :],
                                        start=(f == 0), stop=(f == NF - 1))
                last.then_inc(s["shd_done"], 1)

        def votes_by_expert(g):
            for b in range(NB):
                last = e.transpose(kb[0][0:E, b * S:(b + 1) * S], v.votes[:, b, :], v.ident[:])
            last.then_inc(s["vote_tr"], 1)

        def step(gh, gt, gs):
            head, tail = gh is not None, gt is not None

            def conv(h):
                if h % 4 == 0:
                    wait(e, s["kv_ready"], 4 * gt + h // 4 + 1)
                o = mb[h % 4]
                k = v.kv[:, h // 4 % 2, :, h % 4, :]
                e.matmul(o[:, 0:PW], v.toep[:, h, 0:P], k[:, 0, :], start=True, stop=True)
                e.matmul(o[:, PW:2 * PW], v.toep[:, h, P:2 * P], k[:, 0, :], start=True, stop=False)
                e.matmul(o[:, PW:2 * PW], v.toep[:, h, 0:P], k[:, 1, :], start=False, stop=True)\
                    .then_inc(s["conv_done"], 1)

            if tail:
                e.wait_ge(s["d_done"], 2)
                for h in range(4):
                    conv(h)
                for h in range(4, 8):
                    wait(e, s["conv_evac"], HEADS * gt + h - 3)
                    conv(h)
            if head:
                wait(e, s["xn_s"], 4 * gh + 4)
                if gs is not None:
                    wait(e, s["x3T_s"], 2 * gt)
                    wait(e, s["logit_read"], gt + 1)
                for k in range(2):
                    transposes(v.xn, k, "x_tr")
            if gs is not None:
                wait_apart(e, v, s["y_s"], 2 * gt + 2)
                wait_apart(e, v, s["dve_r"], RDVE * gt)
                votes_by_expert(gs)
            if head:
                e.wait_ge(s["weights_in"], 16 * 5)
                wait(e, s["xT_s"], 4 * gh + 4)
                for k in range(4):
                    if tail:
                        wait(e, s["conv_evac"], HEADS * gt + 5 + k)
                    dense(mb[k][:], v.wlr, (k + 2) % 4 * P, v.xT, "lr_done")
            if tail:
                wait(e, s["x2_s"], 4 * gt + 4)
                if not head:
                    wait(e, s["x3T_s"], 2 * gt)
                    wait(e, s["logit_read"], gt + 1)
                for k in range(2):
                    transposes(v.x2, k, "x2_tr")
                for h in range(8, 12):
                    if head:
                        wait(e, s["right_s"] if h < 10 else s["left_s"], 2 * gh + h % 2 + 1)
                    else:
                        wait(e, s["conv_evac"], HEADS * gt + h - 3)
                    conv(h)
            if head:
                wait(e, s["cvs"], 8 * gh + 8)
                for k in range(4):
                    if tail:
                        wait(e, s["conv_evac"], HEADS * gt + 9 + k)
                    else:
                        wait(e, s["right_s"] if k < 2 else s["left_s"], 2 * gh + k % 2 + 1)
                    dense(mb[k][:], v.wg, k * P, v.cv, "gates_done")
            if tail:
                for h in range(12, 16):
                    if head:
                        wait(e, s["gate_s"], 4 * gh + h - 11)
                    else:
                        wait(e, s["conv_evac"], HEADS * gt + h - 3)
                    conv(h)
            if gs is not None:
                for f in range(2):
                    shared_up(gs, f, [(s["conv_evac"], HEADS * gt + 13 + 2 * f + k) for k in range(2)])
            if head:
                if gs is None:
                    if tail:
                        wait(e, s["conv_evac"], HEADS * gt + HEADS)
                    else:
                        wait(e, s["gate_s"], 4 * gh + 4)
                    keep_clock(mb[3], 5 if tail else 7)
                wait(e, s["lr_s"], C * gh + C)
                if gs is not None:
                    wait(e, s["voteT_s"], gs + 1)
                elif tail:
                    wait(e, s["y_s"], 2 * gh)
                for k in range(2):
                    for b in range(2):
                        for c in range(C):
                            t0 = (2 * k + b) * S
                            last = e.matmul(kb[k][:, b * D:(b + 1) * D], v.left[:, c, t0:t0 + S], v.wo[:, c, :],
                                            start=(c == 0), stop=(c == C - 1))
                    last.then_inc(s["out_done"], 1)
                if gs is not None:
                    wait(e, s["x1_s"], 2 * gh + 2)
                    shared_up(gs, 2, [(s["shg_s"], NF * gs + 2), (s["shh_s"], NF * gs + 2)])
                if tail:
                    wait(e, s["q_s"], 2 * gt + 2)
                wait(e, s["x1n_s"], 4 * gh + 4)
                for k in range(2):
                    transposes(v.xn, k, "x1_tr")
                wait(e, s["x1T_s"], 4 * gh + 4)
                for j in range(FJ):
                    if j == 4 and gs is not None:
                        wait(e, s["shh_s"], NF * gs + NF)
                        shared_down(gs, [0, 1])
                    for k in range(2):
                        i = 2 * j + k
                        if i < 4 and gs is not None:
                            wait(e, s["shg_s"] if k == 0 else s["shh_s"], NF * gs + j + 1)
                        elif i < 4 and tail:
                            wait(e, s["conv_evac"], HEADS * gt + 13 + i)
                        elif i < 4:
                            wait(e, s["gate_s"], 4 * gh + i + 1)
                        else:
                            wait(e, s["gelu_s"] if k == 0 else s["h_s"], FJ * gh + j - 1)
                        dense(mb[i % 4][:], v.wup, k * F + j * P, v.xT, "up_done")
            elif gs is not None:
                wait(e, s["voteT_s"], gs + 1)
                shared_up(gs, 2, [(s["shg_s"], NF * gs + 2), (s["shh_s"], NF * gs + 2)])
                wait(e, s["shh_s"], NF * gs + NF)
                shared_down(gs, [0, 1])
            def down(blocks, done):
                for k, b in blocks:
                    for j in range(FJ):
                        t0 = (2 * k + b) * S
                        last = e.matmul(kb[k][:, b * D:(b + 1) * D], v.mlp[:, j, t0:t0 + S], v.wdn[:, j, :],
                                        start=(j == 0), stop=(j == FJ - 1))
                if done:
                    last.then_inc(s["down_done"], 1)

            if head:
                wait(e, s["h_s"], FJ * gh + FJ)
                if gs is not None:
                    wait(e, s["sh_s"], 2 * gs + 2)
                down([(0, 0)], False)
            if tail:
                wait(e, s["qstep"], QSTEPS * gt + QSTEPS)
                wait(e, s["qpool"], QSTEPS * gt + QSTEPS)
                if not head:
                    wait(e, s["q_s"], 2 * gt + 2)
                for k in range(2):
                    for b in range(2):
                        for c in range(C):
                            last = e.transpose(tb[k][:, (b * C + c) * P:(b * C + c + 1) * P],
                                               v.acc[:, c].rearrange("p h (i b) -> p (h i) b", b=NB)[:, :, 2 * k + b],
                                               v.ident[:])
                    last.then_inc(s["o_tr"], 1)
            if head:
                down([(0, 1)], True)
                down([(1, 0)], False)
            if tail:
                e.wait_ge(s["shw_in"], 16 * 3)
                if not head:
                    keep_clock(mb[1], 6)
                wait(e, s["x3_s"], 4 * gt + 4)
                for k in range(2):
                    transposes(v.rows, k, "x3_tr")
            if tail:
                wait(e, s["x3T_s"], 2 * gt + 2)
                for b in range(NB):
                    for c in range(C):
                        last = e.matmul(tb[0][:, b * E:(b + 1) * E], v.x3T[:, c, b * S:(b + 1) * S], v.wgate[:, c, :],
                                        start=(c == 0), stop=(c == C - 1))
                last.then_inc(s["logit_done"], 1)
            if head:
                down([(1, 1)], True)

        over_groups(e, step)

        e.wait_ge(s["logit_read"], G + 1)
        shared_up(G - 1, 0, [(s["x3T_s"], 2 * G)] * 2)
        e.wait_ge(s["sh_s"], 2 * (G - 1))
        e.wait_ge(s["dve_r"], RDVE * G)
        votes_by_expert(G - 1)
        shared_up(G - 1, 1, [(s["x3T_s"], 2 * G)] * 2)
        shared_up(G - 1, 2, [(s["voteT_s"], G)] * 2)
        e.wait_ge(s["shh_s"], NF * G)
        shared_down(G - 1, [0])
        e.wait_ge(s["pick_s"], PDVE * (G - 1) + 17)
        e.transpose(tb[0][:, 0:E], v.firstd[:].rearrange("p k n -> p (k n)"), v.ident[0:E, 0:E]).then_inc(s["pickT_s"], 1)
        shared_down(G - 1, [1])
        e.wait_ge(s["idx_s"], 2)
        e.wait_ge(s["sh_s"], 2 * G)
        e.wait_ge(s["shh_s"], NF * G)

        def place_rows(pair):
            wait(e, s[f"gat{pair.row}"], 16 * pair.turn + 16)
            if not pair.first(2):
                wait(e, s["gT_s"], pair.p - 1)
            for c in range(C):
                last = e.transpose(tb[pair.half][:, c * P:(c + 1) * P], v.xg[:, pair.row, c * P:(c + 1) * P], v.ident[:])
            last.then_inc(s["g_tr"], 1)

        def gate_up(pair):
            wgu = v.ring[pair.slot][0]
            wait(e, s["gT_s"], pair.p + 1)
            wait(e, s[f"wring{pair.slot}"], 32 * pair.load + 32)
            if not pair.first(2):
                wait(e, s["he_s"], pair.p - 1)
            for k in range(2):
                for x in range(2):
                    for f in range(2):
                        o1 = mb[pair.half][0:FH, k * 256 + (2 * x + f) * CAP:k * 256 + (2 * x + f + 1) * CAP]
                        for c in range(C):
                            last = e.matmul(o1, wgu[:, x, c, k * FE + f * FH:k * FE + (f + 1) * FH],
                                            v.xgT[:, pair.half, c, x * CAP:(x + 1) * CAP], start=(c == 0), stop=(c == C - 1))
            last.then_inc(s["gu_done"], 1)

        def down(pair):
            wd = v.ring[pair.slot][1]
            wait(e, s["he_s"], pair.p + 1)
            if not pair.first(2):
                wait(e, s["dout_s"], pair.p - 1)
            for x in range(2):
                for f in range(2):
                    last = e.matmul(kb[pair.half][x * CAP:(x + 1) * CAP, 0:D], v.he[0:FH, pair.half, x, f, :],
                                    wd[0:FH, x, f, :], start=(f == 0), stop=(f == 1))
            last.then_inc(s["dn_done"], 1)

        def expert_step(pair, before):
            if pair is not None:
                place_rows(pair)
            if before is not None:
                down(before)
            if pair is not None:
                gate_up(pair)

        over_pairs(e, expert_step)

        def sums(i, first):
            for k in range(1, FR, 2):
                if first:
                    e.wait_ge(s["dout_s"], EP)
                else:
                    wait(e, s["f_s"], (i - 1) * FR + k + 1)
                wait(e, s[f"z{k}"], 16 * i + 16)
                for z in range(ZR):
                    last = e.matmul(kb[k // 2][:, 0:D], v.ident[:], v.zin[:, k, z * D:(z + 1) * D],
                                    start=(z == 0), stop=(z == ZR - 1))
                last.then_inc(s["sum_pe"], 1)

        sums(0, True)
        with e.Fori(1, B // FR) as i:
            sums(i, False)




def query_products(e, v, steps, heads):
    parts = []

    def product(d, t, cols):
        n = (HD - d) * NB
        y = v.ycv[:, :, heads, DOFF[d] * NB:DOFF[d] * NB + n]
        if d == 0:
            steps.did(e.tensor_tensor(v.acc[:, :, heads, :], v.q[:, :, heads, :], y, ALU.mult))
        else:
            wait(e, steps.sem, steps.base + steps.n)
            steps.did(e.tensor_tensor(v.tmp[:, t, :, heads, 0:n], v.q[:, :, heads, cols], y, ALU.mult))

    def add(d, t, cols):
        n = (HD - d) * NB
        wait(e, steps.sem, steps.base + steps.n - (1 if t == 0 else 0))
        steps.did(e.tensor_tensor(v.acc[:, :, heads, cols], v.acc[:, :, heads, cols], v.tmp[:, t, :, heads, 0:n], ALU.add))

    parts.append(lambda: product(0, 0, None))
    for d in range(1, HD):
        lo, hi = slice(0, (HD - d) * NB), slice(d * NB, HD * NB)
        for step, t, cols in ((product, 0, hi), (product, 1, lo), (add, 0, lo), (add, 1, hi)):
            parts.append(lambda step=step, d=d, t=t, cols=cols: step(d, t, cols))
    return parts


def dve_program(nc, block, v):
    s = v.s
    tb, mb, kb = v.tb, v.mb, v.kb
    hsteps, rsteps, qsteps = Steps(s["dve_h"], HDVE), Steps(s["dve_r"], RDVE), Steps(s["qstep"], QSTEPS)
    psteps = Steps(s["pick_s"], PDVE)
    NF = len(FSC)

    @block.vector
    def _(e):
        e.memset(v.eps_rms[:], EPS_RMS)
        e.memset(v.eps_ln[:], EPS_LN)
        e.memset(v.one[:], 1.0)
        e.memset(v.ones[:], 1.0)
        e.memset(v.pp[:], 2.0)
        e.memset(v.rtv[:, :, :, 0:3], 0.0)
        e.memset(v.cand[:], 0.0)
        e.memset(v.empty_row[:], 0.0)
        e.memset(v.idx_all[:], T).then_inc(s["consts_s"], 1)
        e.wait_ge(s["consts_s"], 1)
        e.memset(v.empty_row[0:1, D:ROW], float(4 * NZ)).then_inc(s["logit_read"], 1)
        e.wait_ge(s["tnum_s"], 1)

        def norm_apply(dst, src, inv, done):
            for b in range(NB):
                e.tensor_scalar(dst[:, b, :], src[:, b, :], inv[:, b:b + 1], None, ALU.mult).then_inc(s[done], 1)

        def feature_copy(k, name, done):
            for c in range(C):
                e.tensor_scalar(v.xT[:, c, k * 2 * S:(k + 1) * 2 * S].rearrange("p (b s) -> p b s", b=2),
                                tb[k][:].rearrange("p (b c s) -> p b c s", b=2, c=C)[:, :, c, :],
                                col(v, name, c), None, ALU.mult).then_inc(s[done], 1)

        def votes_in(g):
            psteps.begin(g)
            wait(e, s["vote_tr"], g + 1)
            e.tensor_copy(v.cand[:, CAP:], kb[0][0:E, :]).then_inc(s["voteT_s"], 1)
            wait_apart(e, v, s["voteT_s"], g + 1)

        def rounds(a, b):
            for k in range(a, b):
                m = v.first[:, 8 * k:8 * k + 8]
                if k:
                    wait_apart(e, v, psteps.sem, psteps.base + psteps.n)
                n = psteps.did(e.max(m, v.cand[:]))
                wait_apart(e, v, psteps.sem, n)
                n = psteps.did(e.match_replace(v.cand[:], m, v.cand[:], 0.0))

        def keep_first():
            wait(e, psteps.sem, psteps.base + psteps.n)
            psteps.did(e.tensor_copy(v.cand[:, 0:CAP], v.first[:]))
            psteps.end()

        def shared_rows(g, f):
            n, bank = FSC[f], (mb[1], mb[3], kb[1])[f]
            wait(e, s["shg_s"], NF * g + f + 1)
            wait(e, s["shu_done"], (NF * g + f) * 2 + 2)
            e.tensor_tensor(v.shh[0:n, f, :], bank[0:n, :], v.sgl[0:n, f % 2, :], ALU.mult).then_inc(s["shh_s"], 1)

        def shared_sums(g):
            for k in range(2):
                wait(e, s["shd_done"], 2 * g + k + 1)
                e.tensor_tensor(v.u[:, 2 * k:2 * k + 2, :], kb[k][:].rearrange("p (b n) -> p b n", b=2),
                                v.rows[:, 2 * k:2 * k + 2, 0:D], ALU.add).then_inc(s["sh_s"], 1)

        def step(gh, gt, gs):
            head, tail = gh is not None, gt is not None
            if head:
                hsteps.begin(gh)
                wait(e, s["rms1_s"], gh + 1)
                e.reciprocal(v.inv1, v.rms1).then_inc(s["inv1_s"], 1)
                wait(e, s["inv1_s"], gh + 1)
                norm_apply(v.xn, v.xin, v.inv1, "xn_s")
            if tail:
                wait(e, s["sdA_s"], gt + 1)
                e.reciprocal(v.isA, v.sdA).then_inc(s["isA_s"], 1)
                wait(e, s["isA_s"], gt + 1)
                for b in range(NB):
                    e.tensor_scalar(v.x2[:, b, :], v.xs[:, b, :], v.mv[:, 0, b, 0:1], v.isA[:, b:b + 1],
                                    ALU.subtract, ALU.mult).then_inc(s["x2_s"], 1)
            if head:
                if not tail:
                    e.wait_ge(s["consts_in"], 16 * 4)
                for k in range(2):
                    wait(e, s["x_tr"], 2 * gh + k + 1)
                    feature_copy(k, "norm1", "xT_s")
                if not tail:
                    e.wait_ge(s["lru_s"], 4)
                    e.tensor_tensor(v.lru[:, 0], v.lru[:, 0], v.lru[:, 2], ALU.add).then_inc(s["lru_s"], 1)
                    e.wait_ge(s["lru_s"], 5)
                    e.tensor_scalar(v.lru[:, 1], v.lru[:, 0], -LRU_C, None, ALU.mult)
                    e.tensor_scalar(v.lru[:, 0], v.lru[:, 0], LRU_C, None, ALU.mult).then_inc(s["lru_s"], 1)
            if gs is not None:
                votes_in(gs)
                rounds(0, 4)
            if head:
                for c in range(C):
                    wait(e, s["right_s"], 2 * gh + c + 1)
                    o = v.cv[:, c, :].rearrange("p (b n) -> p b n", b=NB)
                    e.tensor_scalar(o, v.rtv[:, c, :, 0:S], col(v, "conv_w", c), col(v, "conv_b", c), ALU.mult, ALU.add)\
                        .then_inc(s["cvs"], 1)
                for k in range(1, 4):
                    for c in range(C):
                        o = v.cv[:, c, :].rearrange("p (b n) -> p b n", b=NB)
                        wait(e, s["cvs"], 8 * gh + 2 * k - 1 + c)
                        e.scalar_tensor_tensor(out=o, in0=v.rtv[:, c, :, k:k + S], scalar=col(v, "conv_w", C * k + c),
                                               in1=o, op0=ALU.mult, op1=ALU.add).then_inc(s["cvs"], 1)
            if tail:
                for k in range(2):
                    wait(e, s["x2_tr"], 2 * gt + k + 1)
                    e.tensor_copy(v.q.rearrange("p c h (i b) -> p b c (h i)", b=NB)[:, 2 * k:2 * k + 2],
                                  tb[k][:].rearrange("p (b c s) -> p b c s", b=2, c=C)).then_inc(s["q_s"], 1)
            if gs is not None:
                rounds(4, 8)
                keep_first()
            if head:
                a, i = v.ri[:, 0:2, :], v.ri[:, 2:4, :]
                wait(e, s["gate_s"], 4 * gh + 4)
                wait(e, s["gates_done"], 4 * gh + 4)
                wait(e, s["cvs"], 8 * gh + 8)
                hsteps.did(e.tensor_tensor(i, i, v.cv, ALU.mult))
                for c in range(C):
                    wait(e, s["act_a"], 2 * gh + c + 1)
                    n = hsteps.did(e.tensor_tensor(v.hs[:, c, :], a[:, c, :], a[:, c, :], ALU.mult))
                    wait(e, hsteps.sem, n)
                    wait(e, s["th_s"], 2 * gh + c + 1)
                    hsteps.did(e.scalar_tensor_tensor(out=v.th[:, c, :], in0=v.hs[:, c, :], scalar=1.0, in1=v.th[:, c, :],
                                                      op0=ALU.add, op1=ALU.mult))
                hsteps.did(e.memset(v.ri[:, 0:2, :].rearrange("p c (b s) -> p (c b) s", b=NB)[:, :, 0:1], 0.0))
                for c in range(C):
                    wait(e, s["mult_s"], C * gh + c + 1)
                    n = hsteps.did(e.tensor_tensor(v.th[:, c, :], v.th[:, c, :], i[:, c, :], ALU.mult))
                    wait(e, hsteps.sem, n)
                    n = hsteps.did(e.tensor_tensor_scan(v.hs[:, c, :], a[:, c, :], v.th[:, c, :], 0.0, ALU.mult, ALU.add))
                    wait(e, hsteps.sem, n)
                    wait(e, s["left_s"], 2 * gh + c + 1)
                    e.tensor_tensor(v.left[:, c, :], v.left[:, c, :], v.hs[:, c, :], ALU.mult).then_inc(s["lr_s"], 1)
            if gs is not None and head:
                shared_rows(gs, 0)
                shared_rows(gs, 1)
            if head:
                for k in range(2):
                    wait(e, s["out_done"], 2 * gh + k + 1)
                    wait(e, s["xo_s"], gh + 1)
                    e.tensor_tensor(v.xo[:, 2 * k:2 * k + 2, :], kb[k][:].rearrange("p (b n) -> p b n", b=2),
                                    v.xo[:, 2 * k:2 * k + 2, :], ALU.add).then_inc(s["x1_s"], 1)
                wait(e, s["rms2_s"], gh + 1)
                n = hsteps.did(e.reciprocal(v.inv2, v.rms2))
                wait(e, hsteps.sem, n)
                norm_apply(v.xn, v.xo, v.inv2, "x1n_s")
                for k in range(2):
                    wait(e, s["x1_tr"], 2 * gh + k + 1)
                    feature_copy(k, "norm2", "x1T_s")

            if tail:
                qsteps.begin(gt)
                parts = query_products(e, v, qsteps, slice(0, HEADS_DVE))
                wait(e, s["conv_evac"], HEADS * gt + HEADS)
                wait(e, s["q_s"], 2 * gt + 2)
            else:
                parts = []
            if head:
                for j in range(FJ):
                    if j == 2 and gs is not None:
                        shared_rows(gs, 2)
                    if j == 5 and gs is not None:
                        shared_sums(gs)
                    wait(e, s["gelu_s"], FJ * gh + j + 1)
                    wait(e, s["up_done"], 2 * FJ * gh + 2 * j + 2)
                    e.scalar_tensor_tensor(out=v.mlp[:, j, :], in0=mb[(2 * j + 1) % 4][:], scalar=col(v, "up2_b", j),
                                           in1=v.gl[:, j % 2, :], op0=ALU.add, op1=ALU.mult).then_inc(s["h_s"], 1)
                    for f in parts[5 * j:5 * j + 5]:
                        f()
            else:
                for n, f in enumerate(parts):
                    if gs is not None and n in (4, 8, 12):
                        shared_rows(gs, n // 4 - 1)
                    if gs is not None and n == 24:
                        shared_sums(gs)
                    f()
            if tail:
                qsteps.end()
                rsteps.begin(gt)
                if gs is not None:
                    wait(e, s["sums_out"], 16 * gs + 16)
                for k in range(2):
                    wait(e, s["o_tr"], 2 * gt + k + 1)
                    e.tensor_tensor(v.u[:, 2 * k:2 * k + 2, :], tb[k][:].rearrange("p (b n) -> p b n", b=2),
                                    v.x2[:, 2 * k:2 * k + 2, :], ALU.add).then_inc(s["u_s"], 1)
                wait(e, s["u_s"], 2 * gt + 2)
                for b in range(NB):
                    last = e.bn_stats(v.bn[:, 1, b, :], v.u[:, b, :])
                n = rsteps.did(last)
                wait_apart(e, v, rsteps.sem, n)
                for b in range(NB):
                    last = e.bn_aggr(v.mv[:, 1, b, :], v.bn[:, 1, b, :])
                last.then_inc(s["lnB_s"], 1)
                wait(e, s["sdB_s"], gt + 1)
                e.reciprocal(v.isB, v.sdB).then_inc(s["isB_s"], 1)
                wait(e, s["isB_s"], gt + 1)
                wait(e, s["rows_out"], 16 * gt + 16)
                for b in range(NB):
                    e.tensor_scalar(v.rows[:, b, 0:D], v.u[:, b, :], v.mv[:, 1, b, 0:1], v.isB[:, b:b + 1],
                                    ALU.subtract, ALU.mult).then_inc(s["x3_s"], 1)
            def residual(k):
                wait(e, s["down_done"], 2 * gh + k + 1)
                wait(e, s["xs_s"], 2 * gh + 2)
                e.tensor_tensor(v.xs[:, 2 * k:2 * k + 2, :], kb[k][:].rearrange("p (b n) -> p b n", b=2),
                                v.xs[:, 2 * k:2 * k + 2, :], ALU.add).then_inc(s["y_s"], 1)
                wait(e, s["y_s"], 2 * gh + k + 1)
                for b in range(2 * k, 2 * k + 2):
                    last = e.bn_stats(v.bn[:, 0, b, :], v.xs[:, b, :])
                return last

            if head:
                residual(0)
            if tail:
                r, sem_r = rsteps, rsteps.sem
                lg = tb[0][:, 0:NB * E].rearrange("p (b n) -> p b n", b=NB)
                wait(e, s["logit_done"], gt + 1)
                e.tensor_reduce(v.mx, lg, AX.X, ALU.max).then_inc(s["mx_s"], 1)
                wait(e, s["mx_s"], gt + 1)
                e.tensor_tensor(v.logit[:], lg, v.mx[:, :, None].to_broadcast((P, NB, E)), ALU.subtract)\
                    .then_inc(s["logit_read"], 1)
            if head:
                n = hsteps.did(residual(1))
                wait_apart(e, v, hsteps.sem, n)
                for b in range(NB):
                    last = e.bn_aggr(v.mv[:, 0, b, :], v.bn[:, 0, b, :])
                last.then_inc(s["lnA_s"], 1)
                hsteps.end()
            if tail:
                wait(e, s["exp_s"], gt + 1)
                n = r.did(e.tensor_reduce(v.sm, v.logit[:], AX.X, ALU.add))
                wait(e, sem_r, n)
                n = r.did(e.reciprocal(v.sm, v.sm))
                wait(e, sem_r, n)
                pv = v.pp[:, :, 2:]
                n = r.did(e.tensor_tensor(pv, v.logit[:], v.sm[:, :, None].to_broadcast((P, NB, E)), ALU.mult))
                wait_apart(e, v, sem_r, n)
                for b in range(NB):
                    last = e.max(v.m8[:, b, :], v.pp[:, b, :])
                n = r.did(last)
                e.tensor_copy(v.rows[:, :, D::2], pv)
                wait_apart(e, v, sem_r, n)
                for b in range(NB):
                    last = e.match_replace(v.pr[:, b, :], v.m8[:, b, :], v.pp[:, b, :], -1.0)
                n = r.did(last)
                wait(e, sem_r, n)
                n = r.did(e.tensor_scalar(v.mask[:], v.pr[:, :, 2:], 0.0, None, ALU.is_lt))
                wait(e, sem_r, n)
                r.did(e.tensor_tensor(v.votes[:], v.mask[:],
                                      v.tnum[:, :, None].to_broadcast((P, NB, E)), ALU.mult))
                n = r.did(e.tensor_tensor_scan(v.cum[:].rearrange("p b n -> p (b n)"), v.ones[:],
                                               v.mask[:].rearrange("p b n -> p (b n)"), 0.0, ALU.mult, ALU.add))
                wait(e, sem_r, n)
                n = r.did(e.tensor_tensor(v.cum[:], v.cum[:], v.mask[:], ALU.subtract))
                wait(e, sem_r, n)
                e.tensor_tensor(v.rows[:, :, D + 1::2], v.cum[:], v.zbase[:, :, None].to_broadcast((P, NB, E)), ALU.add)\
                    .then_inc(s["rows_s"], 1)
                r.did(e.tensor_scalar(v.tnum[:], v.tnum[:], float(-TG), None, ALU.add))
                wait(e, s["rows_s"], gt + 1)
                r.did(e.tensor_scalar(v.zbase[:], v.zbase[:], float(ZR * TG), None, ALU.add))
                r.end()

        over_groups(e, step)

        votes_in(G - 1)
        rounds(0, 2)
        for f in range(2):
            shared_rows(G - 1, f)
        rounds(2, 4)
        shared_rows(G - 1, 2)
        rounds(4, 8)
        e.wait_ge(psteps.sem, PDVE * (G - 1) + 16)
        for k in range(2):
            last = e.tensor_scalar(v.firstd[:, k, :], v.first[:], -1.0, 4096.0, ALU.mult, ALU.add)
        psteps.did(last)
        epilogue(nc, e, v, lambda: shared_sums(G - 1))


def epilogue(nc, e, v, last_sums):
    s = v.s
    tb, mb, kb = v.tb, v.mb, v.kb

    e.wait_ge(s["pickT_s"], 1)
    for x in range(2):
        e.tensor_scalar(v.idx_all[x * CAP:(x + 1) * CAP, 0:EP], tb[0][x * CAP:(x + 1) * CAP, x:E:2], float(T), None, ALU.min)\
            .then_inc(s["idx_s"], 1)
    e.wait_ge(s["idx_s"], 2)
    e.tensor_copy(v.idx_slot[:], v.idx_all[:, 0:RING]).then_inc(s["idxc_s"], 1)
    last_sums()

    def places(pair):
        p, r = pair.p, pair.row
        wait(e, s[f"gat{r}"], 16 * pair.turn + 16)
        if not pair.first(RING):
            wait(e, s[f"scat{r}"], 16 * pair.turn)
        for x in range(2):
            last = e.tensor_copy(v.pz_slot[x * CAP:(x + 1) * CAP, r, :],
                                 v.xg[x * CAP:(x + 1) * CAP, r, bass.ds(p * 4 + (D + 2 * x), 2)])
        last.then_inc(s["pz_s"], 1)
        wait(e, s["pz_s"], p + 1)
        e.tensor_copy(v.z_slot[:, r:r + 1], v.pz_slot[:, r, 1:2]).then_inc(s["zi_s"], 1)
        e.tensor_copy(v.idx_slot[:, r:r + 1], v.idx_all[:, bass.ds(p + RING, 1)]).then_inc(s["idxc_s"], 1)

    def hidden(pair):
        wait(e, s["sg_s"], pair.p + 1)
        if not pair.first(2):
            wait(e, s["dn_done"], pair.p - 1)
        e.tensor_tensor(v.he[0:FH, pair.half].rearrange("p e f n -> p (e f n)"), mb[pair.half][0:FH, 256:512],
                        v.sge[0:FH, pair.half, :], ALU.mult).then_inc(s["he_s"], 1)

    def weighted(pair):
        wait(e, s["dn_done"], pair.p + 1)
        e.tensor_scalar(v.dout[:, pair.row, :], kb[pair.half][:, 0:D], v.pz_slot[:, pair.row, 0:1], None, ALU.mult)\
            .then_inc(s["dout_s"], 1)

    def expert_step(pair, before):
        if pair is not None:
            places(pair)
        if before is not None:
            weighted(before)
        if pair is not None:
            hidden(pair)

    over_pairs(e, expert_step)

    def sums_of(k):
        return kb[k // 2][:, 0:D] if k % 2 else v.u[:, k, :]

    def statistics(i, k):
        if k % 2:
            wait(e, s["sum_pe"], i * (FR // 2) + k // 2 + 1)
        else:
            wait(e, s[f"z{k}"], 16 * i + 16)
            e.tensor_reduce(sums_of(k), v.zin[:, k, :].rearrange("p (k d) -> p d k", k=ZR), AX.X, ALU.add)\
                .then_inc(s["sum_dve"], 1)
            wait(e, s["sum_dve"], i * (FR // 2) + k // 2 + 1)
        e.bn_stats(v.bn[:, 2, k, :], sums_of(k)).then_inc(s["stats_s"], 1)

    def spread(i, k):
        wait_apart(e, v, s["stats_s"], i * FR + k + 1)
        e.bn_aggr(v.mv[:, 2, k, :], v.bn[:, 2, k, :]).then_inc(s["aggr_s"], 1)

    def normalise(i, k, first):
        n = i * FR + k
        wait(e, s["fsd"], n + 1)
        e.reciprocal(v.isF[:, k:k + 1], v.sdF[:, k:k + 1]).then_inc(s["isF_s"], 1)
        wait(e, s["isF_s"], n + 1)
        if not first:
            wait(e, s[f"out{k}"], 16 * i)
        e.tensor_scalar(v.x2[:, k, :], sums_of(k), v.mv[:, 2, k, 0:1], v.isF[:, k:k + 1], ALU.subtract, ALU.mult)\
            .then_inc(s["f_s"], 1)

    def final(i, first):
        for k in range(FR):
            statistics(i, k)
            if k:
                normalise(i, k - 1, first)
            spread(i, k)
        normalise(i, FR - 1, first)

    final(0, True)
    with e.Fori(1, B // FR) as i:
        final(i, False)


def _by_chunk(np_, a):
    return np_.ascontiguousarray(a.reshape(-1, P, a.shape[-1]).transpose(1, 0, 2))


def kernel(**inputs):
    import numpy as _np
    import concourse.bacc as _bacc
    from concourse import mybir as _mybir
    from concourse.bass_utils import run_bass_kernel_spmd as _run

    a = {k: _np.asarray(w) for k, w in inputs.items()}
    at = lambda n: a["L0_attn_" + n]
    ff = lambda n: a["L0_ffn_" + n]
    column = lambda w: w.reshape(-1, P).T
    cols = _np.concatenate([column(at("norm1_w")), column(at("norm2_w")), column(at("left_b")), column(at("right_b")),
                            column(at("conv_b"))] + [column(at("conv_w")[k]) for k in range(4)] +
                           [column(at(n)) for n in ("ga_b", "gx_b", "a_param", "up1_b", "up2_b")], axis=1)
    both = lambda m, n: _by_chunk(_np, _np.concatenate([at(m), at(n)], axis=1))
    ssm = a["L0_xattn_ssm_kernel"]
    kpad = _np.concatenate([_np.zeros((HEADS, P - 1), ssm.dtype), ssm], axis=1)
    shd = ff("sh_down").T
    shd = _np.concatenate([shd, _np.zeros((len(FSC) * P - FS, D), shd.dtype)], axis=0)
    gu = _np.stack([ff("w_gate"), ff("w_up")], axis=2)
    arrays = {
        "x": a["x"],
        "ctx": a["ctx_2048"].reshape(G, NB, S, C, P).transpose(0, 4, 3, 2, 1).reshape(G, P, C, S * NB),
        "cols": cols,
        "out_b": at("out_b")[None], "down_b": at("down_b")[None], "d": a["L0_xattn_D"][None], "kpad": kpad,
        "w_left_right": both("left_W", "right_W"), "w_gates": both("ga_W", "gx_W"), "w_out": _by_chunk(_np, at("out_W")),
        "w_up": both("up1_W", "up2_W"), "w_down": _by_chunk(_np, at("down_W")),
        "w_router": _by_chunk(_np, ff("gate_w").T),
        "w_shared": _by_chunk(_np, _np.concatenate([ff("sh_gate").T, ff("sh_up").T], axis=1)),
        "w_shared_down": _by_chunk(_np, shd),
        "w_experts": gu.reshape(EP, 2, C, P, 2 * FE).transpose(0, 3, 1, 2, 4),
        "w_experts_down": ff("w_down").reshape(EP, 2, 2, FH, D).transpose(0, 3, 1, 2, 4),
    }
    nc = _bacc.Bacc("TRN2", target_bir_lowering=False, num_devices=1)
    feeds, args = {}, []
    for name, w in arrays.items():
        w = _np.ascontiguousarray(w)
        feeds[f"in_{name}_dram"] = w
        args.append(nc.dram_tensor(f"in_{name}_dram", w.shape, _mybir.dt.from_np(w.dtype), kind="ExternalInput").ap())
    args.append(nc.dram_tensor("out_0_dram", (B, S, D), F32, kind="ExternalOutput").ap())
    build(nc, *args)
    r = _run(nc, [feeds], core_ids=[0])
    return r.results[0]["out_0_dram"]
```
